# Optimizing a Trainium2 kernel written in Bass

```python
import numpy as np
import jax
import jax.numpy as jnp

def _softmax(x, axis=-1):
    return jax.nn.softmax(x, axis=axis)

def _gelu(x):
    return jax.nn.gelu(x, approximate=True)

def _silu(x):
    return jax.nn.silu(x)

def _sigmoid(x):
    return jax.nn.sigmoid(x)

def _layernorm(x, axis=-1, eps=1e-05):
    m = jnp.mean(x, axis=axis, keepdims=True)
    v = jnp.var(x, axis=axis, keepdims=True)
    return (x - m) / jnp.sqrt(v + eps)

def _scatter_add(tgt, idx, src, axis=0):
    return tgt.at[idx].add(src)

def _segment_sum(src, seg, n):
    return jax.ops.segment_sum(src, seg, n)
kernel_name = 'mk_conv_seq_d2_conv_nhwc192_r4_908793'

def setup_inputs(seed: int=0):
    np.random.seed(seed)
    _w = jnp.asarray

    def _rec_inputs():
        import jax
        import jax.numpy as jnp
        _gk = jax.random.key(seed)
        x = -0.000357 + 1 * jax.random.normal(jax.random.fold_in(_gk, 1), (32, 56, 56, 48), jnp.float32)
        return x
    x = _rec_inputs()

    def _L0_conv_setup():
        import jax, jax.numpy as jnp
        import numpy as np
        from jax import lax

        def quick_gelu(x):
            return x * jax.nn.sigmoid(1.702 * x)
        key = jax.random.key(seed)
        ks = jax.random.split(key, 12)
        B, H, W, C, D, M = (32, 56, 56, 48, 16, 8)
        g = lambda k, shape, s: jax.random.normal(k, shape, jnp.float32) * s
        return {'x': jax.random.normal(ks[0], (B, H, W, C), jnp.float32), 'W1': g(ks[1], (16, C), 0.05), 'b1': jnp.zeros((16,), jnp.float32), 'W2': g(ks[2], (16, 16), 0.05), 'b2': jnp.zeros((16,), jnp.float32), 'mask_token': g(ks[3], (M, 16), 0.05), 'Wh': g(ks[4], (D * D * 9, 16), 0.02), 'bh': g(ks[5], (D * D * 9,), 0.02), 'Wd': g(ks[6], (D, C), 0.05), 'bd': jnp.zeros((D,), jnp.float32), 'Wu': g(ks[7], (C, D), 0.02), 'bu': jnp.zeros((C,), jnp.float32)}
    _L0_conv_all = _L0_conv_setup()
    _L0_conv_in = {k: v for k, v in _L0_conv_all.items() if k in ('W1', 'b1', 'W2', 'b2', 'mask_token', 'Wh', 'bh', 'Wd', 'bd', 'Wu', 'bu')}
    del _L0_conv_all

    def _L1_conv_setup():
        import jax, jax.numpy as jnp
        import numpy as np
        B, H, W, C = (32, 56, 56, 48)
        WS, SHIFT, HEADS = (7, 3, 6)
        HEAD_DIM = C // HEADS
        SCALE = 0.17677669529663687
        HIDDEN = 4 * C
        N = WS * WS
        EPS = 0.001

        def _rel_index(ws):
            coords = np.stack(np.meshgrid(np.arange(ws), np.arange(ws), indexing='ij')).reshape(2, -1)
            rel = (coords[:, :, None] - coords[:, None, :]).transpose(1, 2, 0)
            rel[:, :, 0] += ws - 1
            rel[:, :, 1] += ws - 1
            rel[:, :, 0] *= 2 * ws - 1
            return rel.sum(-1)

        def _attn_mask(h, w, ws, ss):
            img = np.zeros((h, w), np.float32)
            cnt = 0
            for hs in (slice(0, -ws), slice(-ws, -ss), slice(-ss, None)):
                for wsl in (slice(0, -ws), slice(-ws, -ss), slice(-ss, None)):
                    img[hs, wsl] = cnt
                    cnt += 1
            win = img.reshape(h // ws, ws, w // ws, ws).transpose(0, 2, 1, 3).reshape(-1, ws * ws)
            diff = win[:, None, :] - win[:, :, None]
            return np.where(diff != 0, -100.0, 0.0).astype(np.float32)
        REL_IDX = jnp.asarray(_rel_index(WS).reshape(-1))
        ATTN_MASK = jnp.asarray(_attn_mask(H, W, WS, SHIFT))
        NW = ATTN_MASK.shape[0]

        def _window_partition(x, ws):
            b, h, w, c = x.shape
            x = x.reshape(b, h // ws, ws, w // ws, ws, c).transpose(0, 1, 3, 2, 4, 5)
            return x.reshape(-1, ws, ws, c)

        def _window_reverse(x, ws, h, w):
            c = x.shape[-1]
            x = x.reshape(-1, h // ws, w // ws, ws, ws, c).transpose(0, 1, 3, 2, 4, 5)
            return x.reshape(-1, h, w, c)

        def _layer_norm(x, g, b):
            mu = jnp.mean(x, axis=-1, keepdims=True)
            var = jnp.var(x, axis=-1, keepdims=True)
            return (x - mu) * jax.lax.rsqrt(var + EPS) * g + b

        def _forward(x, ln1_g, ln1_b, w_qkv, b_qkv, bias_table, w_proj, b_proj, ln2_g, ln2_b, w_ffn1, bn1_scale, bn1_shift, w_ffn2, bn2_scale, bn2_shift):
            shortcut = x
            h = _layer_norm(x, ln1_g, ln1_b)
            h = jnp.roll(h, (-SHIFT, -SHIFT), axis=(1, 2))
            xw = _window_partition(h, WS).reshape(-1, N, C)
            qkv = xw @ w_qkv + b_qkv
            qkv = qkv.reshape(-1, N, 3, HEADS, HEAD_DIM).transpose(2, 0, 3, 1, 4)
            q, k, v = (qkv[0] * SCALE, qkv[1], qkv[2])
            attn = jnp.einsum('whnd,whmd->whnm', q, k)
            rel_bias = bias_table[REL_IDX].reshape(N, N, HEADS).transpose(2, 0, 1)
            attn = attn + rel_bias[None]
            attn = attn.reshape(-1, NW, HEADS, N, N) + ATTN_MASK[None, :, None]
            attn = jax.nn.softmax(attn.reshape(-1, HEADS, N, N), axis=-1)
            o = jnp.einsum('whnm,whmd->whnd', attn, v)
            o = o.transpose(0, 2, 1, 3).reshape(-1, N, C)
            o = o @ w_proj + b_proj
            o = _window_reverse(o.reshape(-1, WS, WS, C), WS, H, W)
            o = jnp.roll(o, (SHIFT, SHIFT), axis=(1, 2))
            x = shortcut + o
            y = _layer_norm(x, ln2_g, ln2_b)
            dn = ('NHWC', 'HWIO', 'NHWC')
            y = jax.lax.conv_general_dilated(y, w_ffn1, (1, 1), 'SAME', dimension_numbers=dn)
            y = y * bn1_scale + bn1_shift
            y = jax.nn.gelu(y, approximate=False)
            y = jax.lax.conv_general_dilated(y, w_ffn2, (1, 1), 'SAME', dimension_numbers=dn)
            y = y * bn2_scale + bn2_shift
            return x + y
        key = jax.random.key(seed)
        ks = jax.random.split(key, 8)
        s = lambda n: 0.02
        return {'x': jax.random.normal(ks[0], (B, H, W, C), jnp.float32), 'ln1_g': jnp.ones((C,), jnp.float32), 'ln1_b': jnp.zeros((C,), jnp.float32), 'w_qkv': jax.random.normal(ks[1], (C, 3 * C), jnp.float32) * C ** (-0.5), 'b_qkv': jnp.zeros((3 * C,), jnp.float32), 'bias_table': jax.random.truncated_normal(ks[2], -2.0, 2.0, ((2 * WS - 1) ** 2, HEADS), jnp.float32) * 0.02, 'w_proj': jax.random.normal(ks[3], (C, C), jnp.float32) * C ** (-0.5), 'b_proj': jnp.zeros((C,), jnp.float32), 'ln2_g': jnp.ones((C,), jnp.float32), 'ln2_b': jnp.zeros((C,), jnp.float32), 'w_ffn1': jax.random.normal(ks[4], (3, 3, C, HIDDEN), jnp.float32) * (9 * C) ** (-0.5), 'bn1_scale': jnp.ones((HIDDEN,), jnp.float32), 'bn1_shift': jnp.zeros((HIDDEN,), jnp.float32), 'w_ffn2': jax.random.normal(ks[5], (1, 1, HIDDEN, C), jnp.float32) * HIDDEN ** (-0.5), 'bn2_scale': jnp.ones((C,), jnp.float32), 'bn2_shift': jnp.zeros((C,), jnp.float32)}
    _L1_conv_all = _L1_conv_setup()
    _L1_conv_in = {k: v for k, v in _L1_conv_all.items() if k in ('ln1_g', 'ln1_b', 'w_qkv', 'b_qkv', 'bias_table', 'w_proj', 'b_proj', 'ln2_g', 'ln2_b', 'w_ffn1', 'bn1_scale', 'bn1_shift', 'w_ffn2', 'bn2_scale', 'bn2_shift')}
    del _L1_conv_all
    return {'x': x, 'L0_conv_W1': _L0_conv_in['W1'], 'L0_conv_b1': _L0_conv_in['b1'], 'L0_conv_W2': _L0_conv_in['W2'], 'L0_conv_b2': _L0_conv_in['b2'], 'L0_conv_mask_token': _L0_conv_in['mask_token'], 'L0_conv_Wh': _L0_conv_in['Wh'], 'L0_conv_bh': _L0_conv_in['bh'], 'L0_conv_Wd': _L0_conv_in['Wd'], 'L0_conv_bd': _L0_conv_in['bd'], 'L0_conv_Wu': _L0_conv_in['Wu'], 'L0_conv_bu': _L0_conv_in['bu'], 'L1_conv_ln1_g': _L1_conv_in['ln1_g'], 'L1_conv_ln1_b': _L1_conv_in['ln1_b'], 'L1_conv_w_qkv': _L1_conv_in['w_qkv'], 'L1_conv_b_qkv': _L1_conv_in['b_qkv'], 'L1_conv_bias_table': _L1_conv_in['bias_table'], 'L1_conv_w_proj': _L1_conv_in['w_proj'], 'L1_conv_b_proj': _L1_conv_in['b_proj'], 'L1_conv_ln2_g': _L1_conv_in['ln2_g'], 'L1_conv_ln2_b': _L1_conv_in['ln2_b'], 'L1_conv_w_ffn1': _L1_conv_in['w_ffn1'], 'L1_conv_bn1_scale': _L1_conv_in['bn1_scale'], 'L1_conv_bn1_shift': _L1_conv_in['bn1_shift'], 'L1_conv_w_ffn2': _L1_conv_in['w_ffn2'], 'L1_conv_bn2_scale': _L1_conv_in['bn2_scale'], 'L1_conv_bn2_shift': _L1_conv_in['bn2_shift']}

def reference(x, L0_conv_W1, L0_conv_b1, L0_conv_W2, L0_conv_b2, L0_conv_mask_token, L0_conv_Wh, L0_conv_bh, L0_conv_Wd, L0_conv_bd, L0_conv_Wu, L0_conv_bu, L1_conv_ln1_g, L1_conv_ln1_b, L1_conv_w_qkv, L1_conv_b_qkv, L1_conv_bias_table, L1_conv_w_proj, L1_conv_b_proj, L1_conv_ln2_g, L1_conv_ln2_b, L1_conv_w_ffn1, L1_conv_bn1_scale, L1_conv_bn1_shift, L1_conv_w_ffn2, L1_conv_bn2_scale, L1_conv_bn2_shift):
    import jax
    import jax.numpy as jnp

    def _L0_conv_ref(x, W1, b1, W2, b2, mask_token, Wh, bh, Wd, bd, Wu, bu):
        import jax, jax.numpy as jnp
        import numpy as np
        from jax import lax

        def quick_gelu(x):
            return x * jax.nn.sigmoid(1.702 * x)
        B, H, W_, C = x.shape
        D = Wd.shape[0]
        M = mask_token.shape[0]
        pf = jax.nn.relu(jnp.einsum('bhwc,kc->bhwk', x, W1) + b1)
        pf = jnp.einsum('bhwk,jk->bhwj', pf, W2) + b2
        mask = jnp.einsum('bhwk,mk->mbhw', pf, mask_token)
        mask = jax.nn.softmax(mask.reshape(M, B, -1), axis=-1).reshape(M, B, H, W_)
        mwf = (mask.sum(0)[..., None] * pf).sum(axis=(1, 2))
        conv_w = (jnp.einsum('bk,ok->bo', mwf, Wh) + bh).reshape(B, D, D, 3, 3)
        xd = jnp.einsum('bhwc,dc->bhwd', x, Wd) + bd
        xp = quick_gelu(xd.transpose(0, 3, 1, 2))

        def conv1(xi, wi):
            return lax.conv_general_dilated(xi[None], wi, (1, 1), [(1, 1), (1, 1)])[0]
        xc = jax.vmap(conv1)(xp, conv_w)
        xd2 = quick_gelu(xc.transpose(0, 2, 3, 1))
        xu = jnp.einsum('bhwd,cd->bhwc', xd2, Wu) + bu
        return xu + x

    def _L1_conv_ref(x, ln1_g, ln1_b, w_qkv, b_qkv, bias_table, w_proj, b_proj, ln2_g, ln2_b, w_ffn1, bn1_scale, bn1_shift, w_ffn2, bn2_scale, bn2_shift):
        import jax, jax.numpy as jnp
        import numpy as np
        B, H, W, C = (32, 56, 56, 48)
        WS, SHIFT, HEADS = (7, 3, 6)
        HEAD_DIM = C // HEADS
        SCALE = 0.17677669529663687
        HIDDEN = 4 * C
        N = WS * WS
        EPS = 0.001

        def _rel_index(ws):
            coords = np.stack(np.meshgrid(np.arange(ws), np.arange(ws), indexing='ij')).reshape(2, -1)
            rel = (coords[:, :, None] - coords[:, None, :]).transpose(1, 2, 0)
            rel[:, :, 0] += ws - 1
            rel[:, :, 1] += ws - 1
            rel[:, :, 0] *= 2 * ws - 1
            return rel.sum(-1)

        def _attn_mask(h, w, ws, ss):
            img = np.zeros((h, w), np.float32)
            cnt = 0
            for hs in (slice(0, -ws), slice(-ws, -ss), slice(-ss, None)):
                for wsl in (slice(0, -ws), slice(-ws, -ss), slice(-ss, None)):
                    img[hs, wsl] = cnt
                    cnt += 1
            win = img.reshape(h // ws, ws, w // ws, ws).transpose(0, 2, 1, 3).reshape(-1, ws * ws)
            diff = win[:, None, :] - win[:, :, None]
            return np.where(diff != 0, -100.0, 0.0).astype(np.float32)
        REL_IDX = jnp.asarray(_rel_index(WS).reshape(-1))
        ATTN_MASK = jnp.asarray(_attn_mask(H, W, WS, SHIFT))
        NW = ATTN_MASK.shape[0]

        def _window_partition(x, ws):
            b, h, w, c = x.shape
            x = x.reshape(b, h // ws, ws, w // ws, ws, c).transpose(0, 1, 3, 2, 4, 5)
            return x.reshape(-1, ws, ws, c)

        def _window_reverse(x, ws, h, w):
            c = x.shape[-1]
            x = x.reshape(-1, h // ws, w // ws, ws, ws, c).transpose(0, 1, 3, 2, 4, 5)
            return x.reshape(-1, h, w, c)

        def _layer_norm(x, g, b):
            mu = jnp.mean(x, axis=-1, keepdims=True)
            var = jnp.var(x, axis=-1, keepdims=True)
            return (x - mu) * jax.lax.rsqrt(var + EPS) * g + b

        def _forward(x, ln1_g, ln1_b, w_qkv, b_qkv, bias_table, w_proj, b_proj, ln2_g, ln2_b, w_ffn1, bn1_scale, bn1_shift, w_ffn2, bn2_scale, bn2_shift):
            shortcut = x
            h = _layer_norm(x, ln1_g, ln1_b)
            h = jnp.roll(h, (-SHIFT, -SHIFT), axis=(1, 2))
            xw = _window_partition(h, WS).reshape(-1, N, C)
            qkv = xw @ w_qkv + b_qkv
            qkv = qkv.reshape(-1, N, 3, HEADS, HEAD_DIM).transpose(2, 0, 3, 1, 4)
            q, k, v = (qkv[0] * SCALE, qkv[1], qkv[2])
            attn = jnp.einsum('whnd,whmd->whnm', q, k)
            rel_bias = bias_table[REL_IDX].reshape(N, N, HEADS).transpose(2, 0, 1)
            attn = attn + rel_bias[None]
            attn = attn.reshape(-1, NW, HEADS, N, N) + ATTN_MASK[None, :, None]
            attn = jax.nn.softmax(attn.reshape(-1, HEADS, N, N), axis=-1)
            o = jnp.einsum('whnm,whmd->whnd', attn, v)
            o = o.transpose(0, 2, 1, 3).reshape(-1, N, C)
            o = o @ w_proj + b_proj
            o = _window_reverse(o.reshape(-1, WS, WS, C), WS, H, W)
            o = jnp.roll(o, (SHIFT, SHIFT), axis=(1, 2))
            x = shortcut + o
            y = _layer_norm(x, ln2_g, ln2_b)
            dn = ('NHWC', 'HWIO', 'NHWC')
            y = jax.lax.conv_general_dilated(y, w_ffn1, (1, 1), 'SAME', dimension_numbers=dn)
            y = y * bn1_scale + bn1_shift
            y = jax.nn.gelu(y, approximate=False)
            y = jax.lax.conv_general_dilated(y, w_ffn2, (1, 1), 'SAME', dimension_numbers=dn)
            y = y * bn2_scale + bn2_shift
            return x + y
        return _forward(x, ln1_g, ln1_b, w_qkv, b_qkv, bias_table, w_proj, b_proj, ln2_g, ln2_b, w_ffn1, bn1_scale, bn1_shift, w_ffn2, bn2_scale, bn2_shift)

    def _gn(v, G=32, eps=1e-05):
        B_, H_, W_, C_ = v.shape
        g = v.reshape(B_, H_, W_, G, C_ // G)
        m = jnp.mean(g, axis=(1, 2, 4), keepdims=True)
        s = jnp.var(g, axis=(1, 2, 4), keepdims=True)
        return ((g - m) / jnp.sqrt(s + eps)).reshape(v.shape)

    def _ln_c(v, eps=1e-06):
        m = jnp.mean(v, axis=-1, keepdims=True)
        s = jnp.var(v, axis=-1, keepdims=True)
        return (v - m) / jnp.sqrt(s + eps)

    def _ln_t(v, eps=1e-05):
        m = jnp.mean(v, axis=-1, keepdims=True)
        s = jnp.var(v, axis=-1, keepdims=True)
        return (v - m) / jnp.sqrt(s + eps)

    def _to_tokens(v):
        B_, H_, W_, C_ = v.shape
        return v.reshape(B_, H_ * W_, C_)

    def _from_tokens(t, like):
        return t.reshape(like.shape)
    x = _L0_conv_ref(x, L0_conv_W1, L0_conv_b1, L0_conv_W2, L0_conv_b2, L0_conv_mask_token, L0_conv_Wh, L0_conv_bh, L0_conv_Wd, L0_conv_bd, L0_conv_Wu, L0_conv_bu)
    x = _L1_conv_ref(x, L1_conv_ln1_g, L1_conv_ln1_b, L1_conv_w_qkv, L1_conv_b_qkv, L1_conv_bias_table, L1_conv_w_proj, L1_conv_b_proj, L1_conv_ln2_g, L1_conv_ln2_b, L1_conv_w_ffn1, L1_conv_bn1_scale, L1_conv_bn1_shift, L1_conv_w_ffn2, L1_conv_bn2_scale, L1_conv_bn2_shift)
    return x

_drawn_inputs = setup_inputs


def setup_inputs(seed=0):
    import zlib

    import numpy as np

    out = dict(_drawn_inputs(seed))
    spreads = {'L0_conv_b1': (0.0, 0.8),
     'L0_conv_b2': (0.0, 0.8),
     'L0_conv_bd': (0.0, 0.8),
     'L0_conv_bu': (0.0, 2.0),
     'L1_conv_ln1_g': (1.0, 0.6),
     'L1_conv_ln1_b': (0.0, 0.8),
     'L1_conv_b_qkv': (0.0, 0.8),
     'L1_conv_b_proj': (0.0, 2.0),
     'L1_conv_ln2_g': (1.0, 0.6),
     'L1_conv_ln2_b': (0.0, 0.8),
     'L1_conv_bn1_scale': (1.0, 0.6),
     'L1_conv_bn1_shift': (0.0, 2.0),
     'L1_conv_bn2_scale': (1.0, 0.6),
     'L1_conv_bn2_shift': (0.0, 2.0)}
    factors = {'L0_conv_W1': 8.0,
     'L0_conv_W2': 8.0,
     'L0_conv_mask_token': 8.0,
     'L0_conv_Wh': 7.467,
     'L0_conv_bh': 32.769,
     'L0_conv_Wd': 8.0,
     'L0_conv_Wu': 7.821,
     'L1_conv_bias_table': 64.0,
     'L1_conv_w_qkv': 8.0,
     'L1_conv_w_proj': 8.0,
     'L1_conv_w_ffn1': 8.0,
     'L1_conv_w_ffn2': 8.0}
    for name, (base, spread) in spreads.items():
        noise = np.random.default_rng([zlib.crc32(name.encode()), seed]).standard_normal(out[name].shape)
        drawn = base * np.exp(spread * noise) if base else spread * noise
        out[name] = jnp.asarray(drawn.astype(out[name].dtype))
    for name, factor in factors.items():
        out[name] = (out[name] * factor).astype(out[name].dtype)
    return out
```

```python
from contextlib import ExitStack

import numpy as np

import concourse.bass as bass
from concourse import mybir

F32 = mybir.dt.float32
ALU = mybir.AluOpType
ACT = mybir.ActivationFunctionType
AX = mybir.AxisListType

B, H, W, C = 32, 56, 56, 48
D, M = 16, 8
WS, SHIFT, HEADS = 7, 3, 6
HD = C // HEADS
HID = 4 * C
N = WS * WS
NWC = W // WS
HW = H * W
SCALE = 0.17677669529663687
EPS = 1e-3
TAPS = 9

GI = 128 // D
PAIRS = GI // 2
GROUPS = B // GI
P1 = 2 * C
R1 = 8
T1 = R1 * W
C1 = H // R1
STORES = 3

BO = 64
PP = BO + C
T2 = WS * W
RC = H // WS
CHUNKS = RC * B // 2
OP = BO + C + HEADS
HN = HEADS * N
DUOS = NWC // 2
YW = W + 2
TY = WS * YW
XP = W + SHIFT


class Pack:

    def __init__(self, shapes):
        self.place, self.width = {}, 0
        for name, (rows, cols) in shapes.items():
            self.place[name] = (rows, self.width, cols)
            self.width += cols

    def at(self, tile, name):
        rows, start, cols = self.place[name]
        return tile[0:rows, start:start + cols]

    def filled(self, arrays):
        out = np.zeros((128, self.width), np.float32)
        for name, (rows, start, cols) in self.place.items():
            out[0:rows, start:start + cols] = arrays[name].reshape(rows, cols)
        return out


PACK1 = Pack({
    "w1": (P1, PAIRS * 128), "wd": (P1, PAIRS * 128), "w2": (128, 128), "mt": (128, GI * M),
    "wh": (128, 2 * TAPS * D), "bh": (D, TAPS * D), "wu": (128, PAIRS * P1),
    "b1": (128, 1), "b2": (128, 1), "bd": (128, 1), "bu": (P1, 1),
    "same_image": (GI * M, 128), "same_k": (128, 128), "image": (128, GI), "ci": (128, 2 * D),
    "spread_ci": (D, 128),
})
PACK2 = Pack({
    "wq": (PP, PP), "wk": (PP, PP), "wv": (PP, 2 * C), "wvd": (PP, PP), "wp": (PP, PP),
    "g1": (PP, 1), "be1": (PP, 1), "bq": (PP, 1), "bk": (PP, 1), "bv": (PP, 1), "bp": (PP, 1),
    "g2": (PP, 1), "be2": (PP, 1), "rel": (2 * N, HN), "masked": (2 * N, 4 * N),
    "center": (PP, PP), "mean": (PP, PP), "head": (PP, HEADS), "eps": (PP, 1),
    "vhead": (2 * N, HEADS // 2 * C), "vones": (2 * N, HEADS // 2 * HEADS), "den": (OP, PP),
    "ident": (2 * N, 2 * N),
})
PACK3 = Pack({
    "wa": (128, 3 * HID), "wb": (C, HID), "wf2": (HID // 2, 2 * C),
    "s1": (HID // 2, 2), "t1": (HID // 2, 2), "s2": (C, 1), "t2": (C, 1),
})


def layer0(nc, x, pack, x1s):
    ctx = ExitStack()
    with ctx:
        def sb(name, shape):
            return ctx.enter_context(nc.sbuf_tensor(name, shape, F32))

        def sem(name):
            return ctx.enter_context(nc.semaphore(name))

        cw = sb("cw1", [128, PACK1.width])
        xt = [sb(f"xt{k}", [P1, PAIRS, HW]) for k in range(2)]
        hidden = sb("hidden", [128, 2, T1])
        feat = sb("feat", [128, HW])
        mask = sb("mask", [GI * M, HW])
        down = sb("down", [128, H + 2, W + 2])
        conv = sb("conv", [128, 2, T1])
        cwt = sb("cwt", [128, TAPS, GI, D])
        prod = sb("prod", [128, T1])
        part = sb("part", [128, C1])
        mwf = sb("mwf", [128, 1])
        mdiag = sb("mdiag", [128, GI])
        mrep = sb("mrep", [128, 2, GI, D])
        lmax = sb("lmax", [GI * M, 1])
        nmax = sb("nmax", [GI * M, 1])
        lsum = sb("lsum", [GI * M, 1])
        rsum = sb("rsum", [GI * M, 1])
        msel = sb("msel", [GI * M, 128])
        ps = [ctx.enter_context(nc.psum_tensor(f"pa{i}", [128, 512], F32)) for i in range(8)]

        weights_in = sem("l0_weights_in")
        x_in = [sem(f"l0_x_in{k}") for k in range(2)]
        x_out = [sem(f"l0_x_out{k}") for k in range(2)]
        pad_zero = sem("l0_pad_zero")
        w1_done, wd_done, w2_done, mt_done = sem("w1_done"), sem("wd_done"), sem("w2_done"), sem("mt_done")
        relu_done, down_done, feat_done, logit_done = sem("relu_done"), sem("down_done"), sem("feat_done"), sem("logit_done")
        lmax_done, nmax_done, exp_done, rsum_done, msel_done = (
            sem("lmax_done"), sem("nmax_done"), sem("l0_exp_done"), sem("rsum_done"), sem("msel_done"))
        msum_done, part_done, mwf_done, mdiag_done = sem("msum_done"), sem("part_done"), sem("mwf_done"), sem("mdiag_done")
        rep_done, mrep_done, cw_done, cwt_done = sem("rep_done"), sem("mrep_done"), sem("cw_done"), sem("cwt_done")
        conv_done, gelu_done, up_done, x1_done = sem("conv_done"), sem("gelu_done"), sem("up_done"), sem("x1_done")

        def w(name):
            return PACK1.at(cw, name)

        w1 = w("w1").rearrange("c (p m) -> c p m", p=PAIRS)
        wd = w("wd").rearrange("c (p m) -> c p m", p=PAIRS)
        wh = w("wh").rearrange("c (s n) -> c s n", s=2)
        wu = w("wu").rearrange("c (p m) -> c p m", p=PAIRS)
        ci = w("ci").rearrange("c (s n) -> c s n", s=2)

        def cols(c):
            return slice(c * T1, (c + 1) * T1)

        block = ctx.enter_context(nc.Block())

        @block.sync
        def _(sp):
            sp.dma_start(cw[:, :], pack).then_inc(weights_in, 16)

            def load(k, g):
                for p in range(PAIRS):
                    sp.dma_start(xt[k][:, p, :], x[bass.ds((g * PAIRS + p) * P1, P1), :]).then_inc(x_in[k], 16)

            def store(k, g):
                whole = (RC - 1) * T2
                start, wrap = SHIFT * W, SHIFT * W
                for p in range(PAIRS):
                    pair = g * PAIRS + p
                    sp.dma_start(x1s[0:RC - 1, pair, :, :].rearrange("n c t -> c n t"),
                                 xt[k][:, p, start:start + whole].rearrange("c (n t) -> c n t", n=RC - 1)).then_inc(x_out[k], 16)
                    sp.dma_start(x1s[RC - 1, pair, :, 0:T2 - wrap], xt[k][:, p, start + whole:HW]).then_inc(x_out[k], 16)
                    sp.dma_start(x1s[RC - 1, pair, :, T2 - wrap:T2], xt[k][:, p, 0:wrap]).then_inc(x_out[k], 16)

            for k in range(2):
                load(k, k)
            for g in range(GROUPS):
                k = g % 2
                sp.wait_ge(x1_done, (g + 1) * C1 * PAIRS)
                store(k, g)
                if g + 2 < GROUPS:
                    sp.wait_ge(x_out[k], (g // 2 + 1) * PAIRS * STORES * 16)
                    load(k, g + 2)
            for k in range(2):
                sp.wait_ge(x_out[k], GROUPS // 2 * PAIRS * STORES * 16)

        @block.gpsimd
        def _(pool):
            pool.memset(down[:, :, :], 0.0).then_inc(pad_zero, 1)

        @block.tensor
        def _(pe):
            pe.wait_ge(weights_in, 16)
            with pe.Fori(0, GROUPS // 2) as gg:
                for k in range(2):
                    g = gg * 2 + k
                    pe.wait_ge(x_in[k], gg * (PAIRS * 16) + PAIRS * 16)
                    for c in range(C1 + 2):
                        if c < C1:
                            if c >= 2:
                                pe.wait_ge(relu_done, g * C1 + c - 1)
                            for p in range(PAIRS):
                                mm = pe.matmul(ps[c % 2][:, 0:T1], w1[:, p, :], xt[k][:, p, cols(c)],
                                               start=p == 0, stop=p == PAIRS - 1)
                            mm.then_inc(w1_done, 1)
                            if c >= 2:
                                pe.wait_ge(down_done, g * C1 + c - 1)
                            if c == 0:
                                pe.wait_ge(x1_done, g * (C1 * PAIRS))
                            for p in range(PAIRS):
                                mm = pe.matmul(ps[2 + c % 2][:, 0:T1], wd[:, p, :], xt[k][:, p, cols(c)],
                                               start=p == 0, stop=p == PAIRS - 1)
                            mm.then_inc(wd_done, 1)
                        if 1 <= c <= C1:
                            pe.wait_ge(relu_done, g * C1 + c)
                            if c >= 3:
                                pe.wait_ge(feat_done, g * C1 + c - 2)
                            pe.matmul(ps[4 + (c - 1) % 2][:, 0:T1], w("w2"), hidden[:, (c - 1) % 2, :],
                                      start=True, stop=True).then_inc(w2_done, 1)
                        if c >= 2:
                            pe.wait_ge(feat_done, g * C1 + c - 1)
                            if c >= 4:
                                pe.wait_ge(logit_done, g * C1 + c - 3)
                            pe.matmul(ps[6 + c % 2][0:GI * M, 0:T1], w("mt"), feat[:, cols(c - 2)],
                                      start=True, stop=True).then_inc(mt_done, 1)
                    pe.wait_ge(msel_done, g + 1)
                    for c in range(C1):
                        if c >= 2:
                            pe.wait_ge(part_done, g * C1 + c - 1)
                        pe.matmul(ps[6 + c % 2][:, 0:T1], msel[:, :], mask[:, cols(c)],
                                  start=True, stop=True).then_inc(msum_done, 1)
                    pe.wait_ge(mdiag_done, g + 1)
                    pe.matmul(ps[4][:, 0:GI], w("same_k"), mdiag[:, :], start=True, stop=True).then_inc(rep_done, 1)
                    pe.wait_ge(mrep_done, 2 * g + 2)
                    for s in range(2):
                        pe.matmul(ps[5][:, 0:TAPS * D], mrep[:, s, :, :].rearrange("q i c -> q (i c)"), wh[:, s, :],
                                  start=s == 0, stop=False)
                    pe.matmul(ps[5][:, 0:TAPS * D], w("spread_ci"), w("bh"), start=False, stop=True).then_inc(cw_done, 1)
                    pe.wait_ge(cwt_done, g + 1)
                    for c in range(C1 + 1):
                        if c < C1:
                            if c >= 2:
                                pe.wait_ge(gelu_done, g * C1 + c - 1)
                            for t in range(TAPS):
                                mm = pe.matmul(ps[c % 2][:, 0:T1], cwt[:, t, :, :].rearrange("q i c -> q (i c)"),
                                               down[:, c * R1 + t // 3:c * R1 + t // 3 + R1, t % 3:t % 3 + W],
                                               start=t == 0, stop=t == TAPS - 1)
                            mm.then_inc(conv_done, 1)
                        if c >= 1:
                            pe.wait_ge(gelu_done, g * C1 + c)
                            for p in range(PAIRS):
                                if c >= 2:
                                    pe.wait_ge(x1_done, (g * C1 + c - 2) * PAIRS + p + 1)
                                pe.matmul(ps[2 + p][0:P1, 0:T1], wu[:, p, :], conv[:, (c - 1) % 2, :],
                                          start=True, stop=True).then_inc(up_done, 1)

        @block.scalar
        def _(act):
            act.wait_ge(weights_in, 16)
            act.wait_ge(pad_zero, 1)
            with act.Fori(0, GROUPS // 2) as gg:
                for k in range(2):
                    g = gg * 2 + k
                    for c in range(C1):
                        act.wait_ge(w1_done, g * C1 + c + 1)
                        if c >= 2:
                            act.wait_ge(w2_done, g * C1 + c - 1)
                        act.activation(hidden[:, c % 2, :], ps[c % 2][:, 0:T1], ACT.Relu,
                                       bias=w("b1")).then_inc(relu_done, 1)
                        act.wait_ge(wd_done, g * C1 + c + 1)
                        act.activation(down[:, 1 + c * R1:1 + (c + 1) * R1, 1:1 + W],
                                       ps[2 + c % 2][:, 0:T1].rearrange("q (r n) -> q r n", r=R1),
                                       ACT.Gelu_apprx_sigmoid, bias=w("bd")).then_inc(down_done, 1)
                    act.wait_ge(nmax_done, g + 1)
                    act.activation(mask[:, :], mask[:, :], ACT.Exp, bias=nmax[:, :],
                                   accum_out=lsum[:, :]).then_inc(exp_done, 1)
                    for c in range(C1):
                        act.wait_ge(conv_done, g * C1 + c + 1)
                        if c >= 2:
                            act.wait_ge(up_done, (g * C1 + c - 1) * PAIRS)
                        act.activation(conv[:, c % 2, :], ps[c % 2][:, 0:T1],
                                       ACT.Gelu_apprx_sigmoid).then_inc(gelu_done, 1)

        @block.vector
        def _(dve):
            dve.wait_ge(weights_in, 16)
            with dve.Fori(0, GROUPS // 2) as gg:
                for k in range(2):
                    g = gg * 2 + k
                    for c in range(C1 + 1):
                        if c < C1:
                            dve.wait_ge(w2_done, g * C1 + c + 1)
                            dve.tensor_scalar(feat[:, cols(c)], ps[4 + c % 2][:, 0:T1], w("b2"), None,
                                              op0=ALU.add).then_inc(feat_done, 1)
                        if c >= 1:
                            dve.wait_ge(mt_done, g * C1 + c)
                            dve.tensor_copy(mask[:, cols(c - 1)], ps[6 + (c - 1) % 2][0:GI * M, 0:T1]).then_inc(logit_done, 1)
                    dve.wait_ge(logit_done, g * C1 + C1)
                    dve.tensor_reduce(lmax[:, :], mask[:, :], AX.X, ALU.max).then_inc(lmax_done, 1)
                    dve.wait_ge(lmax_done, g + 1)
                    dve.tensor_scalar(nmax[:, :], lmax[:, :], -1.0, None, op0=ALU.mult).then_inc(nmax_done, 1)
                    dve.wait_ge(exp_done, g + 1)
                    dve.reciprocal(rsum[:, :], lsum[:, :]).then_inc(rsum_done, 1)
                    dve.wait_ge(rsum_done, g + 1)
                    dve.tensor_scalar(msel[:, :], w("same_image"), rsum[:, 0:1], None, op0=ALU.mult).then_inc(msel_done, 1)
                    for c in range(C1):
                        dve.wait_ge(msum_done, g * C1 + c + 1)
                        dve.wait_ge(part_done, g * C1 + c)
                        dve.tensor_tensor_reduce(out=prod[:, :], in0=ps[6 + c % 2][:, 0:T1], in1=feat[:, cols(c)],
                                                 scale=1.0, scalar=0.0, op0=ALU.mult, op1=ALU.add,
                                                 accum_out=part[:, c:c + 1]).then_inc(part_done, 1)
                    dve.wait_ge(part_done, g * C1 + C1)
                    dve.reduce_sum(mwf[:, :], part[:, :], AX.X).then_inc(mwf_done, 1)
                    dve.wait_ge(mwf_done, g + 1)
                    dve.tensor_scalar(mdiag[:, :], w("image"), mwf[:, 0:1], None, op0=ALU.mult).then_inc(mdiag_done, 1)
                    dve.wait_ge(rep_done, g + 1)
                    for s in range(2):
                        dve.tensor_tensor(mrep[:, s, :, :], ps[4][:, 0:GI].unsqueeze(2).to_broadcast([128, GI, D]),
                                          ci[:, s, :].unsqueeze(1).to_broadcast([128, GI, D]),
                                          ALU.mult).then_inc(mrep_done, 1)
                    dve.wait_ge(cw_done, g + 1)
                    image = w("image")
                    for i in range(GI):
                        ins = dve.tensor_scalar(cwt[:, :, i, :], ps[5][:, 0:TAPS * D].rearrange("q (t c) -> q t c", t=TAPS),
                                                image[:, i:i + 1], None, op0=ALU.mult)
                    ins.then_inc(cwt_done, 1)
                    for c in range(C1):
                        for p in range(PAIRS):
                            dve.wait_ge(up_done, (g * C1 + c) * PAIRS + p + 1)
                            dve.scalar_tensor_tensor(out=xt[k][:, p, cols(c)], in0=ps[2 + p][0:P1, 0:T1],
                                                     scalar=w("bu"), in1=xt[k][:, p, cols(c)],
                                                     op0=ALU.add, op1=ALU.add).then_inc(x1_done, 1)


def attention(nc, x1s, pack, x2s, ys):
    ctx = ExitStack()
    with ctx:
        def sb(name, shape):
            return ctx.enter_context(nc.sbuf_tensor(name, shape, F32))

        def sem(name):
            return ctx.enter_context(nc.semaphore(name))

        cw = sb("cw2", [128, PACK2.width])
        wqs, wks, wvs = sb("wqs", [PP, PP]), sb("wks", [PP, PP]), sb("wvs", [PP, 2 * C])
        bqs, bks, bvs, bps = sb("bqs", [PP, 1]), sb("bks", [PP, 1]), sb("bvs", [PP, 1]), sb("bps", [PP, 1])
        bias = sb("bias", [2 * N, 2, 2, HN])
        xin = [sb(f"xin{a}", [PP, WS, XP]) for a in range(2)]
        xres = [sb(f"xres{a}", [PP, WS, W]) for a in range(2)]
        xc = sb("xc", [PP, T2])
        sq = sb("sq", [PP, T2])
        lnv = sb("lnv", [PP, T2])
        rstd = sb("rstd", [PP, T2])
        h = sb("h", [PP, NWC, 2, N])
        ks = sb("ks", [PP, NWC, N])
        qbd = [sb(f"qbd{a}", [PP, NWC, 2 * N]) for a in range(2)]
        kex = [sb(f"kex{a}", [PP, NWC, HEADS, N]) for a in range(2)]
        vex = [sb(f"vex{a}", [2 * N, NWC, HEADS // 2, OP]) for a in range(2)]
        s_sb = [sb(f"s{i}", [2 * N, 2, HN]) for i in range(2)]
        mx = [sb(f"mx{i}", [2 * N, 2, HEADS]) for i in range(2)]
        pt = [sb(f"pt{i}", [2 * N, 2, HN]) for i in range(2)]
        osb = [sb(f"osb{a}", [OP, WS, W]) for a in range(2)]
        rden = sb("rden", [PP, T2])
        odiv = sb("odiv", [PP, T2])
        xo = [sb(f"xo{a}", [PP, WS, W]) for a in range(2)]
        xc2, sq2, lnv2, rstd2 = sb("xc2", [PP, T2]), sb("sq2", [PP, T2]), sb("lnv2", [PP, T2]), sb("rstd2", [PP, T2])
        y = [sb(f"y{a}", [PP, WS, YW]) for a in range(2)]

        ps_s = [ctx.enter_context(nc.psum_tensor(f"ps_s{i}", [128, 2, 512], F32)) for i in range(2)]
        ps_t = ctx.enter_context(nc.psum_tensor("ps_t", [128, 2, 512], F32))
        ps_o = ctx.enter_context(nc.psum_tensor("ps_o", [128, 512], F32))
        ps_m = ctx.enter_context(nc.psum_tensor("ps_m", [128, 512], F32))

        weights_in, zeroed, vones_set = sem("at_weights_in"), sem("at_zeroed"), sem("vones_set")
        folded, bias_mm, biases, bp_mm, tables, pad_set = (
            sem("folded"), sem("bias_mm"), sem("biases"), sem("bp_mm"), sem("tables"), sem("pad_set"))
        x_in = [sem(f"at_x_in{a}") for a in range(2)]
        x2_out = [sem(f"x2_out{a}") for a in range(2)]
        y_out = [sem(f"y_out{a}") for a in range(2)]
        wrapped, xres_set = sem("wrapped"), sem("xres_set")
        center_mm, xc_copied, squared, var_mm, ln_done, rstd_done, h_done, h_twice = (
            sem("center_mm"), sem("xc_copied"), sem("squared"), sem("var_mm"), sem("ln_done"), sem("rstd_done"), sem("h_done"),
            sem("h_twice"))
        q_mm, q_set, k_mm, k_set, v_mm, v_set, kex_set = (
            sem("q_mm"), sem("q_set"), sem("k_mm"), sem("k_set"), sem("v_mm"), sem("v_set"), sem("kex_set"))
        o_set, den_mm, rden_set, odiv_set, proj_mm, x2_set = (
            sem("o_set"), sem("den_mm"), sem("rden_set"), sem("odiv_set"), sem("proj_mm"), sem("x2_set"))
        center2_mm, xc2_copied, squared2, var2_mm, ln2_done, rstd2_done, ymul_done, y_set = (
            sem("center2_mm"), sem("xc2_copied"), sem("squared2"), sem("var2_mm"), sem("ln2_done"), sem("rstd2_done"),
            sem("ymul_done"), sem("y_set"))
        s_mm, s_biased, max_done, shifted, exp_done, t_mm, pt_set, pv_mm = (
            sem("s_mm"), sem("s_biased"), sem("max_done"), sem("shifted"), sem("exp_done"), sem("t_mm"), sem("pt_set"), sem("pv_mm"))

        def w(name):
            return PACK2.at(cw, name)

        pairs = B // 2

        def each_chunk(body):
            split = (RC - 1) * pairs // 2
            last = CHUNKS // 2 - 1
            body(0, 0, 0, 0)
            body(1, 0, 1, 0)
            for low, start, end in ((0, 1, split), (1, split, last)):
                with body.engine.Fori(start, end) as m:
                    body(m * 2, m, 0, low)
                    body(m * 2 + 1, m, 1, low)
            body(CHUNKS - 2, last, 0, 1)
            body(CHUNKS - 1, last, 1, 1)

        def at_edges(n):
            if isinstance(n, int):
                return n >= 2, n >= 1, n + 1 < CHUNKS, n + 2 < CHUNKS
            return True, True, True, True

        def windows(ap):
            return ap.rearrange("c (r w k) -> c w r k", r=WS, w=NWC)

        block = ctx.enter_context(nc.Block())

        @block.sync
        def _(sp):
            sp.dma_start(cw[:, :], pack).then_inc(weights_in, 16)

            def load(n, a):
                for i in range(2):
                    sp.dma_start(xin[a][BO * i:BO * i + C, :, 0:W],
                                 x1s[n, C * i:C * i + C, :].rearrange("c (r n) -> c r n", r=WS)).then_inc(x_in[a], 16)

            def store(n, a):
                sp.wait_ge(x2_set, n + 1)
                sp.wait_ge(y_set, n + 1)
                for i in range(2):
                    sp.dma_start(x2s[n, C * i:C * i + C, :].rearrange("c (r n) -> c r n", r=WS),
                                 xo[a][BO * i:BO * i + C, :, :]).then_inc(x2_out[a], 16)
                    sp.dma_start(ys[n, C * i:C * i + C, :].rearrange("c (r n) -> c r n", r=WS),
                                 y[a][BO * i:BO * i + C, :, :]).then_inc(y_out[a], 16)

            def load_ahead(n, a):
                sp.wait_ge(xres_set, n + 1)
                sp.wait_ge(center_mm, n + 1)
                load(n + 2, a)

            sp.wait_ge(zeroed, 1)
            load(0, 0)
            load(1, 1)
            load_ahead(0, 0)
            load_ahead(1, 1)
            with sp.Fori(1, CHUNKS // 2 - 1) as m:
                for a in range(2):
                    load_ahead(m * 2 + a, a)
                    store(m * 2 + a - 2, a)
            for n in range(CHUNKS - 4, CHUNKS):
                store(n, n % 2)
            for a in range(2):
                sp.wait_ge(x2_out[a], CHUNKS // 2 * 32)
                sp.wait_ge(y_out[a], CHUNKS // 2 * 32)

        @block.gpsimd
        def _(pool):
            for a in range(2):
                pool.memset(qbd[a][:, :, :], 0.0)
                pool.memset(vex[a][:, :, :, :], 0.0)
                pool.memset(y[a][:, :, :], 0.0)
                ins = pool.memset(xin[a][:, :, :], 0.0)
            ins.then_inc(zeroed, 1)
            pool.wait_ge(zeroed, 1)
            pool.wait_ge(weights_in, 16)
            ones = w("vones").rearrange("q (j h) -> q j h", j=HEADS // 2)
            for a in range(2):
                for win in range(NWC):
                    for o in (C, BO + C):
                        ins = pool.tensor_copy(vex[a][:, win, :, o:o + HEADS], ones)
            ins.then_inc(vones_set, 1)

            def twice(n):
                pool.wait_ge(rstd_done, n + 1)
                if at_edges(n)[1]:
                    pool.wait_ge(v_mm, n * 2)
                pool.tensor_tensor(h[:, :, 1, :].rearrange("c w (r k) -> c w r k", r=WS), windows(xc[:, :]), windows(rstd[:, :]),
                                   ALU.mult).then_inc(h_twice, 1)

            def keys(n, a):
                pool.wait_ge(k_set, n + 1)
                for win in range(NWC):
                    if win == 0 and at_edges(n)[0]:
                        pool.wait_ge(s_mm, n * DUOS - DUOS)
                    ins = pool.tensor_tensor(kex[a][:, win, :, :],
                                             ks[:, win, :].unsqueeze(1).to_broadcast([PP, HEADS, N]),
                                             w("head").unsqueeze(2).to_broadcast([PP, HEADS, N]), ALU.mult)
                ins.then_inc(kex_set, 1)

            def divide(n, a):
                pool.wait_ge(rden_set, n + 1)
                if at_edges(n)[1]:
                    pool.wait_ge(proj_mm, n)
                pool.tensor_tensor(odiv[:, :], osb[a][0:PP, :, :].rearrange("c r n -> c (r n)"), rden[:, :],
                                   ALU.mult).then_inc(odiv_set, 1)

            def normalize2(n, m, a):
                pool.wait_ge(rstd2_done, n + 1)
                if at_edges(n)[0]:
                    pool.wait_ge(y_out[a], m * 32)
                pool.tensor_tensor(y[a][:, :, 1:1 + W], xc2[:, :].rearrange("c (r n) -> c r n", r=WS),
                                   rstd2[:, :].rearrange("c (r n) -> c r n", r=WS), ALU.mult).then_inc(ymul_done, 1)

            def body(n, m, a, low):
                before2, before, after, after2 = at_edges(n)
                if before2:
                    normalize2(n - 2, m - 1, a)
                if before:
                    divide(n - 1, 1 - a)
                if after:
                    twice(n + 1)
                    keys(n + 1, 1 - a)

            twice(0)
            keys(0, 0)
            body.engine = pool
            each_chunk(body)
            last = CHUNKS // 2 - 1
            normalize2(CHUNKS - 2, last, 0)
            divide(CHUNKS - 1, 1)
            normalize2(CHUNKS - 1, last, 1)

        @block.tensor
        def _(pe):
            pe.wait_ge(weights_in, 16)
            for i, name in enumerate(("wq", "wk", "wvd")):
                mm = pe.matmul(ps_m[0:PP, i:i + 1], w(name), w("be1"), start=True, stop=True)
            mm.then_inc(bias_mm, 1)
            pe.wait_ge(biases, 3)
            pe.matmul(ps_m[0:PP, 3:4], w("wp"), bvs[:, :], start=True, stop=True).then_inc(bp_mm, 1)
            pe.wait_ge(pad_set, 1)
            pe.wait_ge(folded, 3)

            def scores(n, d, a):
                t = n * DUOS + d
                if d == 0:
                    pe.wait_ge(q_set, n * 2 + 2)
                    pe.wait_ge(kex_set, n + 1)
                if not isinstance(n, int) or t >= 2:
                    pe.wait_ge(s_biased, t - 1)
                for i in range(2):
                    win = 2 * d + i
                    mm = pe.matmul(ps_s[d % 2][0:2 * N, i, 0:HN], qbd[a][:, win, :],
                                   kex[a][:, win, :, :].rearrange("c h k -> c (h k)"), start=True, stop=True)
                mm.then_inc(s_mm, 1)

            def transposes(n, d):
                t = n * DUOS + d
                pe.wait_ge(exp_done, t + 1)
                if not isinstance(n, int) or t >= 1:
                    pe.wait_ge(pt_set, t)
                for i in range(2):
                    for j in range(HEADS // 2):
                        part = slice(j * 2 * N, (j + 1) * 2 * N)
                        mm = pe.transpose(ps_t[0:2 * N, i, part], s_sb[d % 2][:, i, part], w("ident"))
                mm.then_inc(t_mm, 1)

            def values(n, d, a):
                t = n * DUOS + d
                pe.wait_ge(pt_set, t + 1)
                if d == 0:
                    pe.wait_ge(v_set, n * 2 + 2)
                if d % 2 == 0 and (not isinstance(n, int) or t >= 2):
                    pe.wait_ge(o_set, n * 2 + d // 2)
                for i in range(2):
                    win = 2 * d + i
                    for j in range(HEADS // 2):
                        mm = pe.matmul(ps_o[0:OP, (win % 4) * 2 * N:(win % 4 + 1) * 2 * N], vex[a][:, win, j, :],
                                       pt[d % 2][:, i, j * 2 * N:(j + 1) * 2 * N], start=j == 0, stop=j == HEADS // 2 - 1)
                mm.then_inc(pv_mm, 1)

            def misc(lhs, rhs, signal, rows=PP):
                pe.matmul(ps_m[0:PP, 0:T2], lhs, rhs, start=True, stop=True).then_inc(signal, 1)

            def center(n, a):
                pe.wait_ge(wrapped, n + 1)
                misc(w("center"), xin[a][:, :, SHIFT:XP], center_mm)

            def variance(n):
                pe.wait_ge(squared, n + 1)
                misc(w("mean"), sq[:, :], var_mm)

            def queries(n):
                pe.wait_ge(h_done, n + 1)
                misc(wqs[:, :], h[:, :, 0, :], q_mm)

            def keys(n):
                pe.wait_ge(q_set, n * 2 + 2)
                misc(wks[:, :], h[:, :, 0, :], k_mm)

            def value_rows(n, half):
                if half == 0:
                    pe.wait_ge(h_twice, n + 1)
                else:
                    pe.wait_ge(v_set, n * 2 + 1)
                for i in range(4):
                    win = 4 * half + i
                    mm = pe.matmul(ps_m[0:2 * N, i * 2 * C:(i + 1) * 2 * C],
                                   h[:, win, :, :].rearrange("c i k -> c (i k)"),
                                   wvs[:, :], start=True, stop=True)
                mm.then_inc(v_mm, 1)

            def denominators(n, a):
                pe.wait_ge(o_set, n * 2 + 2)
                misc(w("den"), osb[a][:, :, :].rearrange("c r n -> c (r n)"), den_mm)

            def project(n):
                pe.wait_ge(odiv_set, n + 1)
                misc(w("wp"), odiv[:, :], proj_mm)

            def center2(n, a):
                pe.wait_ge(x2_set, n + 1)
                misc(w("center"), xo[a][:, :, :], center2_mm)

            def variance2(n):
                pe.wait_ge(squared2, n + 1)
                misc(w("mean"), sq2[:, :], var2_mm)

            def body(n, m, a, low):
                before2, before, after, _ = at_edges(n)
                scores(n, 0, a)
                if before2:
                    variance2(n - 2)
                if before:
                    transposes(n - 1, DUOS - 1)
                if after:
                    if before2:
                        pe.wait_ge(ln2_done, n - 1)
                    else:
                        pe.wait_ge(v_set, n * 2 + 2)
                    center(n + 1, 1 - a)
                if before:
                    values(n - 1, DUOS - 1, 1 - a)

                scores(n, 1, a)
                if after:
                    variance(n + 1)
                transposes(n, 0)
                if before:
                    if after:
                        pe.wait_ge(ln_done, n + 2)
                    elif before2:
                        pe.wait_ge(ln2_done, n - 1)
                    denominators(n - 1, 1 - a)
                values(n, 0, a)

                scores(n, 2, a)
                if after:
                    if before:
                        pe.wait_ge(rden_set, n)
                    queries(n + 1)
                transposes(n, 1)
                if after:
                    keys(n + 1)
                values(n, 1, a)
                if before:
                    if after:
                        pe.wait_ge(k_set, n + 2)
                    project(n - 1)

                scores(n, 3, a)
                if after:
                    if before:
                        pe.wait_ge(x2_set, n)
                    else:
                        pe.wait_ge(k_set, n + 2)
                    value_rows(n + 1, 0)
                transposes(n, 2)
                if after:
                    value_rows(n + 1, 1)
                values(n, 2, a)
                if before:
                    if after:
                        pe.wait_ge(v_set, n * 2 + 4)
                    center2(n - 1, 1 - a)

            center(0, 0)
            variance(0)
            queries(0)
            keys(0)
            pe.wait_ge(k_set, 1)
            pe.wait_ge(vones_set, 1)
            value_rows(0, 0)
            value_rows(0, 1)
            pe.wait_ge(v_set, 2)
            body.engine = pe
            each_chunk(body)
            n = CHUNKS - 1
            variance2(n - 1)
            transposes(n, DUOS - 1)
            values(n, DUOS - 1, 1)
            pe.wait_ge(ln2_done, n)
            denominators(n, 1)
            project(n)
            center2(n, 1)
            variance2(n)

        @block.scalar
        def _(act):
            act.preload_act_table_set("natural_log_exp_and_others")

            def wrap(n, m, a):
                act.wait_ge(x_in[a], m * 32 + 32)
                act.activation(xin[a][:, :, W:XP], xin[a][:, :, 0:SHIFT], ACT.Copy).then_inc(wrapped, 1)

            def square(n):
                act.wait_ge(xc_copied, n + 1)
                act.activation(sq[:, :], xc[:, :], ACT.Square).then_inc(squared, 1)

            def rsqrt(n):
                act.wait_ge(var_mm, n + 1)
                act.activation(lnv[:, :], ps_m[0:PP, 0:T2], ACT.Ln, bias=w("eps")).then_inc(ln_done, 1)
                act.wait_ge(ln_done, n + 1)
                act.activation(rstd[:, :], lnv[:, :], ACT.Exp, scale=-0.5).then_inc(rstd_done, 1)

            def queries(n, a):
                act.wait_ge(q_mm, n + 1)
                if at_edges(n)[0]:
                    act.wait_ge(s_mm, n * DUOS - DUOS)
                for i in range(2):
                    rows = slice(BO * i, BO * i + C)
                    act.activation(qbd[a][rows, :, i * N:(i + 1) * N], ps_m[rows, 0:T2].rearrange("c (w k) -> c w k", w=NWC), ACT.Identity, bias=bqs[rows, :]).then_inc(q_set, 1)

            def keys(n):
                act.wait_ge(k_mm, n + 1)
                if at_edges(n)[1]:
                    act.wait_ge(kex_set, n)
                act.activation(ks[:, :, :], ps_m[0:PP, 0:T2].rearrange("c (w k) -> c w k", w=NWC),
                               ACT.Identity, bias=bks[:, :]).then_inc(k_set, 1)

            def exps(n, d):
                act.wait_ge(shifted, n * DUOS + d + 1)
                act.activation(s_sb[d % 2][:, :, :], s_sb[d % 2][:, :, :], ACT.Exp).then_inc(exp_done, 1)

            def transposed(n, d):
                t = n * DUOS + d
                act.wait_ge(t_mm, t + 1)
                if not isinstance(n, int) or t >= 2:
                    act.wait_ge(pv_mm, t - 1)
                act.activation(pt[d % 2][:, :, :], ps_t[0:2 * N, :, 0:HN], ACT.Copy).then_inc(pt_set, 1)

            def square2(n):
                act.wait_ge(xc2_copied, n + 1)
                act.activation(sq2[:, :], xc2[:, :], ACT.Square).then_inc(squared2, 1)

            def rsqrt2(n):
                act.wait_ge(var2_mm, n + 1)
                act.activation(lnv2[:, :], ps_m[0:PP, 0:T2], ACT.Ln, bias=w("eps")).then_inc(ln2_done, 1)
                act.wait_ge(ln2_done, n + 1)
                if at_edges(n)[1]:
                    act.wait_ge(ymul_done, n)
                act.activation(rstd2[:, :], lnv2[:, :], ACT.Exp, scale=-0.5).then_inc(rstd2_done, 1)

            def body(n, m, a, low):
                before2, before, after, after2 = at_edges(n)
                if before2:
                    rsqrt2(n - 2)
                if before:
                    transposed(n - 1, DUOS - 1)
                exps(n, 0)
                if after:
                    square(n + 1)
                    rsqrt(n + 1)
                transposed(n, 0)
                exps(n, 1)
                if after:
                    queries(n + 1, 1 - a)
                transposed(n, 1)
                if after:
                    keys(n + 1)
                exps(n, 2)
                transposed(n, 2)
                exps(n, 3)
                if before:
                    square2(n - 1)
                if after2:
                    wrap(n + 2, m + 1, a)

            act.wait_ge(weights_in, 16)
            wrap(0, 0, 0)
            wrap(1, 0, 1)
            square(0)
            rsqrt(0)
            act.wait_ge(biases, 4)
            act.wait_ge(zeroed, 1)
            queries(0, 0)
            keys(0)
            body.engine = act
            each_chunk(body)
            n = CHUNKS - 1
            rsqrt2(n - 1)
            transposed(n, DUOS - 1)
            square2(n)
            rsqrt2(n)

        @block.vector
        def _(dve):
            dve.wait_ge(weights_in, 16)
            dve.tensor_scalar(wqs[:, :], w("wq"), w("g1"), SCALE, op0=ALU.mult, op1=ALU.mult).then_inc(folded, 1)
            dve.tensor_scalar(wks[:, :], w("wk"), w("g1"), None, op0=ALU.mult).then_inc(folded, 1)
            dve.tensor_scalar(wvs[:, :], w("wv"), w("g1"), None, op0=ALU.mult).then_inc(folded, 1)
            masked = w("masked").rearrange("q (s k) -> q s k", s=4)
            for s in range(4):
                dve.tensor_tensor(bias[:, s // 2, s % 2, :].rearrange("q (h k) -> q h k", h=HEADS),
                                  w("rel").rearrange("q (h k) -> q h k", h=HEADS),
                                  masked[:, s, :].unsqueeze(1).to_broadcast([2 * N, HEADS, N]), ALU.add).then_inc(tables, 1)
            dve.wait_ge(bias_mm, 1)
            dve.tensor_scalar(bqs[:, :], ps_m[0:PP, 0:1], w("bq"), SCALE, op0=ALU.add, op1=ALU.mult).then_inc(biases, 1)
            dve.tensor_scalar(bks[:, :], ps_m[0:PP, 1:2], w("bk"), None, op0=ALU.add).then_inc(biases, 1)
            dve.tensor_scalar(bvs[:, :], ps_m[0:PP, 2:3], w("bv"), None, op0=ALU.add).then_inc(biases, 1)
            dve.wait_ge(bp_mm, 1)
            dve.tensor_scalar(bps[:, :], ps_m[0:PP, 3:4], w("bp"), None, op0=ALU.add).then_inc(biases, 1)
            dve.wait_ge(biases, 4)
            dve.wait_ge(tables, 4)
            dve.wait_ge(zeroed, 1)
            dve.engine_nop().then_inc(pad_set, 1)

            def softmax_shift(n, d, low):
                t = n * DUOS + d
                i = d % 2
                s4 = s_sb[i][:, :, :].rearrange("q w (h k) -> q (w h) k", h=HEADS)
                dve.wait_ge(s_mm, t + 1)
                if not isinstance(n, int) or t >= 2:
                    dve.wait_ge(t_mm, t - 1)
                table = bias[:, low, :, :] if d == DUOS - 1 else bias[:, low, 0, :].unsqueeze(1).to_broadcast([2 * N, 2, HN])
                dve.tensor_tensor(s_sb[i][:, :, :], ps_s[i][0:2 * N, :, 0:HN], table, ALU.add).then_inc(s_biased, 1)
                dve.wait_ge(s_biased, t + 1)
                mxi = mx[i][:, :, :].rearrange("q w h -> q (w h)")
                dve.tensor_reduce(mxi, s4, AX.X, ALU.max).then_inc(max_done, 1)
                dve.wait_ge(max_done, t + 1)
                dve.tensor_tensor(s4, s4, mxi.unsqueeze(2).to_broadcast([2 * N, 2 * HEADS, N]),
                                  ALU.subtract).then_inc(shifted, 1)

            def center_copy(n):
                dve.wait_ge(center_mm, n + 1)
                dve.tensor_copy(xc[:, :], ps_m[0:PP, 0:T2]).then_inc(xc_copied, 1)

            def normalize(n):
                dve.wait_ge(rstd_done, n + 1)
                if at_edges(n)[1]:
                    dve.wait_ge(v_mm, n * 2)
                dve.tensor_tensor(h[:, :, 0, :].rearrange("c w (r k) -> c w r k", r=WS), windows(xc[:, :]), windows(rstd[:, :]),
                                  ALU.mult).then_inc(h_done, 1)

            def outputs(n, half, a):
                dve.wait_ge(pv_mm, n * DUOS + 2 * half + 2)
                for i, rows in enumerate((slice(0, BO), slice(BO, OP))):
                    ins = dve.tensor_copy(
                        osb[a][rows, :, half * 4 * WS:(half + 1) * 4 * WS].rearrange("c r (w k) -> c w r k", w=4),
                        ps_o[rows, 0:8 * N].rearrange("c (w i r k) -> c i w r k", w=4, i=2, r=WS)[:, i, :, :, :])
                ins.then_inc(o_set, 1)

            def reciprocals(n):
                dve.wait_ge(den_mm, n + 1)
                if at_edges(n)[1]:
                    dve.wait_ge(odiv_set, n)
                dve.reciprocal(rden[:, :], ps_m[0:PP, 0:T2]).then_inc(rden_set, 1)

            def residual(n, m, a):
                dve.wait_ge(proj_mm, n + 1)
                dve.wait_ge(xres_set, n + 1)
                if at_edges(n)[0]:
                    dve.wait_ge(x2_out[a], m * 32)
                rolled = ps_m[0:PP, 0:T2].rearrange("c (r n) -> c r n", r=WS)
                cut = W - SHIFT
                dve.tensor_tensor(xo[a][:, :, SHIFT:W], rolled[:, :, 0:cut], xres[a][:, :, 0:cut], ALU.add)
                dve.tensor_tensor(xo[a][:, :, 0:SHIFT], rolled[:, :, cut:W], xres[a][:, :, cut:W], ALU.add).then_inc(x2_set, 1)

            def residual_in(n, a):
                dve.wait_ge(wrapped, n + 1)
                if at_edges(n)[0]:
                    dve.wait_ge(x2_set, n - 1)
                dve.tensor_scalar(xres[a][:, :, :], xin[a][:, :, SHIFT:XP], bps[:, 0:1], None, op0=ALU.add).then_inc(xres_set, 1)

            def value_rows(n, half, a):
                dve.wait_ge(v_mm, n * 2 + half + 1)
                if half == 0 and at_edges(n)[0]:
                    dve.wait_ge(pv_mm, n * DUOS - DUOS)
                for i in range(4):
                    win = 4 * half + i
                    to = vex[a][:, win, :, :]
                    for k in range(2):
                        ins = dve.tensor_tensor(
                            to[:, :, BO * k:BO * k + C],
                            ps_m[0:2 * N, (i * 2 + k) * C:(i * 2 + k + 1) * C].unsqueeze(1).to_broadcast([2 * N, HEADS // 2, C]),
                            w("vhead").rearrange("q (j c) -> q j c", j=HEADS // 2), ALU.mult)
                ins.then_inc(v_set, 1)

            def center_copy2(n):
                dve.wait_ge(center2_mm, n + 1)
                if at_edges(n)[1]:
                    dve.wait_ge(ymul_done, n)
                dve.tensor_copy(xc2[:, :], ps_m[0:PP, 0:T2]).then_inc(xc2_copied, 1)

            def y_affine(n, a):
                dve.wait_ge(ymul_done, n + 1)
                dve.tensor_scalar(y[a][:, :, 1:1 + W], y[a][:, :, 1:1 + W], w("g2"), w("be2"),
                                  op0=ALU.mult, op1=ALU.add).then_inc(y_set, 1)

            def body(n, m, a, low):
                before2, before, after, _ = at_edges(n)
                softmax_shift(n, 0, low)
                if after:
                    center_copy(n + 1)
                if before:
                    outputs(n - 1, 1, 1 - a)
                softmax_shift(n, 1, low)
                if after:
                    normalize(n + 1)
                if before:
                    reciprocals(n - 1)
                if before2:
                    y_affine(n - 2, a)
                softmax_shift(n, 2, low)
                outputs(n, 0, a)
                if before:
                    residual(n - 1, m - 1 + a, 1 - a)
                if after:
                    residual_in(n + 1, 1 - a)
                softmax_shift(n, 3, low)
                if after:
                    value_rows(n + 1, 0, 1 - a)
                    value_rows(n + 1, 1, 1 - a)
                if before:
                    center_copy2(n - 1)

            center_copy(0)
            normalize(0)
            residual_in(0, 0)
            dve.wait_ge(vones_set, 1)
            value_rows(0, 0, 0)
            value_rows(0, 1, 0)
            body.engine = dve
            each_chunk(body)
            n = CHUNKS - 1
            outputs(n, 1, 1)
            y_affine(n - 1, 0)
            reciprocals(n)
            residual(n, CHUNKS // 2 - 1, 1)
            center_copy2(n)
            y_affine(n, 1)


def feed_forward(nc, x2s, ys, pack, out):
    ctx = ExitStack()
    with ctx:
        def sb(name, shape):
            return ctx.enter_context(nc.sbuf_tensor(name, shape, F32))

        def sem(name):
            return ctx.enter_context(nc.semaphore(name))

        half = HID // 2
        rest = 128 - 2 * C
        slots = 4
        cw = sb("cw3", [128, PACK3.width])
        ya = [sb(f"ya{a}", [128, H * YW]) for a in range(2)]
        yb = [sb(f"yb{a}", [C, H * YW]) for a in range(2)]
        xr = [sb(f"xr{a}", [C, HW]) for a in range(2)]
        hid = sb("hid", [half, slots, T1])
        ps_h = [ctx.enter_context(nc.psum_tensor(f"ps_h{i}", [128, 512], F32)) for i in range(slots)]
        ps_f = [ctx.enter_context(nc.psum_tensor(f"ps_f{i}", [128, 512], F32)) for i in range(2)]

        weights_in, zeroed = sem("ff_weights_in"), sem("ff_zeroed")
        y_in = [sem(f"y_in{a}") for a in range(2)]
        x2_in = [sem(f"x2_in{a}") for a in range(2)]
        out_done = [sem(f"out_done{a}") for a in range(2)]
        h_mm, gelu_done, f_mm, shift_added, result = sem("h_mm"), sem("ff_gelu_done"), sem("f_mm"), sem("shift_added"), sem("result")
        Y_DMAS, X_DMAS = 18, 3

        def w(name):
            return PACK3.at(cw, name)

        wa = w("wa").rearrange("q (k m) -> q k m", k=3)
        wf2 = w("wf2").rearrange("q (k m) -> q k m", k=2)
        block = ctx.enter_context(nc.Block())

        @block.sync
        def _(sp):
            sp.dma_start(cw[:, :], pack).then_inc(weights_in, 16)
            sp.wait_ge(zeroed, 1)

            def load_y(pair, a, tile, first, channels, shift, move):
                count = channels.stop - channels.start
                src = ys[:, pair, a * C + channels.start:a * C + channels.stop, :]
                mid = (RC - 1) * WS
                to = (SHIFT + 1 - shift) * YW - move
                sp.dma_start(tile[first:first + count, to:to + mid * YW].rearrange("c (n t) -> c n t", n=RC - 1),
                             src[0:RC - 1, :, :].rearrange("n c t -> c n t")).then_inc(y_in[a], 16)
                low = H - SHIFT - mid - (1 if shift == 0 else 0)
                to += mid * YW
                sp.dma_start(tile[first:first + count, to:to + low * YW], src[RC - 1, :, 0:low * YW]).then_inc(y_in[a], 16)
                skip = 1 if shift == 2 else 0
                start = (H - SHIFT - mid + skip) * YW + move
                size = (SHIFT - skip) * YW - move
                to = (skip + 1 - shift) * YW
                sp.dma_start(tile[first:first + count, to:to + size], src[RC - 1, :, start:start + size]).then_inc(y_in[a], 16)

            def load(pair, a):
                load_y(pair, a, ya[a], 0, slice(0, C), 0, 0)
                load_y(pair, a, ya[a], C, slice(0, C), 1, 0)
                load_y(pair, a, ya[a], 2 * C, slice(0, rest), 2, 0)
                for kw in range(3):
                    load_y(pair, a, yb[a], kw * (C - rest), slice(rest, C), 2, kw)
                src = x2s[:, pair, a * C:(a + 1) * C, :]
                mid, edge = (RC - 1) * T2, SHIFT * W
                sp.dma_start(xr[a][:, edge:edge + mid].rearrange("c (n t) -> c n t", n=RC - 1),
                             src[0:RC - 1, :, :].rearrange("n c t -> c n t")).then_inc(x2_in[a], 16)
                sp.dma_start(xr[a][:, edge + mid:HW], src[RC - 1, :, 0:T2 - edge]).then_inc(x2_in[a], 16)
                sp.dma_start(xr[a][:, 0:edge], src[RC - 1, :, T2 - edge:T2]).then_inc(x2_in[a], 16)

            load(0, 0)
            load(0, 1)
            with sp.Fori(0, B // 2 - 1) as m:
                for a in range(2):
                    sp.wait_ge(result, (m * 2 + a) * C1 + C1)
                    sp.dma_start(out[m * 2 + a, :, :], xr[a][:, :]).then_inc(out_done[a], 16)
                    sp.wait_ge(out_done[a], m * 16 + 16)
                    load(m + 1, a)
            for a in range(2):
                sp.wait_ge(result, (B - 2 + a) * C1 + C1)
                sp.dma_start(out[B - 2 + a, :, :], xr[a][:, :]).then_inc(out_done[a], 16)
            for a in range(2):
                sp.wait_ge(out_done[a], B // 2 * 16)

        @block.gpsimd
        def _(pool):
            for a in range(2):
                pool.memset(ya[a][:, :], 0.0)
                ins = pool.memset(yb[a][:, :], 0.0)
            ins.then_inc(zeroed, 1)

        @block.tensor
        def _(pe):
            pe.wait_ge(weights_in, 16)
            with pe.Fori(0, B // 2) as m:
                for a in range(2):
                    image = m * 2 + a
                    yav = ya[a][:, :].rearrange("q (r n) -> q r n", r=H)
                    ybv = yb[a][:, :].rearrange("q (r n) -> q r n", r=H)
                    pe.wait_ge(y_in[a], m * (Y_DMAS * 16) + Y_DMAS * 16)
                    for c in range(C1 + 1):
                        if c < C1:
                            rows = slice(c * R1, (c + 1) * R1)
                            for k in range(2):
                                u = 2 * c + k
                                bank = u % slots
                                if u >= slots:
                                    pe.wait_ge(gelu_done, image * (2 * C1) + u - slots + 1)
                                for kw in range(3):
                                    pe.matmul(ps_h[bank][0:half, 0:T1], wa[:, kw, k * half:(k + 1) * half],
                                              yav[:, rows, kw:kw + W], start=kw == 0, stop=False)
                                pe.matmul(ps_h[bank][0:half, 0:T1], w("wb")[:, k * half:(k + 1) * half],
                                          ybv[:, rows, 0:W], start=False, stop=True).then_inc(h_mm, 1)
                        if c >= 1:
                            pe.wait_ge(gelu_done, image * (2 * C1) + 2 * c)
                            if c != 2:
                                pe.wait_ge(result, image * C1 + max(c - 2, 0))
                            for k in range(2):
                                mm = pe.matmul(ps_f[c % 2][0:C, 0:T1], wf2[:, k, :], hid[:, (2 * c - 2 + k) % slots, :],
                                               start=k == 0, stop=k == 1)
                            mm.then_inc(f_mm, 1)

        @block.scalar
        def _(act):
            act.wait_ge(weights_in, 16)
            with act.Fori(0, B // 2) as m:
                for a in range(2):
                    image = m * 2 + a
                    for u in range(2 * C1):
                        act.wait_ge(h_mm, image * (2 * C1) + u + 1)
                        if u >= slots:
                            act.wait_ge(f_mm, image * C1 + (u - slots) // 2 + 1)
                        act.activation(hid[:, u % slots, :], ps_h[u % slots][0:half, 0:T1], ACT.Gelu,
                                       bias=w("t1")[:, u % 2:u % 2 + 1], scale=w("s1")[:, u % 2:u % 2 + 1]).then_inc(gelu_done, 1)

        @block.vector
        def _(dve):
            dve.wait_ge(weights_in, 16)
            with dve.Fori(0, B // 2) as m:
                for a in range(2):
                    image = m * 2 + a
                    dve.wait_ge(x2_in[a], m * (X_DMAS * 16) + X_DMAS * 16)
                    dve.tensor_scalar(xr[a][:, :], xr[a][:, :], w("t2"), None, op0=ALU.add).then_inc(shift_added, 1)
                    dve.wait_ge(shift_added, image + 1)
                    for c in range(C1):
                        dve.wait_ge(f_mm, image * C1 + c + 1)
                        cols = slice(c * T1, (c + 1) * T1)
                        dve.scalar_tensor_tensor(out=xr[a][:, cols], in0=ps_f[(c + 1) % 2][0:C, 0:T1], scalar=w("s2"),
                                                 in1=xr[a][:, cols], op0=ALU.mult, op1=ALU.add).then_inc(result, 1)


def program(nc, x, pack1, pack2, pack3, out):
    scratch = (RC, B // 2, 2 * C, T2)
    x1s = nc.dram_tensor("x1_chunks", scratch, F32, kind="Internal").ap()
    x2s = nc.dram_tensor("x2_chunks", scratch, F32, kind="Internal").ap()
    ys = nc.dram_tensor("y_chunks", (RC, B // 2, 2 * C, TY), F32, kind="Internal").ap()

    def chunks(s):
        return s.rearrange("n p c t -> (n p) c t")

    layer0(nc, x, pack1, x1s)
    attention(nc, chunks(x1s), pack2, chunks(x2s), chunks(ys))
    feed_forward(nc, x2s, ys, pack3, out)


def packed_layer0(W1, b1, W2, b2, mask_token, Wh, bh, Wd, bd, Wu, bu):
    w1 = np.zeros((2, C, PAIRS, GI, D), np.float32)
    wd = np.zeros((2, C, PAIRS, GI, D), np.float32)
    wu = np.zeros((GI, D, PAIRS, 2, C), np.float32)
    w2 = np.zeros((GI, D, GI, D), np.float32)
    mt = np.zeros((GI, D, GI, M), np.float32)
    for i in range(GI):
        p, a = divmod(i, 2)
        w1[a, :, p, i, :] = W1.T
        wd[a, :, p, i, :] = Wd.T
        wu[i, :, p, a, :] = Wu.T
        w2[i, :, i, :] = W2.T
        mt[i, :, i, :] = mask_token.T
    wh = Wh.reshape(D, D, TAPS, D).transpose(1, 3, 2, 0).reshape(2, 128, TAPS * D).transpose(1, 0, 2)
    bht = bh.reshape(D, D, TAPS).transpose(1, 2, 0)
    ci = np.zeros((D // 2, D, 2, D), np.float32)
    for c in range(D):
        ci[c % (D // 2), :, c // (D // 2), c] = 1
    spread = np.tile(np.eye(D, dtype=np.float32), (1, GI))
    return PACK1.filled({
        "w1": w1, "wd": wd, "w2": w2, "mt": mt, "wh": wh, "bh": bht, "wu": wu,
        "b1": np.tile(b1, GI), "b2": np.tile(b2, GI), "bd": np.tile(bd, GI), "bu": np.tile(bu, 2),
        "same_image": np.kron(np.eye(GI), np.ones((M, D))), "same_k": np.kron(np.ones((GI, D // 2)), np.eye(D)),
        "image": np.kron(np.eye(GI), np.ones((D, 1))), "ci": ci, "spread_ci": spread,
    })


def both(v):
    out = np.zeros((PP,) + v.shape[1:], np.float32)
    out[0:C] = v
    out[BO:PP] = v
    return out


def diagonal(v):
    out = np.zeros((PP, PP), np.float32)
    out[0:C, 0:C] = v
    out[BO:PP, BO:PP] = v
    return out


def packed_attention(ln1_g, ln1_b, w_qkv, b_qkv, bias_table, w_proj, b_proj, ln2_g, ln2_b):
    r, c = (v.reshape(-1) for v in np.meshgrid(np.arange(WS), np.arange(WS), indexing="ij"))
    place = (r[:, None] - r[None, :] + WS - 1) * (2 * WS - 1) + (c[:, None] - c[None, :] + WS - 1)
    rel = bias_table[place].transpose(0, 2, 1)
    cut = WS - SHIFT
    row_cut = (r[:, None] < cut) != (r[None, :] < cut)
    col_cut = (c[:, None] < cut) != (c[None, :] < cut)
    none = np.zeros((N, N), bool)
    masked = np.stack([none, col_cut, row_cut, row_cut | col_cut], 1) * np.float32(-100.0)
    wv = np.zeros((PP, 2 * C), np.float32)
    wv[0:C, 0:C] = w_qkv[:, 2 * C:]
    wv[BO:PP, C:] = w_qkv[:, 2 * C:]
    head = np.kron(np.eye(HEADS), np.ones((HD, 1)))
    vhead = np.zeros((2, N, HEADS // 2, C), np.float32)
    vones = np.zeros((2, N, HEADS // 2, HEADS), np.float32)
    for j in range(HEADS // 2):
        for i in range(2):
            vhead[i, :, j, :] = head[:, 2 * j + i]
            vones[i, :, j, 2 * j + i] = 1
    den = np.zeros((OP, PP), np.float32)
    for o in (0, BO):
        den[o + C:o + C + HEADS, o:o + C] = head.T
    den[C, C:BO] = 1
    third = [slice(i * C, (i + 1) * C) for i in range(3)]
    return PACK2.filled({
        "wq": diagonal(w_qkv[:, third[0]]), "wk": diagonal(w_qkv[:, third[1]]), "wv": wv,
        "wvd": diagonal(w_qkv[:, third[2]]), "wp": diagonal(w_proj),
        "g1": both(ln1_g), "be1": both(ln1_b), "bq": both(b_qkv[third[0]]), "bk": both(b_qkv[third[1]]),
        "bv": both(b_qkv[third[2]]), "bp": both(b_proj), "g2": both(ln2_g), "be2": both(ln2_b),
        "rel": np.concatenate([rel, rel]), "masked": np.concatenate([masked, masked]),
        "center": diagonal(np.eye(C) - 1 / C), "mean": diagonal(np.full((C, C), 1 / C)),
        "head": both(head), "eps": np.full(PP, EPS, np.float32), "vhead": vhead, "vones": vones, "den": den,
        "ident": np.eye(2 * N),
    })


def packed_feed_forward(w_ffn1, bn1_scale, bn1_shift, w_ffn2, bn2_scale, bn2_shift):
    rest = 128 - 2 * C
    half = HID // 2
    taps = w_ffn1.transpose(1, 0, 2, 3)
    wa = taps.reshape(3, 3 * C, HID)[:, 0:128].transpose(1, 0, 2)
    wb = taps[:, 2, rest:].reshape(C, HID)
    wf2 = w_ffn2.reshape(2, half, C).transpose(1, 0, 2)
    return PACK3.filled({
        "wa": wa, "wb": wb, "wf2": wf2, "s1": bn1_scale.reshape(2, half).T, "t1": bn1_shift.reshape(2, half).T,
        "s2": bn2_scale, "t2": bn2_shift,
    })


def kernel(x, **weights):
    import concourse.bacc as bacc
    from concourse.bass_utils import run_bass_kernel_spmd

    a = {name: np.asarray(v) for name, v in weights.items()}

    def take(prefix, *names):
        return [a[prefix + name] for name in names]

    arrays = {
        "x": np.ascontiguousarray(np.asarray(x).reshape(B, HW, C).transpose(0, 2, 1)).reshape(B * C, HW),
        "pack1": packed_layer0(*take("L0_conv_", "W1", "b1", "W2", "b2", "mask_token", "Wh", "bh", "Wd", "bd", "Wu", "bu")),
        "pack2": packed_attention(*take("L1_conv_", "ln1_g", "ln1_b", "w_qkv", "b_qkv", "bias_table", "w_proj", "b_proj",
                                        "ln2_g", "ln2_b")),
        "pack3": packed_feed_forward(*take("L1_conv_", "w_ffn1", "bn1_scale", "bn1_shift", "w_ffn2", "bn2_scale",
                                           "bn2_shift")),
    }
    nc = bacc.Bacc("TRN2", target_bir_lowering=False, num_devices=1)
    aps = [nc.dram_tensor(name, v.shape, F32, kind="ExternalInput").ap() for name, v in arrays.items()]
    out = nc.dram_tensor("out", (B, C, HW), F32, kind="ExternalOutput").ap()
    program(nc, *aps, out)
    result = run_bass_kernel_spmd(nc, [arrays], core_ids=[0])
    return np.ascontiguousarray(result.results[0]["out"].transpose(0, 2, 1)).reshape(B, H, W, C)
```

```python
from contextlib import ExitStack

import numpy as np

import concourse.bass as bass
from concourse import mybir

F32 = mybir.dt.float32
F32R = mybir.dt.float32r
ALU = mybir.AluOpType
ACT = mybir.ActivationFunctionType
AX = mybir.AxisListType

B, H, W, C = 32, 56, 56, 48
D, M = 16, 8
WS, SHIFT, HEADS = 7, 3, 6
HD = C // HEADS
HID = 4 * C
N = WS * WS
NWC = W // WS
HW = H * W
SCALE = 0.17677669529663687
EPS = 1e-3
TAPS = 9

GI = 128 // D
PAIRS = GI // 2
GROUPS = B // GI
P1 = 2 * C
R1 = 8
T1 = R1 * W
C1 = H // R1
STORES = 3

BO = 64
PP = BO + C
T2 = WS * W
RC = H // WS
CHUNKS = RC * B // 2
OP = BO + C + HEADS
HN = HEADS * N
DUOS = NWC // 2
YW = W + 2
TY = WS * YW
XP = W + SHIFT


class Pack:

    def __init__(self, shapes):
        self.place, self.width = {}, 0
        for name, (rows, cols) in shapes.items():
            self.place[name] = (rows, self.width, cols)
            self.width += cols

    def at(self, tile, name):
        rows, start, cols = self.place[name]
        return tile[0:rows, start:start + cols]

    def filled(self, arrays):
        out = np.zeros((128, self.width), np.float32)
        for name, (rows, start, cols) in self.place.items():
            out[0:rows, start:start + cols] = arrays[name].reshape(rows, cols)
        return out


PACK1 = Pack({
    "w1": (P1, PAIRS * 128), "wd": (P1, PAIRS * 128), "w2": (128, 128), "mt": (128, GI * M),
    "wh": (128, 2 * TAPS * D), "bh": (D, TAPS * D), "wu": (128, PAIRS * P1),
    "b1": (128, 1), "b2": (128, 1), "bd": (128, 1), "bu": (P1, 1),
    "same_image": (GI * M, 128), "same_k": (128, 128), "image": (128, GI), "ci": (128, 2 * D),
    "spread_ci": (D, 128),
})
PACK2 = Pack({
    "wq": (PP, PP), "wk": (PP, PP), "wv": (PP, 2 * C), "wvd": (PP, PP), "wp": (PP, PP),
    "g1": (PP, 1), "be1": (PP, 1), "bq": (PP, 1), "bk": (PP, 1), "bv": (PP, 1), "bp": (PP, 1),
    "g2": (PP, 1), "be2": (PP, 1), "rel": (2 * N, HN), "masked": (2 * N, 4 * N),
    "center": (PP, PP), "mean": (PP, PP), "head": (PP, HEADS), "eps": (PP, 1),
    "couple": (2 * N, 2), "vones": (2 * N, HEADS // 2 * HEADS), "den": (OP, PP),
    "ident": (2 * N, 2 * N),
})
PACK3 = Pack({
    "wa": (128, 3 * HID), "wb": (PP, HID), "wf2": (HID // 2, 2 * C),
    "s1": (HID // 2, 2), "t1": (HID // 2, 2), "s2": (C, 1), "t2": (C, 1),
})


def layer0(nc, x, pack, x1s):
    ctx = ExitStack()
    with ctx:
        def sb(name, shape):
            return ctx.enter_context(nc.sbuf_tensor(name, shape, F32))

        def sem(name):
            return ctx.enter_context(nc.semaphore(name))

        cw = sb("cw1", [128, PACK1.width])
        xt = [sb(f"xt{k}", [P1, PAIRS, HW]) for k in range(2)]
        hidden = sb("hidden", [128, 2, T1])
        feat = sb("feat", [128, HW])
        mask = sb("mask", [GI * M, HW])
        down = sb("down", [128, H + 2, W + 2])
        conv = sb("conv", [128, 2, T1])
        cwt = sb("cwt", [128, TAPS, GI, D])
        prod = sb("prod", [128, T1])
        part = sb("part", [128, C1])
        mwf = sb("mwf", [128, 1])
        mdiag = sb("mdiag", [128, GI])
        mrep = sb("mrep", [128, 2, GI, D])
        lmax = sb("lmax", [GI * M, 1])
        nmax = sb("nmax", [GI * M, 1])
        lsum = sb("lsum", [GI * M, 1])
        rsum = sb("rsum", [GI * M, 1])
        msel = sb("msel", [GI * M, 128])
        ps = [ctx.enter_context(nc.psum_tensor(f"pa{i}", [128, 512], F32)) for i in range(8)]

        weights_in = sem("l0_weights_in")
        x_in = [sem(f"l0_x_in{k}") for k in range(2)]
        x_out = [sem(f"l0_x_out{k}") for k in range(2)]
        pad_zero = sem("l0_pad_zero")
        w1_done, wd_done, w2_done, mt_done = sem("w1_done"), sem("wd_done"), sem("w2_done"), sem("mt_done")
        relu_done, down_done, feat_done, logit_done = sem("relu_done"), sem("down_done"), sem("feat_done"), sem("logit_done")
        lmax_done, nmax_done, exp_done, rsum_done, msel_done = (
            sem("lmax_done"), sem("nmax_done"), sem("l0_exp_done"), sem("rsum_done"), sem("msel_done"))
        msum_done, part_done, mwf_done, mdiag_done = sem("msum_done"), sem("part_done"), sem("mwf_done"), sem("mdiag_done")
        rep_done, mrep_done, cw_done, cwt_done = sem("rep_done"), sem("mrep_done"), sem("cw_done"), sem("cwt_done")
        conv_done, gelu_done, up_done, x1_done = sem("conv_done"), sem("gelu_done"), sem("up_done"), sem("x1_done")

        def w(name):
            return PACK1.at(cw, name)

        w1 = w("w1").rearrange("c (p m) -> c p m", p=PAIRS)
        wd = w("wd").rearrange("c (p m) -> c p m", p=PAIRS)
        wh = w("wh").rearrange("c (s n) -> c s n", s=2)
        wu = w("wu").rearrange("c (p m) -> c p m", p=PAIRS)
        ci = w("ci").rearrange("c (s n) -> c s n", s=2)

        def cols(c):
            return slice(c * T1, (c + 1) * T1)

        block = ctx.enter_context(nc.Block())

        @block.sync
        def _(sp):
            sp.dma_start(cw[:, :], pack).then_inc(weights_in, 16)

            def load(k, g):
                for p in range(PAIRS):
                    sp.dma_start(xt[k][:, p, :], x[bass.ds((g * PAIRS + p) * P1, P1), :]).then_inc(x_in[k], 16)

            def store(k, g):
                whole = (RC - 1) * T2
                start, wrap = SHIFT * W, SHIFT * W
                for p in range(PAIRS):
                    pair = g * PAIRS + p
                    sp.dma_start(x1s[0:RC - 1, pair, :, :].rearrange("n c t -> c n t"),
                                 xt[k][:, p, start:start + whole].rearrange("c (n t) -> c n t", n=RC - 1)).then_inc(x_out[k], 16)
                    sp.dma_start(x1s[RC - 1, pair, :, 0:T2 - wrap], xt[k][:, p, start + whole:HW]).then_inc(x_out[k], 16)
                    sp.dma_start(x1s[RC - 1, pair, :, T2 - wrap:T2], xt[k][:, p, 0:wrap]).then_inc(x_out[k], 16)

            for k in range(2):
                load(k, k)
            for g in range(GROUPS):
                k = g % 2
                sp.wait_ge(x1_done, (g + 1) * C1 * PAIRS + 1)
                store(k, g)
                if g + 2 < GROUPS:
                    sp.wait_ge(x_out[k], (g // 2 + 1) * PAIRS * STORES * 16)
                    load(k, g + 2)
            for k in range(2):
                sp.wait_ge(x_out[k], GROUPS // 2 * PAIRS * STORES * 16)

        @block.gpsimd
        def _(pool):
            pool.memset(down[:, :, :], 0.0).then_inc(pad_zero, 1)

        @block.tensor
        def _(pe):
            pe.wait_ge(weights_in, 16)
            with pe.Fori(0, GROUPS // 2) as gg:
                for k in range(2):
                    g = gg * 2 + k
                    pe.wait_ge(x_in[k], gg * (PAIRS * 16) + PAIRS * 16)
                    for c in range(C1 + 2):
                        if c < C1:
                            if c >= 2:
                                pe.wait_ge(relu_done, g * C1 + c - 1)
                            for p in range(PAIRS):
                                mm = pe.matmul(ps[c % 2][:, 0:T1], w1[:, p, :], xt[k][:, p, cols(c)],
                                               start=p == 0, stop=p == PAIRS - 1)
                            mm.then_inc(w1_done, 1)
                            if c >= 2:
                                pe.wait_ge(down_done, g * C1 + c - 1)
                            if c == 0:
                                pe.wait_ge(x1_done, g * (C1 * PAIRS) + 1)
                            for p in range(PAIRS):
                                mm = pe.matmul(ps[2 + c % 2][:, 0:T1], wd[:, p, :], xt[k][:, p, cols(c)],
                                               start=p == 0, stop=p == PAIRS - 1)
                            mm.then_inc(wd_done, 1)
                        if 1 <= c <= C1:
                            pe.wait_ge(relu_done, g * C1 + c)
                            if c >= 3:
                                pe.wait_ge(feat_done, g * C1 + c - 2)
                            pe.matmul(ps[4 + (c - 1) % 2][:, 0:T1], w("w2"), hidden[:, (c - 1) % 2, :],
                                      start=True, stop=True).then_inc(w2_done, 1)
                        if c >= 2:
                            pe.wait_ge(feat_done, g * C1 + c - 1)
                            if c >= 4:
                                pe.wait_ge(logit_done, g * C1 + c - 3)
                            pe.matmul(ps[6 + c % 2][0:GI * M, 0:T1], w("mt"), feat[:, cols(c - 2)],
                                      start=True, stop=True).then_inc(mt_done, 1)
                    pe.wait_ge(msel_done, g + 1)
                    for c in range(C1):
                        if c >= 2:
                            pe.wait_ge(part_done, g * C1 + c - 1)
                        pe.matmul(ps[6 + c % 2][:, 0:T1], msel[:, :], mask[:, cols(c)],
                                  start=True, stop=True).then_inc(msum_done, 1)
                    pe.wait_ge(mdiag_done, g + 1)
                    pe.matmul(ps[4][:, 0:GI], w("same_k"), mdiag[:, :], start=True, stop=True).then_inc(rep_done, 1)
                    pe.wait_ge(mrep_done, 2 * g + 2)
                    for s in range(2):
                        pe.matmul(ps[5][:, 0:TAPS * D], mrep[:, s, :, :].rearrange("q i c -> q (i c)"), wh[:, s, :],
                                  start=s == 0, stop=False)
                    pe.matmul(ps[5][:, 0:TAPS * D], w("spread_ci"), w("bh"), start=False, stop=True).then_inc(cw_done, 1)
                    pe.wait_ge(cwt_done, g + 1)
                    for c in range(C1 + 1):
                        if c < C1:
                            if c >= 2:
                                pe.wait_ge(gelu_done, g * C1 + c - 1)
                            for t in range(TAPS):
                                mm = pe.matmul(ps[c % 2][:, 0:T1], cwt[:, t, :, :].rearrange("q i c -> q (i c)"),
                                               down[:, c * R1 + t // 3:c * R1 + t // 3 + R1, t % 3:t % 3 + W],
                                               start=t == 0, stop=t == TAPS - 1)
                            mm.then_inc(conv_done, 1)
                        if c >= 1:
                            pe.wait_ge(gelu_done, g * C1 + c)
                            for p in range(PAIRS):
                                if c >= 2:
                                    pe.wait_ge(x1_done, (g * C1 + c - 2) * PAIRS + p + 2)
                                pe.matmul(ps[2 + p][0:P1, 0:T1], wu[:, p, :], conv[:, (c - 1) % 2, :],
                                          start=True, stop=True).then_inc(up_done, 1)

        @block.scalar
        def _(act):
            act.wait_ge(weights_in, 16)
            act.wait_ge(pad_zero, 1)
            with act.Fori(0, GROUPS // 2) as gg:
                for k in range(2):
                    g = gg * 2 + k
                    for c in range(C1):
                        act.wait_ge(w1_done, g * C1 + c + 1)
                        if c >= 2:
                            act.wait_ge(w2_done, g * C1 + c - 1)
                        act.activation(hidden[:, c % 2, :], ps[c % 2][:, 0:T1], ACT.Relu,
                                       bias=w("b1")).then_inc(relu_done, 1)
                        act.wait_ge(wd_done, g * C1 + c + 1)
                        act.activation(down[:, 1 + c * R1:1 + (c + 1) * R1, 1:1 + W],
                                       ps[2 + c % 2][:, 0:T1].rearrange("q (r n) -> q r n", r=R1),
                                       ACT.Gelu_apprx_sigmoid, bias=w("bd")).then_inc(down_done, 1)
                    act.wait_ge(nmax_done, g + 1)
                    act.activation(mask[:, :], mask[:, :], ACT.Exp, bias=nmax[:, :],
                                   accum_out=lsum[:, :]).then_inc(exp_done, 1)
                    for c in range(C1):
                        act.wait_ge(conv_done, g * C1 + c + 1)
                        if c >= 2:
                            act.wait_ge(up_done, (g * C1 + c - 1) * PAIRS)
                        act.activation(conv[:, c % 2, :], ps[c % 2][:, 0:T1],
                                       ACT.Gelu_apprx_sigmoid).then_inc(gelu_done, 1)

        @block.vector
        def _(dve):
            dve.engine_nop().then_inc(x1_done, 1)
            dve.wait_ge(weights_in, 16)
            with dve.Fori(0, GROUPS // 2) as gg:
                for k in range(2):
                    g = gg * 2 + k
                    for c in range(C1 + 1):
                        if c < C1:
                            dve.wait_ge(w2_done, g * C1 + c + 1)
                            dve.tensor_scalar(feat[:, cols(c)], ps[4 + c % 2][:, 0:T1], w("b2"), None,
                                              op0=ALU.add).then_inc(feat_done, 1)
                        if c >= 1:
                            dve.wait_ge(mt_done, g * C1 + c)
                            dve.tensor_copy(mask[:, cols(c - 1)], ps[6 + (c - 1) % 2][0:GI * M, 0:T1]).then_inc(logit_done, 1)
                    dve.wait_ge(logit_done, g * C1 + C1)
                    dve.tensor_reduce(lmax[:, :], mask[:, :], AX.X, ALU.max).then_inc(lmax_done, 1)
                    dve.wait_ge(lmax_done, g + 1)
                    dve.tensor_scalar(nmax[:, :], lmax[:, :], -1.0, None, op0=ALU.mult).then_inc(nmax_done, 1)
                    dve.wait_ge(exp_done, g + 1)
                    dve.reciprocal(rsum[:, :], lsum[:, :]).then_inc(rsum_done, 1)
                    dve.wait_ge(rsum_done, g + 1)
                    dve.tensor_scalar(msel[:, :], w("same_image"), rsum[:, 0:1], None, op0=ALU.mult).then_inc(msel_done, 1)
                    for c in range(C1):
                        dve.wait_ge(msum_done, g * C1 + c + 1)
                        if c >= 1:
                            dve.wait_ge(part_done, g * C1 + c)
                        dve.tensor_tensor_reduce(out=prod[:, :], in0=ps[6 + c % 2][:, 0:T1], in1=feat[:, cols(c)],
                                                 scale=1.0, scalar=0.0, op0=ALU.mult, op1=ALU.add,
                                                 accum_out=part[:, c:c + 1]).then_inc(part_done, 1)
                    dve.wait_ge(part_done, g * C1 + C1)
                    dve.reduce_sum(mwf[:, :], part[:, :], AX.X).then_inc(mwf_done, 1)
                    dve.wait_ge(mwf_done, g + 1)
                    dve.tensor_scalar(mdiag[:, :], w("image"), mwf[:, 0:1], None, op0=ALU.mult).then_inc(mdiag_done, 1)
                    dve.wait_ge(rep_done, g + 1)
                    for s in range(2):
                        dve.tensor_tensor(mrep[:, s, :, :], ps[4][:, 0:GI].unsqueeze(2).to_broadcast([128, GI, D]),
                                          ci[:, s, :].unsqueeze(1).to_broadcast([128, GI, D]),
                                          ALU.mult).then_inc(mrep_done, 1)
                    dve.wait_ge(cw_done, g + 1)
                    image = w("image")
                    for i in range(GI):
                        ins = dve.tensor_scalar(cwt[:, :, i, :], ps[5][:, 0:TAPS * D].rearrange("q (t c) -> q t c", t=TAPS),
                                                image[:, i:i + 1], None, op0=ALU.mult)
                    ins.then_inc(cwt_done, 1)
                    for c in range(C1):
                        for p in range(PAIRS):
                            dve.wait_ge(up_done, (g * C1 + c) * PAIRS + p + 1)
                            dve.scalar_tensor_tensor(out=xt[k][:, p, cols(c)], in0=ps[2 + p][0:P1, 0:T1],
                                                     scalar=w("bu"), in1=xt[k][:, p, cols(c)],
                                                     op0=ALU.add, op1=ALU.add).then_inc(x1_done, 1)


def attention(nc, x1s, pack, x2s, ys):
    ctx = ExitStack()
    with ctx:
        def sb(name, shape):
            return ctx.enter_context(nc.sbuf_tensor(name, shape, F32))

        def sem(name):
            return ctx.enter_context(nc.semaphore(name))

        cw = sb("cw2", [128, PACK2.width])
        wqs, wks, wvs = sb("wqs", [PP, PP]), sb("wks", [PP, PP]), sb("wvs", [PP, 2 * C])
        bqs, bks, bvs, bps = sb("bqs", [PP, 1]), sb("bks", [PP, 1]), sb("bvs", [PP, 1]), sb("bps", [PP, 1])
        bias = sb("bias", [2 * N, 2, 2, HN])
        xin = [sb(f"xin{a}", [PP, WS, XP]) for a in range(2)]
        xres = [sb(f"xres{a}", [PP, WS, W]) for a in range(2)]
        xc = sb("xc", [PP, T2])
        sq = sb("sq", [PP, T2])
        lnv = sb("lnv", [PP, T2])
        rstd = sb("rstd", [PP, T2])
        h = sb("h", [PP, NWC, 2, N])
        ks = sb("ks", [PP, NWC, N])
        qbd = [sb(f"qbd{a}", [PP, NWC, 2 * N]) for a in range(2)]
        kex = [sb(f"kex{a}", [PP, NWC, HEADS, N]) for a in range(2)]
        vex = [sb(f"vex{a}", [2 * N, NWC, HEADS // 2, 2 * BO]) for a in range(2)]
        s_sb = [sb(f"s{i}", [2 * N, 2, HN]) for i in range(2)]
        mx = [sb(f"mx{i}", [2 * N, 2, HEADS]) for i in range(2)]
        pt = [sb(f"pt{i}", [2 * N, 2 * HN + OP - 2 * N]) for i in range(2)]
        osb = [sb(f"osb{a}", [OP, WS, W]) for a in range(2)]
        lnd = sb("lnd", [PP, T2])
        rden = sb("rden", [PP, T2])
        odiv = sb("odiv", [PP, T2])
        xo = [sb(f"xo{a}", [PP, WS, W]) for a in range(2)]
        xc2, sq2, lnv2, rstd2 = sb("xc2", [PP, T2]), sb("sq2", [PP, T2]), sb("lnv2", [PP, T2]), sb("rstd2", [PP, T2])
        y = [sb(f"y{a}", [PP, WS, YW]) for a in range(2)]

        ps_s = [ctx.enter_context(nc.psum_tensor(f"ps_s{i}", [128, 512], F32)) for i in range(3)]
        ps_t = ctx.enter_context(nc.psum_tensor("ps_t", [128, 2, 512], F32))
        ps_o = ctx.enter_context(nc.psum_tensor("ps_o", [128, 512], F32))
        ps_m = [ctx.enter_context(nc.psum_tensor(f"ps_m{i}", [128, 512], F32)) for i in range(2)]

        weights_in, zeroed, vones_set = sem("at_weights_in"), sem("at_zeroed"), sem("vones_set")
        folded, bias_mm, biases, bp_mm, tables, pad_set = (
            sem("folded"), sem("bias_mm"), sem("biases"), sem("bp_mm"), sem("tables"), sem("pad_set"))
        x_in = [sem(f"at_x_in{a}") for a in range(2)]
        x2_out = [sem(f"x2_out{a}") for a in range(2)]
        y_out = [sem(f"y_out{a}") for a in range(2)]
        wrapped, xres_set = sem("wrapped"), sem("xres_set")
        center_mm, xc_copied, squared, var_mm, ln_done, rstd_done, h_done, h_twice = (
            sem("center_mm"), sem("xc_copied"), sem("squared"), sem("var_mm"), sem("ln_done"), sem("rstd_done"), sem("h_done"),
            sem("h_twice"))
        q_mm, q_set, k_mm, k_set, v_mm, v_set, kex_set = (
            sem("q_mm"), sem("q_set"), sem("k_mm"), sem("k_set"), sem("v_mm"), sem("v_set"), sem("kex_set"))
        o_set, den_mm, lnd_done, rden_set, odiv_set, proj_mm, x2_set = (
            sem("o_set"), sem("den_mm"), sem("lnd_done"), sem("rden_set"), sem("odiv_set"), sem("proj_mm"), sem("x2_set"))
        center2_mm, xc2_copied, squared2, var2_mm, ln2_done, rstd2_done, ymul_done, y_set = (
            sem("center2_mm"), sem("xc2_copied"), sem("squared2"), sem("var2_mm"), sem("ln2_done"), sem("rstd2_done"),
            sem("ymul_done"), sem("y_set"))
        s_mm, s_biased, max_done, shifted, exp_done, t_mm, pt_set, pv_mm = (
            sem("s_mm"), sem("s_biased"), sem("max_done"), sem("shifted"), sem("exp_done"), sem("t_mm"), sem("pt_set"), sem("pv_mm"))

        def w(name):
            return PACK2.at(cw, name)

        pairs = B // 2

        def each_chunk(body):
            split = (RC - 1) * pairs // 2
            last = CHUNKS // 2 - 1
            body(0, 0, 0, 0)
            body(1, 0, 1, 0)
            for low, start, end in ((0, 1, split), (1, split, last)):
                with body.engine.Fori(start, end) as m:
                    body(m * 2, m, 0, low)
                    body(m * 2 + 1, m, 1, low)
            body(CHUNKS - 2, last, 0, 1)
            body(CHUNKS - 1, last, 1, 1)

        def at_edges(n):
            if isinstance(n, int):
                return n >= 2, n >= 1, n + 1 < CHUNKS, n + 2 < CHUNKS
            return True, True, True, True

        def windows(ap):
            return ap.rearrange("c (r w k) -> c w r k", r=WS, w=NWC)

        block = ctx.enter_context(nc.Block())

        @block.sync
        def _(sp):
            sp.dma_start(cw[:, :], pack).then_inc(weights_in, 16)

            def load(n, a):
                for i in range(2):
                    sp.dma_start(xin[a][BO * i:BO * i + C, :, 0:W],
                                 x1s[n, C * i:C * i + C, :].rearrange("c (r n) -> c r n", r=WS)).then_inc(x_in[a], 16)

            def store(n, a):
                sp.wait_ge(x2_set, n + 1)
                sp.wait_ge(y_set, n + 1)
                for i in range(2):
                    sp.dma_start(x2s[n, C * i:C * i + C, :].rearrange("c (r n) -> c r n", r=WS),
                                 xo[a][BO * i:BO * i + C, :, :]).then_inc(x2_out[a], 16)
                    sp.dma_start(ys[n, C * i:C * i + C, :].rearrange("c (r n) -> c r n", r=WS),
                                 y[a][BO * i:BO * i + C, :, :]).then_inc(y_out[a], 16)

            def load_ahead(n, a):
                sp.wait_ge(xres_set, n + 1)
                sp.wait_ge(center_mm, n + 1)
                load(n + 2, a)

            sp.wait_ge(zeroed, 1)
            load(0, 0)
            load(1, 1)
            load_ahead(0, 0)
            load_ahead(1, 1)
            with sp.Fori(1, CHUNKS // 2 - 1) as m:
                for a in range(2):
                    load_ahead(m * 2 + a, a)
                    store(m * 2 + a - 2, a)
            for n in range(CHUNKS - 4, CHUNKS):
                store(n, n % 2)
            for a in range(2):
                sp.wait_ge(x2_out[a], CHUNKS // 2 * 32)
                sp.wait_ge(y_out[a], CHUNKS // 2 * 32)

        @block.gpsimd
        def _(pool):
            for a in range(2):
                pool.memset(qbd[a][:, :, :], 0.0)
                pool.memset(vex[a][:, :, :, :], 0.0)
                pool.memset(y[a][:, :, :], 0.0)
                pool.memset(pt[a][:, 2 * HN:], 0.0)
                ins = pool.memset(xin[a][:, :, :], 0.0)
            ins.then_inc(zeroed, 1)
            pool.wait_ge(zeroed, 1)
            pool.wait_ge(weights_in, 16)
            ones = w("vones").rearrange("q (j h) -> q j h", j=HEADS // 2)
            for a in range(2):
                for win in range(NWC):
                    for o in (C, BO + C):
                        ins = pool.tensor_copy(vex[a][:, win, :, o:o + HEADS], ones)
            ins.then_inc(vones_set, 1)

            def twice(n):
                pool.wait_ge(rstd_done, n + 1)
                if at_edges(n)[1]:
                    pool.wait_ge(v_mm, n * 2)
                pool.tensor_tensor(h[:, :, 1, :].rearrange("c w (r k) -> c w r k", r=WS), windows(xc[:, :]), windows(rstd[:, :]),
                                   ALU.mult).then_inc(h_twice, 1)

            def keys(n, a):
                pool.wait_ge(k_set, n + 1)
                if at_edges(n)[0]:
                    pool.wait_ge(s_mm, n * NWC - NWC)
                for win in range(NWC):
                    pool.tensor_tensor(kex[a][:, win, :, :],
                                       ks[:, win, :].unsqueeze(1).to_broadcast([PP, HEADS, N]),
                                       w("head").unsqueeze(2).to_broadcast([PP, HEADS, N]), ALU.mult).then_inc(kex_set, 1)

            def divide(n, a):
                pool.wait_ge(rden_set, n + 1)
                if at_edges(n)[1]:
                    pool.wait_ge(proj_mm, n)
                pool.tensor_tensor(odiv[:, :], osb[a][0:PP, :, :].rearrange("c r n -> c (r n)"), rden[:, :],
                                   ALU.mult).then_inc(odiv_set, 1)

            def normalize2(n, m, a):
                pool.wait_ge(rstd2_done, n + 1)
                if at_edges(n)[0]:
                    pool.wait_ge(y_out[a], m * 32)
                pool.tensor_tensor(y[a][:, :, 1:1 + W], xc2[:, :].rearrange("c (r n) -> c r n", r=WS),
                                   rstd2[:, :].rearrange("c (r n) -> c r n", r=WS), ALU.mult).then_inc(ymul_done, 1)

            def body(n, m, a, low):
                before2, before, after, after2 = at_edges(n)
                if before2:
                    normalize2(n - 2, m - 1, a)
                if after:
                    twice(n + 1)
                if before:
                    divide(n - 1, 1 - a)
                if after:
                    keys(n + 1, 1 - a)

            twice(0)
            keys(0, 0)
            body.engine = pool
            each_chunk(body)
            last = CHUNKS // 2 - 1
            normalize2(CHUNKS - 2, last, 0)
            divide(CHUNKS - 1, 1)
            normalize2(CHUNKS - 1, last, 1)

        @block.tensor
        def _(pe):
            pe.wait_ge(weights_in, 16)
            for i, name in enumerate(("wq", "wk", "wvd")):
                mm = pe.matmul(ps_m[0][0:PP, i:i + 1], w(name), w("be1"), start=True, stop=True)
            mm.then_inc(bias_mm, 1)
            pe.wait_ge(biases, 3)
            pe.matmul(ps_m[0][0:PP, 3:4], w("wp"), bvs[:, :], start=True, stop=True).then_inc(bp_mm, 1)
            pe.wait_ge(pad_set, 1)
            pe.wait_ge(folded, 3)

            def scores(n, d, a):
                if d == 0:
                    pe.wait_ge(q_set, n * 2 + 2)
                pe.wait_ge(kex_set, n * NWC + 2 * d + 2)
                for win in (2 * d, 2 * d + 1):
                    if win >= 3:
                        pe.wait_ge(s_biased, n * NWC + win - 2)
                    elif at_edges(n)[1]:
                        pe.wait_ge(s_biased, n * NWC + (-1, 0, -2)[win])
                    pe.matmul(ps_s[win % 3][0:2 * N, 0:HN], qbd[a][:, win, :],
                              kex[a][:, win, :, :].rearrange("c h k -> c (h k)"), start=True, stop=True).then_inc(s_mm, 1)

            def transposes(n, d):
                t = n * DUOS + d
                pe.wait_ge(exp_done, t + 1)
                if not isinstance(n, int) or t >= 1:
                    pe.wait_ge(pt_set, t)
                for i in range(2):
                    for j in range(HEADS // 2):
                        part = slice(j * 2 * N, (j + 1) * 2 * N)
                        mm = pe.transpose(ps_t[0:2 * N, i, part], s_sb[d % 2][:, i, part], w("ident"))
                mm.then_inc(t_mm, 1)

            def values(n, d, a):
                t = n * DUOS + d
                pe.wait_ge(pt_set, t + 1)
                if d == 0:
                    pe.wait_ge(v_set, n * 2 + 2)
                if d % 2 == 0 and (not isinstance(n, int) or t >= 2):
                    pe.wait_ge(o_set, n * 2 + d // 2)
                for i in range(2):
                    win = 2 * d + i
                    for j in range(HEADS // 2):
                        start = i * HN + j * 2 * N
                        mm = pe.matmul(ps_o[0:OP, (win % 4) * OP:(win % 4 + 1) * OP], vex[a][:, win, j, 0:OP],
                                       pt[d % 2][:, start:start + OP], start=j == 0, stop=j == HEADS // 2 - 1)
                mm.then_inc(pv_mm, 1)

            def misc(bank, lhs, rhs, signal):
                pe.matmul(ps_m[bank][0:PP, 0:T2], lhs, rhs, start=True, stop=True).then_inc(signal, 1)

            def center(n, a):
                pe.wait_ge(wrapped, n + 1)
                misc(0, w("center"), xin[a][:, :, SHIFT:XP], center_mm)

            def variance(n):
                pe.wait_ge(squared, n + 1)
                misc(0, w("mean"), sq[:, :], var_mm)

            def queries(n):
                pe.wait_ge(h_done, n + 1)
                misc(1, wqs[:, :], h[:, :, 0, :], q_mm)

            def keys(n):
                misc(0, wks[:, :], h[:, :, 0, :], k_mm)

            def value_rows(n, half):
                if half == 0:
                    pe.wait_ge(h_twice, n + 1)
                    pe.wait_ge(q_set, n * 2 + 2)
                else:
                    pe.wait_ge(k_set, n + 1)
                for i in range(4):
                    win = 4 * half + i
                    mm = pe.matmul(ps_m[1 - half][0:2 * N, i * 2 * C:(i + 1) * 2 * C],
                                   h[:, win, :, :].rearrange("c i k -> c (i k)"), wvs[:, :], start=True, stop=True)
                mm.then_inc(v_mm, 1)

            def denominators(n, a):
                pe.wait_ge(o_set, n * 2 + 2)
                misc(0, w("den"), osb[a][:, :, :].rearrange("c r n -> c (r n)"), den_mm)

            def project(n):
                pe.wait_ge(odiv_set, n + 1)
                misc(1, w("wp"), odiv[:, :], proj_mm)

            def center2(n, a):
                pe.wait_ge(x2_set, n + 1)
                misc(1, w("center"), xo[a][:, :, :], center2_mm)

            def variance2(n):
                pe.wait_ge(squared2, n + 1)
                misc(1, w("mean"), sq2[:, :], var2_mm)

            def body(n, m, a, low):
                before2, before, after, _ = at_edges(n)
                scores(n, 0, a)
                if before:
                    values(n - 1, 2, 1 - a)
                pe.wait_ge(v_set, n * 2 + 2)
                if after:
                    center(n + 1, 1 - a)
                if before:
                    transposes(n - 1, 3)
                if before2:
                    center2(n - 2, a)

                scores(n, 1, a)
                if after:
                    variance(n + 1)
                if before:
                    values(n - 1, 3, 1 - a)
                if before2:
                    variance2(n - 2)
                transposes(n, 0)

                scores(n, 2, a)
                if before2:
                    pe.wait_ge(ln2_done, n - 1)
                if after:
                    pe.wait_ge(ln_done, n + 2)
                    queries(n + 1)
                values(n, 0, a)
                if before:
                    denominators(n - 1, 1 - a)
                transposes(n, 1)

                scores(n, 3, a)
                if after:
                    if before:
                        pe.wait_ge(lnd_done, n)
                    keys(n + 1)
                    value_rows(n + 1, 0)
                values(n, 1, a)
                if after:
                    value_rows(n + 1, 1)
                transposes(n, 2)
                if before:
                    if after:
                        pe.wait_ge(v_set, n * 2 + 3)
                    project(n - 1)

            pe.wait_ge(biases, 4)
            center(0, 0)
            variance(0)
            queries(0)
            pe.wait_ge(ln_done, 1)
            keys(0)
            pe.wait_ge(vones_set, 1)
            value_rows(0, 0)
            value_rows(0, 1)
            body.engine = pe
            each_chunk(body)
            n = CHUNKS - 1
            values(n, 2, 1)
            center2(n - 1, 0)
            transposes(n, 3)
            variance2(n - 1)
            values(n, 3, 1)
            pe.wait_ge(lnd_done, n)
            denominators(n, 1)
            pe.wait_ge(ln2_done, n)
            project(n)
            center2(n, 1)
            variance2(n)

        @block.scalar
        def _(act):
            act.preload_act_table_set("natural_log_exp_and_others")

            def wrap(n, m, a):
                act.wait_ge(x_in[a], m * 32 + 32)
                act.activation(xin[a][:, :, W:XP], xin[a][:, :, 0:SHIFT], ACT.Copy).then_inc(wrapped, 1)

            def centered(n):
                act.wait_ge(center_mm, n + 1)
                if at_edges(n)[1]:
                    act.wait_ge(h_done, n)
                    act.wait_ge(h_twice, n)
                act.activation(xc[:, :], ps_m[0][0:PP, 0:T2], ACT.Copy).then_inc(xc_copied, 1)
                act.activation(sq[:, :], ps_m[0][0:PP, 0:T2], ACT.Square).then_inc(squared, 1)

            def rsqrt(n):
                act.wait_ge(var_mm, n + 1)
                act.activation(lnv[:, :], ps_m[0][0:PP, 0:T2], ACT.Ln, bias=w("eps")).then_inc(ln_done, 1)
                act.wait_ge(ln_done, n + 1)
                act.activation(rstd[:, :], lnv[:, :], ACT.Exp, scale=-0.5).then_inc(rstd_done, 1)

            def queries(n, a):
                act.wait_ge(q_mm, n + 1)
                if at_edges(n)[0]:
                    act.wait_ge(s_mm, n * NWC - NWC)
                for i in range(2):
                    rows = slice(BO * i, BO * i + C)
                    act.activation(qbd[a][rows, :, i * N:(i + 1) * N], ps_m[1][rows, 0:T2].rearrange("c (w k) -> c w k", w=NWC),
                                   ACT.Identity, bias=bqs[rows, :]).then_inc(q_set, 1)

            def keys(n):
                act.wait_ge(k_mm, n + 1)
                if at_edges(n)[1]:
                    act.wait_ge(kex_set, n * NWC)
                act.activation(ks[:, :, :], ps_m[0][0:PP, 0:T2].rearrange("c (w k) -> c w k", w=NWC),
                               ACT.Identity, bias=bks[:, :]).then_inc(k_set, 1)

            def outputs(n, half, a):
                act.wait_ge(pv_mm, n * DUOS + 2 * half + 2)
                for i, rows in enumerate((slice(0, BO), slice(BO, OP))):
                    ins = act.activation(
                        osb[a][rows, :, half * 4 * WS:(half + 1) * 4 * WS].rearrange("c r (w k) -> c w r k", w=4),
                        ps_o[rows, 0:4 * OP].rearrange("c (w n) -> c w n", w=4)[:, :, i * N:(i + 1) * N].rearrange(
                            "c w (r k) -> c w r k", r=WS), ACT.Copy)
                ins.then_inc(o_set, 1)

            def reciprocals(n):
                act.wait_ge(den_mm, n + 1)
                act.activation(lnd[:, :], ps_m[0][0:PP, 0:T2], ACT.Ln).then_inc(lnd_done, 1)
                act.wait_ge(lnd_done, n + 1)
                if at_edges(n)[1]:
                    act.wait_ge(odiv_set, n)
                act.activation(rden[:, :], lnd[:, :], ACT.Exp, scale=-1.0).then_inc(rden_set, 1)

            def exps(n, d):
                act.wait_ge(shifted, n * DUOS + d + 1)
                act.activation(s_sb[d % 2][:, :, :], s_sb[d % 2][:, :, :], ACT.Exp).then_inc(exp_done, 1)

            def transposed(n, d):
                t = n * DUOS + d
                act.wait_ge(t_mm, t + 1)
                if not isinstance(n, int) or t >= 2:
                    act.wait_ge(pv_mm, t - 1)
                act.activation(pt[d % 2][:, 0:2 * HN].rearrange("q (w n) -> q w n", w=2), ps_t[0:2 * N, :, 0:HN],
                               ACT.Copy).then_inc(pt_set, 1)

            def centered2(n):
                act.wait_ge(center2_mm, n + 1)
                if at_edges(n)[1]:
                    act.wait_ge(ymul_done, n)
                act.activation(xc2[:, :], ps_m[1][0:PP, 0:T2], ACT.Copy).then_inc(xc2_copied, 1)
                act.activation(sq2[:, :], ps_m[1][0:PP, 0:T2], ACT.Square).then_inc(squared2, 1)

            def ln2(n):
                act.wait_ge(var2_mm, n + 1)
                act.activation(lnv2[:, :], ps_m[1][0:PP, 0:T2], ACT.Ln, bias=w("eps")).then_inc(ln2_done, 1)

            def rsqrt2(n):
                act.wait_ge(ln2_done, n + 1)
                if at_edges(n)[1]:
                    act.wait_ge(ymul_done, n)
                act.activation(rstd2[:, :], lnv2[:, :], ACT.Exp, scale=-0.5).then_inc(rstd2_done, 1)

            def body(n, m, a, low):
                before2, before, after, after2 = at_edges(n)
                if before:
                    transposed(n - 1, 2)
                    exps(n - 1, 3)
                if after:
                    centered(n + 1)
                if before:
                    transposed(n - 1, 3)
                if before2:
                    centered2(n - 2)
                exps(n, 0)
                if after:
                    rsqrt(n + 1)
                if before:
                    outputs(n - 1, 1, 1 - a)
                exps(n, 1)
                if before2:
                    ln2(n - 2)
                transposed(n, 0)
                if before2:
                    rsqrt2(n - 2)
                if after:
                    queries(n + 1, 1 - a)
                if before:
                    reciprocals(n - 1)
                exps(n, 2)
                transposed(n, 1)
                if after:
                    keys(n + 1)
                if after2:
                    wrap(n + 2, m + 1, a)
                outputs(n, 0, a)

            act.wait_ge(weights_in, 16)
            act.wait_ge(zeroed, 1)
            wrap(0, 0, 0)
            wrap(1, 0, 1)
            centered(0)
            rsqrt(0)
            queries(0, 0)
            keys(0)
            body.engine = act
            each_chunk(body)
            n = CHUNKS - 1
            transposed(n, 2)
            exps(n, 3)
            centered2(n - 1)
            transposed(n, 3)
            ln2(n - 1)
            rsqrt2(n - 1)
            outputs(n, 1, 1)
            reciprocals(n)
            centered2(n)
            ln2(n)
            rsqrt2(n)

        @block.vector
        def _(dve):
            dve.wait_ge(weights_in, 16)
            dve.tensor_scalar(wqs[:, :], w("wq"), w("g1"), SCALE, op0=ALU.mult, op1=ALU.mult).then_inc(folded, 1)
            dve.tensor_scalar(wks[:, :], w("wk"), w("g1"), None, op0=ALU.mult).then_inc(folded, 1)
            dve.tensor_scalar(wvs[:, :], w("wv"), w("g1"), None, op0=ALU.mult).then_inc(folded, 1)
            masked = w("masked").rearrange("q (s k) -> q s k", s=4)
            for s in range(4):
                dve.tensor_tensor(bias[:, s // 2, s % 2, :].rearrange("q (h k) -> q h k", h=HEADS),
                                  w("rel").rearrange("q (h k) -> q h k", h=HEADS),
                                  masked[:, s, :].unsqueeze(1).to_broadcast([2 * N, HEADS, N]), ALU.add).then_inc(tables, 1)
            dve.wait_ge(bias_mm, 1)
            dve.tensor_scalar(bqs[:, :], ps_m[0][0:PP, 0:1], w("bq"), SCALE, op0=ALU.add, op1=ALU.mult).then_inc(biases, 1)
            dve.tensor_scalar(bks[:, :], ps_m[0][0:PP, 1:2], w("bk"), None, op0=ALU.add).then_inc(biases, 1)
            dve.tensor_scalar(bvs[:, :], ps_m[0][0:PP, 2:3], w("bv"), None, op0=ALU.add).then_inc(biases, 1)
            dve.wait_ge(bp_mm, 1)
            dve.tensor_scalar(bps[:, :], ps_m[0][0:PP, 3:4], w("bp"), None, op0=ALU.add).then_inc(biases, 1)
            dve.wait_ge(biases, 4)
            dve.wait_ge(tables, 4)
            dve.wait_ge(zeroed, 1)
            dve.engine_nop().then_inc(pad_set, 1)

            def add_tables(n, d, low):
                t = n * DUOS + d
                i = d % 2
                for k in range(2):
                    win = 2 * d + k
                    dve.wait_ge(s_mm, n * NWC + win + 1)
                    if k == 0 and (not isinstance(n, int) or t >= 2):
                        dve.wait_ge(t_mm, t - 1)
                    dve.tensor_tensor(s_sb[i][:, k, :], ps_s[win % 3][0:2 * N, 0:HN],
                                      bias[:, low, int(win == NWC - 1), :], ALU.add).then_inc(s_biased, 1)

            def shift(n, d):
                t = n * DUOS + d
                i = d % 2
                s4 = s_sb[i][:, :, :].rearrange("q w (h k) -> q (w h) k", h=HEADS)
                dve.wait_ge(s_biased, n * NWC + 2 * d + 2)
                mxi = mx[i][:, :, :].rearrange("q w h -> q (w h)")
                dve.tensor_reduce(mxi, s4, AX.X, ALU.max).then_inc(max_done, 1)
                dve.wait_ge(max_done, t + 1)
                dve.tensor_tensor(s4, s4, mxi.unsqueeze(2).to_broadcast([2 * N, 2 * HEADS, N]),
                                  ALU.subtract).then_inc(shifted, 1)

            def normalize(n):
                dve.wait_ge(rstd_done, n + 1)
                if at_edges(n)[1]:
                    dve.wait_ge(v_mm, n * 2)
                dve.tensor_tensor(h[:, :, 0, :].rearrange("c w (r k) -> c w r k", r=WS), windows(xc[:, :]), windows(rstd[:, :]),
                                  ALU.mult).then_inc(h_done, 1)

            def residual(n, m, a):
                dve.wait_ge(proj_mm, n + 1)
                dve.wait_ge(xres_set, n + 1)
                if at_edges(n)[0]:
                    dve.wait_ge(x2_out[a], m * 32)
                rolled = ps_m[1][0:PP, 0:T2].rearrange("c (r n) -> c r n", r=WS)
                cut = W - SHIFT
                dve.tensor_tensor(xo[a][:, :, SHIFT:W], rolled[:, :, 0:cut], xres[a][:, :, 0:cut], ALU.add)
                dve.tensor_tensor(xo[a][:, :, 0:SHIFT], rolled[:, :, cut:W], xres[a][:, :, cut:W], ALU.add).then_inc(x2_set, 1)

            def residual_in(n, a):
                dve.wait_ge(wrapped, n + 1)
                if at_edges(n)[0]:
                    dve.wait_ge(x2_set, n - 1)
                dve.tensor_scalar(xres[a][:, :, :], xin[a][:, :, SHIFT:XP], bps[:, 0:1], None, op0=ALU.add).then_inc(xres_set, 1)

            def value_rows(n, half, a):
                dve.wait_ge(v_mm, n * 2 + half + 1)
                if half == 0 and at_edges(n)[0]:
                    dve.wait_ge(pv_mm, n * DUOS - DUOS)
                rows = ps_m[1 - half][0:2 * N, 0:4 * 2 * C].rearrange("q (w i c) -> q w i c", w=4, i=2)
                to = vex[a][:, half * 4:half * 4 + 4, :, :]
                for head in range(HEADS):
                    own = slice(head * HD, (head + 1) * HD)
                    ins = dve.tensor_scalar(
                        to[:, :, head // 2, 0:2 * BO].rearrange("q w (i c) -> q w i c", i=2)[:, :, :, own],
                        rows[:, :, :, own], w("couple")[:, head % 2:head % 2 + 1], None, op0=ALU.mult)
                ins.then_inc(v_set, 1)

            def y_affine(n, a):
                dve.wait_ge(ymul_done, n + 1)
                dve.tensor_scalar(y[a][:, :, 1:1 + W], y[a][:, :, 1:1 + W], w("g2"), w("be2"),
                                  op0=ALU.mult, op1=ALU.add).then_inc(y_set, 1)

            def body(n, m, a, low):
                before2, before, after, _ = at_edges(n)
                for d in range(2):
                    add_tables(n, d, low)
                    shift(n, d)
                if after:
                    normalize(n + 1)
                add_tables(n, 2, low)
                shift(n, 2)
                if before2:
                    y_affine(n - 2, a)
                add_tables(n, 3, low)
                if after:
                    value_rows(n + 1, 0, 1 - a)
                shift(n, 3)
                if after:
                    value_rows(n + 1, 1, 1 - a)
                if before:
                    residual(n - 1, m - 1 + a, 1 - a)
                if after:
                    residual_in(n + 1, 1 - a)

            normalize(0)
            residual_in(0, 0)
            dve.wait_ge(vones_set, 1)
            value_rows(0, 0, 0)
            value_rows(0, 1, 0)
            body.engine = dve
            each_chunk(body)
            n = CHUNKS - 1
            y_affine(n - 1, 0)
            residual(n, CHUNKS // 2 - 1, 1)
            y_affine(n, 1)


def feed_forward(nc, x2s, ys, pack, out):
    ctx = ExitStack()
    with ctx:
        def sb(name, shape, dtype=F32):
            return ctx.enter_context(nc.sbuf_tensor(name, shape, dtype))

        def sem(name):
            return ctx.enter_context(nc.semaphore(name))

        half = HID // 2
        rest = 128 - 2 * C
        slots = 4
        cw = sb("cw3", [128, PACK3.width])
        wa_hi, wa_lo = sb("wa_hi", [128, 3 * HID], F32R), sb("wa_lo", [128, 3 * HID], F32R)
        wb_hi, wb_lo = sb("wb_hi", [PP, HID], F32R), sb("wb_lo", [PP, HID], F32R)
        wf_hi, wf_lo = sb("wf_hi", [half, 2 * C], F32R), sb("wf_lo", [half, 2 * C], F32R)
        ya = sb("ya", [128, H * YW])
        yb = sb("yb", [PP, H * YW])
        ya_hi = [sb(f"ya_hi{a}", [128, H * YW], F32R) for a in range(2)]
        ya_lo = [sb(f"ya_lo{a}", [128, H * YW], F32R) for a in range(2)]
        yb_sp = [sb(f"yb_sp{a}", [PP, H * YW], F32R) for a in range(2)]
        xr = [sb(f"xr{a}", [C, HW]) for a in range(2)]
        hid = sb("hid", [half, slots, T1])
        hid_hi, hid_lo = sb("hid_hi", [half, slots, T1], F32R), sb("hid_lo", [half, slots, T1], F32R)
        ps_h = [ctx.enter_context(nc.psum_tensor(f"ps_h{i}", [128, 512], F32)) for i in range(slots)]
        ps_f = [ctx.enter_context(nc.psum_tensor(f"ps_f{i}", [128, 512], F32)) for i in range(2)]

        weights_in, zeroed, w_hi_set, w_lo_set = sem("ff_weights_in"), sem("ff_zeroed"), sem("w_hi_set"), sem("w_lo_set")
        y_in = sem("y_in")
        x2_in = [sem(f"x2_in{a}") for a in range(2)]
        out_done = [sem(f"out_done{a}") for a in range(2)]
        ya_hi_set, yb_hi_set, y_lo_set = sem("ya_hi_set"), sem("yb_hi_set"), sem("y_lo_set")
        h_mm, gelu_done, f_mm, shift_added, result = sem("h_mm"), sem("ff_gelu_done"), sem("f_mm"), sem("shift_added"), sem("result")
        hid_hi_set, hid_lo_set = sem("hid_hi_set"), sem("hid_lo_set")
        Y_DMAS, X_DMAS = 27, 3

        def w(name):
            return PACK3.at(cw, name)

        def by_column(tile):
            return tile[:, :].rearrange("q (k m) -> q k m", k=3)

        block = ctx.enter_context(nc.Block())

        @block.sync
        def _(sp):
            sp.dma_start(cw[:, :], pack).then_inc(weights_in, 16)
            sp.wait_ge(zeroed, 2)

            def load_rows(pair, a, tile, first, channels, shift, move):
                count = channels.stop - channels.start
                src = ys[:, pair, a * C + channels.start:a * C + channels.stop, :]
                mid = (RC - 1) * WS
                to = (SHIFT + 1 - shift) * YW - move
                sp.dma_start(tile[first:first + count, to:to + mid * YW].rearrange("c (n t) -> c n t", n=RC - 1),
                             src[0:RC - 1, :, :].rearrange("n c t -> c n t")).then_inc(y_in, 16)
                low = H - SHIFT - mid - (1 if shift == 0 else 0)
                to += mid * YW
                sp.dma_start(tile[first:first + count, to:to + low * YW], src[RC - 1, :, 0:low * YW]).then_inc(y_in, 16)
                skip = 1 if shift == 2 else 0
                start = (H - SHIFT - mid + skip) * YW + move
                size = (SHIFT - skip) * YW - move
                to = (skip + 1 - shift) * YW
                sp.dma_start(tile[first:first + count, to:to + size], src[RC - 1, :, start:start + size]).then_inc(y_in, 16)

            def load_y(pair, a):
                load_rows(pair, a, ya, 0, slice(0, C), 0, 0)
                load_rows(pair, a, ya, C, slice(0, C), 1, 0)
                load_rows(pair, a, ya, 2 * C, slice(0, rest), 2, 0)
                for first in (0, BO):
                    for kw in range(3):
                        load_rows(pair, a, yb, first + kw * (C - rest), slice(rest, C), 2, kw)

            def load_x(pair, a):
                src = x2s[:, pair, a * C:(a + 1) * C, :]
                mid, edge = (RC - 1) * T2, SHIFT * W
                sp.dma_start(xr[a][:, edge:edge + mid].rearrange("c (n t) -> c n t", n=RC - 1),
                             src[0:RC - 1, :, :].rearrange("n c t -> c n t")).then_inc(x2_in[a], 16)
                sp.dma_start(xr[a][:, edge + mid:HW], src[RC - 1, :, 0:T2 - edge]).then_inc(x2_in[a], 16)
                sp.dma_start(xr[a][:, 0:edge], src[RC - 1, :, T2 - edge:T2]).then_inc(x2_in[a], 16)

            load_y(0, 0)
            load_x(0, 0)
            load_x(0, 1)
            sp.wait_ge(y_lo_set, 2)
            load_y(0, 1)
            with sp.Fori(0, B // 2 - 1) as m:
                for a in range(2):
                    image = m * 2 + a
                    sp.wait_ge(y_lo_set, image * 2 + 4)
                    load_y(m + 1, a)
                    sp.wait_ge(result, image * C1 + C1)
                    sp.dma_start(out[image, :, :], xr[a][:, :]).then_inc(out_done[a], 16)
                    sp.wait_ge(out_done[a], m * 16 + 16)
                    load_x(m + 1, a)
            for a in range(2):
                sp.wait_ge(result, (B - 2 + a) * C1 + C1)
                sp.dma_start(out[B - 2 + a, :, :], xr[a][:, :]).then_inc(out_done[a], 16)
            for a in range(2):
                sp.wait_ge(out_done[a], B // 2 * 16)

        @block.gpsimd
        def _(pool):
            for row in (0, H - 1):
                ins = pool.memset(ya[:, row * YW:(row + 1) * YW], 0.0)
            ins.then_inc(zeroed, 1)

            def images(m):
                for U in range(4 * C1):
                    pool.wait_ge(hid_hi_set, m * (4 * C1) + U + 1)
                    pool.tensor_tensor(hid_lo[:, U % slots, :], hid[:, U % slots, :], hid_hi[:, U % slots, :],
                                       ALU.subtract).then_inc(hid_lo_set, 1)

            with pool.Fori(0, B // 2) as m:
                images(m)

        @block.tensor
        def _(pe):
            def convolve(bank, a, c, k):
                rows = slice(c * R1, (c + 1) * R1)
                hidden = slice(k * half, (k + 1) * half)

                def pixels(tile, kw):
                    return tile.rearrange("q (r n) -> q r n", r=H)[:, rows, kw:kw + W]

                for kw in range(3):
                    for i, (weights, image) in enumerate(((wa_hi, ya_hi), (wa_hi, ya_lo), (wa_lo, ya_hi))):
                        pe.matmul(ps_h[bank][0:half, 0:T1], by_column(weights)[:, kw, hidden],
                                  pixels(image[a][:, :], kw), start=kw == 0 and i == 0, stop=False)
                pe.matmul(ps_h[bank][0:half, 0:T1], wb_hi[:, hidden], pixels(yb_sp[a][:, :], 0), start=False, stop=False)
                pe.matmul(ps_h[bank][0:half, 0:T1], wb_lo[:, hidden], pixels(yb_sp[a][:, :], 0),
                          start=False, stop=True).then_inc(h_mm, 1)

            def feed_back(t, T):
                pe.wait_ge(hid_lo_set, 2 * t + 2)
                if not isinstance(t, int) or t >= 2:
                    pe.wait_ge(result, t - 1)
                for k in range(2):
                    slot, m = (2 * T + k) % slots, slice(k * C, (k + 1) * C)
                    for i, (weights, hidden) in enumerate(((wf_hi, hid_hi), (wf_lo, hid_hi), (wf_hi, hid_lo))):
                        mm = pe.matmul(ps_f[T % 2][0:C, 0:T1], weights[:, m], hidden[:, slot, :],
                                       start=k == 0 and i == 0, stop=k == 1 and i == 2)
                mm.then_inc(f_mm, 1)

            def images(m):
                for a in range(2):
                    pe.wait_ge(y_lo_set, m * 4 + a * 2 + 2)
                    for c in range(C1):
                        T = a * C1 + c
                        t = m * (2 * C1) + T
                        for k in range(2):
                            if not isinstance(m, int) or t * 2 + k >= slots:
                                pe.wait_ge(gelu_done, t * 2 + k - slots + 1)
                            convolve((2 * T + k) % slots, a, c, k)
                        if not isinstance(m, int) or t >= 1:
                            feed_back(t - 1, (T - 1) % (2 * C1))

            pe.wait_ge(w_lo_set, 3)
            images(0)
            with pe.Fori(1, B // 2) as m:
                images(m)
            feed_back(B * C1 - 1, 2 * C1 - 1)

        @block.scalar
        def _(act):
            def images(m):
                for U in range(4 * C1):
                    u = m * (4 * C1) + U
                    act.wait_ge(h_mm, u + 1)
                    if not isinstance(m, int) or u >= slots:
                        act.wait_ge(f_mm, m * (2 * C1) + (U - slots) // 2 + 1)
                    act.activation(hid[:, U % slots, :], ps_h[U % slots][0:half, 0:T1], ACT.Gelu,
                                   bias=w("t1")[:, U % 2:U % 2 + 1], scale=w("s1")[:, U % 2:U % 2 + 1]).then_inc(gelu_done, 1)
                    act.wait_ge(gelu_done, u + 1)
                    act.activation(hid_hi[:, U % slots, :], hid[:, U % slots, :], ACT.Copy).then_inc(hid_hi_set, 1)

            act.wait_ge(weights_in, 16)
            images(0)
            with act.Fori(1, B // 2) as m:
                images(m)

        @block.vector
        def _(dve):
            dve.memset(yb[:, (H - 1) * YW - 2:], 0.0)
            dve.memset(yb[BO // 2:BO, 0:(H - 1) * YW - 2], 0.0).then_inc(zeroed, 1)
            dve.wait_ge(weights_in, 16)
            dve.tensor_copy(wa_hi[:, :], w("wa")).then_inc(w_hi_set, 1)
            dve.tensor_copy(wb_hi[:, :], w("wb")).then_inc(w_hi_set, 1)
            dve.tensor_copy(wf_hi[:, :], w("wf2")).then_inc(w_hi_set, 1)
            dve.wait_ge(w_hi_set, 3)
            dve.tensor_tensor(wf_lo[:, :], w("wf2"), wf_hi[:, :], ALU.subtract).then_inc(w_lo_set, 1)
            dve.tensor_tensor(wa_lo[:, :], w("wa"), wa_hi[:, :], ALU.subtract).then_inc(w_lo_set, 1)
            dve.tensor_tensor(wb_lo[:, :], w("wb"), wb_hi[:, :], ALU.subtract).then_inc(w_lo_set, 1)

            def split_hi_a(image, a):
                dve.wait_ge(y_in, image * (Y_DMAS * 16) + Y_DMAS * 16)
                dve.tensor_copy(ya_hi[a][:, :], ya[:, :]).then_inc(ya_hi_set, 1)

            def split_hi_b(image, a):
                dve.tensor_copy(yb_sp[a][:, :], yb[:, :]).then_inc(yb_hi_set, 1)

            def split_lo_a(image, a):
                dve.wait_ge(ya_hi_set, image + 1)
                dve.tensor_tensor(ya_lo[a][:, :], ya[:, :], ya_hi[a][:, :], ALU.subtract).then_inc(y_lo_set, 1)

            def split_lo_b(image, a):
                dve.wait_ge(yb_hi_set, image + 1)
                dve.tensor_tensor(yb_sp[a][BO:PP, :], yb[BO:PP, :], yb_sp[a][BO:PP, :], ALU.subtract).then_inc(y_lo_set, 1)

            steps = (split_hi_a, split_hi_b, split_lo_a, split_lo_b)

            def add_shift(m, a):
                dve.wait_ge(x2_in[a], m * (X_DMAS * 16) + X_DMAS * 16)
                dve.tensor_scalar(xr[a][:, :], xr[a][:, :], w("t2"), None, op0=ALU.add).then_inc(shift_added, 1)

            def image_done(m, a, split_next):
                image = m * 2 + a
                dve.wait_ge(shift_added, image + 1)
                for c in range(C1):
                    dve.wait_ge(f_mm, image * C1 + c + 1)
                    cols = slice(c * T1, (c + 1) * T1)
                    dve.scalar_tensor_tensor(out=xr[a][:, cols], in0=ps_f[(a * C1 + c) % 2][0:C, 0:T1], scalar=w("s2"),
                                             in1=xr[a][:, cols], op0=ALU.mult, op1=ALU.add).then_inc(result, 1)
                    if split_next and 1 <= c <= len(steps):
                        steps[c - 1](image + 1, 1 - a)

            for step in steps:
                step(0, 0)
            with dve.Fori(0, B // 2 - 1) as m:
                for a in range(2):
                    add_shift(m, a)
                    image_done(m, a, True)
            for a in range(2):
                add_shift(B // 2 - 1, a)
                image_done(B // 2 - 1, a, a == 0)


def program(nc, x, pack1, pack2, pack3, out):
    scratch = (RC, B // 2, 2 * C, T2)
    x1s = nc.dram_tensor("x1_chunks", scratch, F32, kind="Internal").ap()
    x2s = nc.dram_tensor("x2_chunks", scratch, F32, kind="Internal").ap()
    ys = nc.dram_tensor("y_chunks", (RC, B // 2, 2 * C, TY), F32, kind="Internal").ap()

    def chunks(s):
        return s.rearrange("n p c t -> (n p) c t")

    layer0(nc, x, pack1, x1s)
    attention(nc, chunks(x1s), pack2, chunks(x2s), chunks(ys))
    feed_forward(nc, x2s, ys, pack3, out)


def packed_layer0(W1, b1, W2, b2, mask_token, Wh, bh, Wd, bd, Wu, bu):
    w1 = np.zeros((2, C, PAIRS, GI, D), np.float32)
    wd = np.zeros((2, C, PAIRS, GI, D), np.float32)
    wu = np.zeros((GI, D, PAIRS, 2, C), np.float32)
    w2 = np.zeros((GI, D, GI, D), np.float32)
    mt = np.zeros((GI, D, GI, M), np.float32)
    for i in range(GI):
        p, a = divmod(i, 2)
        w1[a, :, p, i, :] = W1.T
        wd[a, :, p, i, :] = Wd.T
        wu[i, :, p, a, :] = Wu.T
        w2[i, :, i, :] = W2.T
        mt[i, :, i, :] = mask_token.T
    wh = Wh.reshape(D, D, TAPS, D).transpose(1, 3, 2, 0).reshape(2, 128, TAPS * D).transpose(1, 0, 2)
    bht = bh.reshape(D, D, TAPS).transpose(1, 2, 0)
    ci = np.zeros((D // 2, D, 2, D), np.float32)
    for c in range(D):
        ci[c % (D // 2), :, c // (D // 2), c] = 1
    spread = np.tile(np.eye(D, dtype=np.float32), (1, GI))
    return PACK1.filled({
        "w1": w1, "wd": wd, "w2": w2, "mt": mt, "wh": wh, "bh": bht, "wu": wu,
        "b1": np.tile(b1, GI), "b2": np.tile(b2, GI), "bd": np.tile(bd, GI), "bu": np.tile(bu, 2),
        "same_image": np.kron(np.eye(GI), np.ones((M, D))), "same_k": np.kron(np.ones((GI, D // 2)), np.eye(D)),
        "image": np.kron(np.eye(GI), np.ones((D, 1))), "ci": ci, "spread_ci": spread,
    })


def both(v):
    out = np.zeros((PP,) + v.shape[1:], np.float32)
    out[0:C] = v
    out[BO:PP] = v
    return out


def diagonal(v):
    out = np.zeros((PP, PP), np.float32)
    out[0:C, 0:C] = v
    out[BO:PP, BO:PP] = v
    return out


def packed_attention(ln1_g, ln1_b, w_qkv, b_qkv, bias_table, w_proj, b_proj, ln2_g, ln2_b):
    r, c = (v.reshape(-1) for v in np.meshgrid(np.arange(WS), np.arange(WS), indexing="ij"))
    place = (r[:, None] - r[None, :] + WS - 1) * (2 * WS - 1) + (c[:, None] - c[None, :] + WS - 1)
    rel = bias_table[place].transpose(0, 2, 1)
    cut = WS - SHIFT
    row_cut = (r[:, None] < cut) != (r[None, :] < cut)
    col_cut = (c[:, None] < cut) != (c[None, :] < cut)
    none = np.zeros((N, N), bool)
    masked = np.stack([none, col_cut, row_cut, row_cut | col_cut], 1) * np.float32(-100.0)
    wv = np.zeros((PP, 2 * C), np.float32)
    wv[0:C, 0:C] = w_qkv[:, 2 * C:]
    wv[BO:PP, C:] = w_qkv[:, 2 * C:]
    head = np.kron(np.eye(HEADS), np.ones((HD, 1)))
    vones = np.zeros((2, N, HEADS // 2, HEADS), np.float32)
    for j in range(HEADS // 2):
        for i in range(2):
            vones[i, :, j, 2 * j + i] = 1
    den = np.zeros((OP, PP), np.float32)
    for o in (0, BO):
        den[o + C:o + C + HEADS, o:o + C] = head.T
    den[C, C:BO] = 1
    third = [slice(i * C, (i + 1) * C) for i in range(3)]
    return PACK2.filled({
        "wq": diagonal(w_qkv[:, third[0]]), "wk": diagonal(w_qkv[:, third[1]]), "wv": wv,
        "wvd": diagonal(w_qkv[:, third[2]]), "wp": diagonal(w_proj),
        "g1": both(ln1_g), "be1": both(ln1_b), "bq": both(b_qkv[third[0]]), "bk": both(b_qkv[third[1]]),
        "bv": both(b_qkv[third[2]]), "bp": both(b_proj), "g2": both(ln2_g), "be2": both(ln2_b),
        "rel": np.concatenate([rel, rel]), "masked": np.concatenate([masked, masked]),
        "center": diagonal(np.eye(C) - 1 / C), "mean": diagonal(np.full((C, C), 1 / C)),
        "head": both(head), "eps": np.full(PP, EPS, np.float32), "couple": np.kron(np.eye(2), np.ones((N, 1))), "vones": vones, "den": den,
        "ident": np.eye(2 * N),
    })


def packed_feed_forward(w_ffn1, bn1_scale, bn1_shift, w_ffn2, bn2_scale, bn2_shift):
    rest = 128 - 2 * C
    half = HID // 2
    taps = w_ffn1.transpose(1, 0, 2, 3)
    wa = taps.reshape(3, 3 * C, HID)[:, 0:128].transpose(1, 0, 2)
    wb = both(taps[:, 2, rest:].reshape(C, HID))
    wf2 = w_ffn2.reshape(2, half, C).transpose(1, 0, 2)
    return PACK3.filled({
        "wa": wa, "wb": wb, "wf2": wf2, "s1": bn1_scale.reshape(2, half).T, "t1": bn1_shift.reshape(2, half).T,
        "s2": bn2_scale, "t2": bn2_shift,
    })


def kernel(x, **weights):
    import concourse.bacc as bacc
    from concourse.bass_utils import run_bass_kernel_spmd

    a = {name: np.asarray(v) for name, v in weights.items()}

    def take(prefix, *names):
        return [a[prefix + name] for name in names]

    arrays = {
        "x": np.ascontiguousarray(np.asarray(x).reshape(B, HW, C).transpose(0, 2, 1)).reshape(B * C, HW),
        "pack1": packed_layer0(*take("L0_conv_", "W1", "b1", "W2", "b2", "mask_token", "Wh", "bh", "Wd", "bd", "Wu", "bu")),
        "pack2": packed_attention(*take("L1_conv_", "ln1_g", "ln1_b", "w_qkv", "b_qkv", "bias_table", "w_proj", "b_proj",
                                        "ln2_g", "ln2_b")),
        "pack3": packed_feed_forward(*take("L1_conv_", "w_ffn1", "bn1_scale", "bn1_shift", "w_ffn2", "bn2_scale",
                                           "bn2_shift")),
    }
    nc = bacc.Bacc("TRN2", target_bir_lowering=False, num_devices=1)
    aps = [nc.dram_tensor(name, v.shape, F32, kind="ExternalInput").ap() for name, v in arrays.items()]
    out = nc.dram_tensor("out", (B, C, HW), F32, kind="ExternalOutput").ap()
    program(nc, *aps, out)
    result = run_bass_kernel_spmd(nc, [arrays], core_ids=[0])
    return np.ascontiguousarray(result.results[0]["out"].transpose(0, 2, 1)).reshape(B, H, W, C)
```

```python
from contextlib import ExitStack

import numpy as np

import concourse.bass as bass
from concourse import mybir

F32 = mybir.dt.float32
F32R = mybir.dt.float32r
ALU = mybir.AluOpType
ACT = mybir.ActivationFunctionType
AX = mybir.AxisListType

B, H, W, C = 32, 56, 56, 48
D, M = 16, 8
WS, SHIFT, HEADS = 7, 3, 6
HD = C // HEADS
HID = 4 * C
N = WS * WS
NWC = W // WS
HW = H * W
SCALE = 0.17677669529663687
EPS = 1e-3
TAPS = 9

GI = 128 // D
PAIRS = GI // 2
GROUPS = B // GI
P1 = 2 * C
R1 = 8
T1 = R1 * W
C1 = H // R1
FIRST = 2
STORES = 5

BO = 64
PP = BO + C
T2 = WS * W
RC = H // WS
CHUNKS = RC * B // 2
OP = BO + C + HEADS
HN = HEADS * N
DUOS = NWC // 2
YW = W + 2
TY = WS * YW
XP = W + SHIFT


class Pack:

    def __init__(self, shapes):
        self.place, self.width = {}, 0
        for name, (rows, cols) in shapes.items():
            self.place[name] = (rows, self.width, cols)
            self.width += cols

    def at(self, tile, name):
        rows, start, cols = self.place[name]
        return tile[0:rows, start:start + cols]

    def filled(self, arrays):
        out = np.zeros((128, self.width), np.float32)
        for name, (rows, start, cols) in self.place.items():
            out[0:rows, start:start + cols] = arrays[name].reshape(rows, cols)
        return out


PACK1 = Pack({
    "w1d": (P1, 4 * D), "w2": (128, 128), "mt": (128, GI * M),
    "wh": (128, 2 * TAPS * D), "bh": (D, TAPS * D), "wu": (128, PAIRS * P1),
    "b1": (128, 1), "b2": (128, 1), "bd": (128, 1), "bu": (P1, 1),
    "same_image": (GI * M, 128), "same_k": (128, 128), "image": (128, GI), "ci": (128, 2 * D),
    "spread_ci": (D, 128),
})
PACK2 = Pack({
    "wq": (PP, PP), "wk": (PP, PP), "wv": (PP, 2 * C), "wvd": (PP, PP), "wp": (PP, PP),
    "g1": (PP, 1), "be1": (PP, 1), "bq": (PP, 1), "bk": (PP, 1), "bv": (PP, 1), "bp": (PP, 1),
    "g2": (PP, 1), "be2": (PP, 1), "rel": (2 * N, HN), "masked": (2 * N, 4 * N),
    "center": (PP, PP), "sum": (PP, PP), "head": (PP, HEADS), "eps": (PP, 1),
    "couple": (2 * N, 2), "vones": (2 * N, HEADS // 2 * HEADS), "den": (OP, PP),
    "ident": (2 * N, 2 * N),
})
PACK3 = Pack({
    "wa": (128, 3 * HID), "wb": (PP, HID), "wf2": (HID // 2, 2 * C),
    "s1": (HID // 2, 2), "t1": (HID // 2, 2), "s2": (C, 1), "t2": (C, 1),
})


def layer0(nc, x, pack, x1s):
    ctx = ExitStack()
    with ctx:
        def sb(name, shape, dtype=F32):
            return ctx.enter_context(nc.sbuf_tensor(name, shape, dtype))

        def sem(name):
            return ctx.enter_context(nc.semaphore(name))

        cw = sb("cw1", [128, PACK1.width])
        xt = [sb(f"xt{k}", [P1, PAIRS, HW]) for k in range(2)]
        hidden = sb("hidden", [128, 2, T1])
        feat = sb("feat", [128, HW])
        mask = sb("mask", [GI * M, HW])
        mid = sb("mid", [128, 2, T1])
        down_hi = sb("down_hi", [128, H + 2, W + 2], F32R)
        down_lo = sb("down_lo", [128, H + 2, W + 2], F32R)
        conv_hi, conv_lo = sb("conv_hi", [128, 2, T1], F32R), sb("conv_lo", [128, 2, T1], F32R)
        cw_hi, cw_lo = sb("cw_hi", [128, TAPS, D], F32R), sb("cw_lo", [128, TAPS, D], F32R)
        cwt_hi = sb("cwt_hi", [128, TAPS, GI, D], F32R)
        cwt_lo = sb("cwt_lo", [128, TAPS, GI, D], F32R)
        wu_hi, wu_lo = sb("wu_hi", [128, PAIRS * P1], F32R), sb("wu_lo", [128, PAIRS * P1], F32R)
        part = sb("part", [128, C1])
        mwf = sb("mwf", [128, 1])
        mdiag = sb("mdiag", [128, GI])
        mrep = sb("mrep", [128, 2, GI, D])
        lmax_by_chunk = sb("lmax_by_chunk", [GI * M, C1])
        lmax = sb("lmax", [GI * M, 1])
        nmax = sb("nmax", [GI * M, 1])
        lsum = sb("lsum", [GI * M, 1])
        rsum = sb("rsum", [GI * M, 1])
        msel = sb("msel", [GI * M, 128])
        ps = [ctx.enter_context(nc.psum_tensor(f"pa{i}", [128, 512], F32)) for i in range(8)]

        weights_in = sem("l0_weights_in")
        x_in = [sem(f"l0_x_in{k}") for k in range(2)]
        x_rest_in = [sem(f"l0_x_rest_in{k}") for k in range(2)]
        x_out = [sem(f"l0_x_out{k}") for k in range(2)]
        pad_zero = sem("l0_pad_zero")
        in_mm, w2_done, mt_done = sem("in_mm"), sem("w2_done"), sem("mt_done")
        wu_hi_set, wu_set, down_hi_set, down_split = sem("wu_hi_set"), sem("wu_set"), sem("down_hi_set"), sem("down_split")
        conv_hi_set, conv_split = sem("conv_hi_set"), sem("conv_split")
        relu_done, down_done, feat_done, logit_done = sem("relu_done"), sem("down_done"), sem("feat_done"), sem("logit_done")
        lmax_done, nmax_done, exp_done, rsum_done, msel_done = (
            sem("lmax_done"), sem("nmax_done"), sem("l0_exp_done"), sem("rsum_done"), sem("msel_done"))
        msum_done, part_done, mwf_done, mdiag_done = sem("msum_done"), sem("part_done"), sem("mwf_done"), sem("mdiag_done")
        rep_done, mrep_done, cw_done = sem("rep_done"), sem("mrep_done"), sem("cw_done")
        cw_hi_set, cw_lo_set, cwt_hi_set, cwt_set = sem("cw_hi_set"), sem("cw_lo_set"), sem("cwt_hi_set"), sem("cwt_set")
        conv_done, gelu_done, up_done, x1_done = sem("conv_done"), sem("gelu_done"), sem("up_done"), sem("x1_done")

        def w(name):
            return PACK1.at(cw, name)

        wh = w("wh").rearrange("c (s n) -> c s n", s=2)
        ci = w("ci").rearrange("c (s n) -> c s n", s=2)

        def cols(c):
            return slice(c * T1, (c + 1) * T1)

        block = ctx.enter_context(nc.Block())

        @block.sync
        def _(sp):
            sp.dma_start(cw[:, :], pack).then_inc(weights_in, 16)

            def load(k, g):
                for part, signal in ((slice(0, FIRST * T1), x_in[k]), (slice(FIRST * T1, HW), x_rest_in[k])):
                    for p in range(PAIRS):
                        sp.dma_start(xt[k][:, p, part], x[bass.ds((g * PAIRS + p) * P1, P1), part]).then_inc(signal, 16)

            def store(k, g):
                wrap = SHIFT * W
                for start, end, chunks in ((0, 3, 3), (3, 5, 5), (5, RC - 1, C1)):
                    sp.wait_ge(x1_done, (g * C1 + chunks) * PAIRS + 1)
                    for p in range(PAIRS):
                        pair = g * PAIRS + p
                        sp.dma_start(x1s[start:end, pair, :, :].rearrange("n c t -> c n t"),
                                     xt[k][:, p, wrap + start * T2:wrap + end * T2].rearrange(
                                         "c (n t) -> c n t", n=end - start)).then_inc(x_out[k], 16)
                        if start == 0:
                            sp.dma_start(x1s[RC - 1, pair, :, T2 - wrap:T2], xt[k][:, p, 0:wrap]).then_inc(x_out[k], 16)
                        if end == RC - 1:
                            sp.dma_start(x1s[RC - 1, pair, :, 0:T2 - wrap], xt[k][:, p, wrap + end * T2:HW]).then_inc(x_out[k], 16)

            for k in range(2):
                load(k, k)
            for g in range(GROUPS):
                k = g % 2
                store(k, g)
                if g + 2 < GROUPS:
                    sp.wait_ge(x_out[k], (g // 2 + 1) * PAIRS * STORES * 16)
                    load(k, g + 2)
            for k in range(2):
                sp.wait_ge(x_out[k], GROUPS // 2 * PAIRS * STORES * 16)

        @block.gpsimd
        def _(pool):
            pool.memset(down_hi[:, :, :].bitcast(F32), 0.0)
            pool.memset(down_lo[:, :, :].bitcast(F32), 0.0).then_inc(pad_zero, 1)
            pool.wait_ge(pad_zero, 1)
            with pool.Fori(0, GROUPS) as g:
                for c in range(C1):
                    inner = (slice(None), slice(1 + c * R1, 1 + (c + 1) * R1), slice(1, 1 + W))
                    pool.wait_ge(down_hi_set, g * C1 + c + 1)
                    pool.tensor_tensor(down_lo[inner], mid[:, c % 2, :].rearrange("q (r n) -> q r n", r=R1), down_hi[inner],
                                       ALU.subtract).then_inc(down_split, 1)
                for c in range(C1):
                    pool.wait_ge(conv_hi_set, g * C1 + c + 1)
                    pool.tensor_tensor(conv_lo[:, c % 2, :], mid[:, c % 2, :], conv_hi[:, c % 2, :],
                                       ALU.subtract).then_inc(conv_split, 1)

        @block.tensor
        def _(pe):
            pe.wait_ge(weights_in, 16)
            pe.wait_ge(wu_set, 1)
            with pe.Fori(0, GROUPS // 2) as gg:
                for k in range(2):
                    g = gg * 2 + k
                    pe.wait_ge(x_in[k], gg * (PAIRS * 16) + PAIRS * 16)
                    for c in range(C1 + 2):
                        if c == FIRST:
                            pe.wait_ge(x_rest_in[k], gg * (PAIRS * 16) + PAIRS * 16)
                        if c < C1:
                            if c == 1:
                                pe.wait_ge(x1_done, g * (C1 * PAIRS) + 1)
                            for p in range(PAIRS):
                                if c >= 2 and p % 2 == 0:
                                    pe.wait_ge(relu_done, (g * C1 + c - 2) * 2 + p // 2 + 1)
                                mm = pe.matmul(ps[2 * (c % 2) + p // 2][64 * (p % 2):64 * (p % 2) + 64, 0:T1],
                                               w("w1d"), xt[k][:, p, cols(c)], start=True, stop=True)
                                if p % 2 == 1:
                                    mm.then_inc(in_mm, 1)
                        if 1 <= c <= C1:
                            pe.wait_ge(relu_done, (g * C1 + c) * 2)
                            if c >= 3:
                                pe.wait_ge(feat_done, g * C1 + c - 2)
                            pe.matmul(ps[4 + (c - 1) % 2][:, 0:T1], w("w2"), hidden[:, (c - 1) % 2, :],
                                      start=True, stop=True).then_inc(w2_done, 1)
                        if c >= 2:
                            pe.wait_ge(feat_done, g * C1 + c - 1)
                            if c >= 4:
                                pe.wait_ge(logit_done, g * C1 + c - 3)
                            pe.matmul(ps[6 + c % 2][0:GI * M, 0:T1], w("mt"), feat[:, cols(c - 2)],
                                      start=True, stop=True).then_inc(mt_done, 1)
                    pe.wait_ge(msel_done, g + 1)
                    for c in range(C1):
                        if c >= 2:
                            pe.wait_ge(part_done, g * C1 + c - 1)
                        pe.matmul(ps[6 + c % 2][:, 0:T1], msel[:, :], mask[:, cols(c)],
                                  start=True, stop=True).then_inc(msum_done, 1)
                    pe.wait_ge(mdiag_done, g + 1)
                    pe.matmul(ps[4][:, 0:GI], w("same_k"), mdiag[:, :], start=True, stop=True).then_inc(rep_done, 1)
                    pe.wait_ge(mrep_done, 2 * g + 2)
                    for s in range(2):
                        pe.matmul(ps[5][:, 0:TAPS * D], mrep[:, s, :, :].rearrange("q i c -> q (i c)"), wh[:, s, :],
                                  start=s == 0, stop=False)
                    pe.matmul(ps[5][:, 0:TAPS * D], w("spread_ci"), w("bh"), start=False, stop=True).then_inc(cw_done, 1)
                    pe.wait_ge(cwt_hi_set, g + 1)
                    pe.wait_ge(down_split, g * C1 + C1)
                    for c in range(C1 + 1):
                        if c < C1:
                            if c >= 2:
                                pe.wait_ge(gelu_done, g * C1 + c - 1)
                            for i, (weights, image) in enumerate(((cwt_hi, down_hi), (cwt_hi, down_lo), (cwt_lo, down_hi))):
                                if c == 0 and i == 2:
                                    pe.wait_ge(cwt_set, g + 1)
                                for t in range(TAPS):
                                    mm = pe.matmul(ps[c % 2][:, 0:T1], weights[:, t, :, :].rearrange("q i c -> q (i c)"),
                                                   image[:, c * R1 + t // 3:c * R1 + t // 3 + R1, t % 3:t % 3 + W],
                                                   start=i == 0 and t == 0, stop=i == 2 and t == TAPS - 1)
                            mm.then_inc(conv_done, 1)
                        if c >= 1:
                            pe.wait_ge(conv_split, g * C1 + c)
                            for p in range(PAIRS):
                                if c >= 2:
                                    pe.wait_ge(x1_done, (g * C1 + c - 2) * PAIRS + p + 2)
                                rows = slice(p * P1, (p + 1) * P1)
                                for i, (weights, image) in enumerate(((wu_hi, conv_hi), (wu_lo, conv_hi), (wu_hi, conv_lo))):
                                    mm = pe.matmul(ps[2 + p][0:P1, 0:T1], weights[:, rows], image[:, (c - 1) % 2, :],
                                                   start=i == 0, stop=i == 2)
                                mm.then_inc(up_done, 1)

        @block.scalar
        def _(act):
            act.wait_ge(weights_in, 16)
            act.wait_ge(pad_zero, 1)
            with act.Fori(0, GROUPS // 2) as gg:
                for k in range(2):
                    g = gg * 2 + k
                    for c in range(C1 + 1):
                        if c < C1:
                            if c >= 2:
                                act.wait_ge(down_split, g * C1 + c - 1)
                            for q in range(2):
                                act.wait_ge(in_mm, (g * C1 + c) * 2 + q + 1)
                                for i in range(2):
                                    rows = slice(64 * q + 32 * i, 64 * q + 32 * i + 32)
                                    ins = act.activation(mid[rows, c % 2, :], ps[2 * (c % 2) + q][64 * i + 32:64 * i + 64, 0:T1],
                                                         ACT.Gelu_apprx_sigmoid, bias=w("bd")[rows, :])
                                ins.then_inc(down_done, 1)
                            act.wait_ge(down_done, (g * C1 + c) * 2 + 2)
                            act.activation(down_hi[:, 1 + c * R1:1 + (c + 1) * R1, 1:1 + W],
                                           mid[:, c % 2, :].rearrange("q (r n) -> q r n", r=R1), ACT.Copy).then_inc(down_hi_set, 1)
                        if c >= 1:
                            act.wait_ge(w2_done, g * C1 + c)
                            act.activation(feat[:, cols(c - 1)], ps[4 + (c - 1) % 2][:, 0:T1], ACT.Identity,
                                           bias=w("b2")).then_inc(feat_done, 1)
                    act.wait_ge(nmax_done, g + 1)
                    act.activation(mask[:, :], mask[:, :], ACT.Exp, bias=nmax[:, :],
                                   accum_out=lsum[:, :]).then_inc(exp_done, 1)
                    for c in range(C1):
                        act.wait_ge(conv_done, g * C1 + c + 1)
                        if c >= 2:
                            act.wait_ge(up_done, (g * C1 + c - 1) * PAIRS)
                        act.activation(mid[:, c % 2, :], ps[c % 2][:, 0:T1], ACT.Gelu_apprx_sigmoid).then_inc(gelu_done, 1)
                        act.wait_ge(gelu_done, g * C1 + c + 1)
                        act.activation(conv_hi[:, c % 2, :], mid[:, c % 2, :], ACT.Copy).then_inc(conv_hi_set, 1)

        @block.vector
        def _(dve):
            dve.engine_nop().then_inc(x1_done, 1)
            dve.wait_ge(weights_in, 16)
            dve.tensor_copy(wu_hi[:, :], w("wu")).then_inc(wu_hi_set, 1)
            dve.wait_ge(wu_hi_set, 1)
            dve.tensor_tensor(wu_lo[:, :], w("wu"), wu_hi[:, :], ALU.subtract).then_inc(wu_set, 1)
            with dve.Fori(0, GROUPS // 2) as gg:
                for k in range(2):
                    g = gg * 2 + k
                    for c in range(C1 + 2):
                        if c < C1:
                            if c >= 2:
                                dve.wait_ge(w2_done, g * C1 + c - 1)
                            for q in range(2):
                                dve.wait_ge(down_done, (g * C1 + c) * 2 + q + 1)
                                for i in range(2):
                                    rows = slice(64 * q + 32 * i, 64 * q + 32 * i + 32)
                                    ins = dve.tensor_scalar(hidden[rows, c % 2, :], ps[2 * (c % 2) + q][64 * i:64 * i + 32, 0:T1],
                                                            w("b1")[rows, :], 0.0, op0=ALU.add, op1=ALU.max)
                                ins.then_inc(relu_done, 1)
                        if c >= 2:
                            dve.wait_ge(mt_done, g * C1 + c - 1)
                            logits = ps[6 + c % 2][0:GI * M, 0:T1]
                            dve.tensor_reduce(lmax_by_chunk[:, c - 2:c - 1], logits, AX.X, ALU.max)
                            dve.tensor_copy(mask[:, cols(c - 2)], logits).then_inc(logit_done, 1)
                    dve.wait_ge(logit_done, g * C1 + C1)
                    dve.tensor_reduce(lmax[:, :], lmax_by_chunk[:, :], AX.X, ALU.max).then_inc(lmax_done, 1)
                    dve.wait_ge(lmax_done, g + 1)
                    dve.tensor_scalar(nmax[:, :], lmax[:, :], -1.0, None, op0=ALU.mult).then_inc(nmax_done, 1)
                    dve.wait_ge(exp_done, g + 1)
                    dve.reciprocal(rsum[:, :], lsum[:, :]).then_inc(rsum_done, 1)
                    dve.wait_ge(rsum_done, g + 1)
                    dve.tensor_scalar(msel[:, :], w("same_image"), rsum[:, 0:1], None, op0=ALU.mult).then_inc(msel_done, 1)
                    for c in range(C1):
                        dve.wait_ge(msum_done, g * C1 + c + 1)
                        if c >= 2:
                            dve.wait_ge(part_done, g * C1 + c - 1)
                        dve.tensor_tensor_reduce(out=hidden[:, c % 2, :], in0=ps[6 + c % 2][:, 0:T1], in1=feat[:, cols(c)],
                                                 scale=1.0, scalar=0.0, op0=ALU.mult, op1=ALU.add,
                                                 accum_out=part[:, c:c + 1]).then_inc(part_done, 1)
                    dve.wait_ge(part_done, g * C1 + C1)
                    dve.reduce_sum(mwf[:, :], part[:, :], AX.X).then_inc(mwf_done, 1)
                    dve.wait_ge(mwf_done, g + 1)
                    dve.tensor_scalar(mdiag[:, :], w("image"), mwf[:, 0:1], None, op0=ALU.mult).then_inc(mdiag_done, 1)
                    dve.wait_ge(rep_done, g + 1)
                    for s in range(2):
                        dve.tensor_tensor(mrep[:, s, :, :], ps[4][:, 0:GI].unsqueeze(2).to_broadcast([128, GI, D]),
                                          ci[:, s, :].unsqueeze(1).to_broadcast([128, GI, D]),
                                          ALU.mult).then_inc(mrep_done, 1)
                    dve.wait_ge(cw_done, g + 1)
                    conv_weights = ps[5][:, 0:TAPS * D].rearrange("q (t c) -> q t c", t=TAPS)
                    dve.tensor_copy(cw_hi[:, :, :], conv_weights).then_inc(cw_hi_set, 1)
                    dve.wait_ge(cw_hi_set, g + 1)
                    dve.tensor_tensor(cw_lo[:, :, :], conv_weights, cw_hi[:, :, :], ALU.subtract).then_inc(cw_lo_set, 1)
                    image = w("image")
                    for i in range(GI):
                        ins = dve.tensor_scalar(cwt_hi[:, :, i, :], cw_hi[:, :, :], image[:, i:i + 1], None, op0=ALU.mult)
                    ins.then_inc(cwt_hi_set, 1)
                    dve.wait_ge(cw_lo_set, g + 1)
                    for i in range(GI):
                        ins = dve.tensor_scalar(cwt_lo[:, :, i, :], cw_lo[:, :, :], image[:, i:i + 1], None, op0=ALU.mult)
                    ins.then_inc(cwt_set, 1)
                    for c in range(C1):
                        for p in range(PAIRS):
                            dve.wait_ge(up_done, (g * C1 + c) * PAIRS + p + 1)
                            dve.scalar_tensor_tensor(out=xt[k][:, p, cols(c)], in0=ps[2 + p][0:P1, 0:T1],
                                                     scalar=w("bu"), in1=xt[k][:, p, cols(c)],
                                                     op0=ALU.add, op1=ALU.add).then_inc(x1_done, 1)


def attention(nc, x1s, pack, x2s, ys):
    ctx = ExitStack()
    with ctx:
        def sb(name, shape, dtype=F32):
            return ctx.enter_context(nc.sbuf_tensor(name, shape, dtype))

        def sem(name):
            return ctx.enter_context(nc.semaphore(name))

        cw = sb("cw2", [128, PACK2.width])
        wqs, wks, wvs = sb("wqs", [PP, PP]), sb("wks", [PP, PP]), sb("wvs", [PP, 2 * C])
        bqs, bks, bvs, bps = sb("bqs", [PP, 1]), sb("bks", [PP, 1]), sb("bvs", [PP, 1]), sb("bps", [PP, 1])
        bias = sb("bias", [2 * N, 2, 2, HN])
        xin = [sb(f"xin{a}", [PP, WS, XP]) for a in range(2)]
        xres = [sb(f"xres{a}", [PP, WS, W]) for a in range(2)]
        xc = sb("xc", [PP, T2])
        sum_r = sb("sum_r", [PP, PP], F32R)
        sq = sb("sq", [PP, T2])
        sq_hi, sq_lo = sb("sq_hi", [PP, T2], F32R), sb("sq_lo", [PP, T2], F32R)
        sq2_hi, sq2_lo = sb("sq2_hi", [PP, T2], F32R), sb("sq2_lo", [PP, T2], F32R)
        lnv = sb("lnv", [PP, T2])
        rstd = sb("rstd", [PP, T2])
        h = sb("h", [PP, NWC, 2, N])
        ks = sb("ks", [PP, NWC, N])
        qbd = [sb(f"qbd{a}", [PP, NWC, 2 * N]) for a in range(2)]
        kex = [sb(f"kex{a}", [PP, NWC, HEADS, N]) for a in range(2)]
        vex = [sb(f"vex{a}", [2 * N, NWC, HEADS // 2, 2 * BO]) for a in range(2)]
        s_sb = [sb(f"s{i}", [2 * N, 2, HN]) for i in range(2)]
        mx = [sb(f"mx{i}", [2 * N, 2, HEADS]) for i in range(2)]
        pt = [sb(f"pt{i}", [2 * N, 2 * HN + OP - 2 * N]) for i in range(2)]
        osb = [sb(f"osb{a}", [OP, WS, W]) for a in range(2)]
        lnd = sb("lnd", [PP, T2])
        rden = sb("rden", [PP, T2])
        odiv = sb("odiv", [PP, T2])
        xo = [sb(f"xo{a}", [PP, WS, W]) for a in range(2)]
        xc2, sq2, lnv2, rstd2 = sb("xc2", [PP, T2]), sb("sq2", [PP, T2]), sb("lnv2", [PP, T2]), sb("rstd2", [PP, T2])
        y = [sb(f"y{a}", [PP, WS, YW]) for a in range(2)]

        ps_s = [ctx.enter_context(nc.psum_tensor(f"ps_s{i}", [128, 512], F32)) for i in range(3)]
        ps_t = ctx.enter_context(nc.psum_tensor("ps_t", [128, 2, 512], F32))
        ps_o = ctx.enter_context(nc.psum_tensor("ps_o", [128, 512], F32))
        ps_m = [ctx.enter_context(nc.psum_tensor(f"ps_m{i}", [128, 512], F32)) for i in range(2)]

        weights_in, xin_zeroed, zeroed, vones_set = sem("at_weights_in"), sem("xin_zeroed"), sem("at_zeroed"), sem("vones_set")
        folded, bias_mm, biases, bp_mm, tables, pad_set = (
            sem("folded"), sem("bias_mm"), sem("biases"), sem("bp_mm"), sem("tables"), sem("pad_set"))
        sum_set = sem("sum_set")
        sq_split, sq2_split = sem("sq_split"), sem("sq2_split")
        x_in = [sem(f"at_x_in{a}") for a in range(2)]
        x2_out = [sem(f"x2_out{a}") for a in range(2)]
        y_out = [sem(f"y_out{a}") for a in range(2)]
        wrapped, xres_set = sem("wrapped"), sem("xres_set")
        center_mm, squared, var_mm, ln_done, rstd_done, h_done, h_twice = (
            sem("center_mm"), sem("squared"), sem("var_mm"), sem("ln_done"), sem("rstd_done"), sem("h_done"),
            sem("h_twice"))
        q_mm, q_set, k_mm, k_set, v_mm, v_set, kex_set = (
            sem("q_mm"), sem("q_set"), sem("k_mm"), sem("k_set"), sem("v_mm"), sem("v_set"), sem("kex_set"))
        o_set, den_mm, lnd_done, rden_set, odiv_set, proj_mm, x2_set = (
            sem("o_set"), sem("den_mm"), sem("lnd_done"), sem("rden_set"), sem("odiv_set"), sem("proj_mm"), sem("x2_set"))
        center2_mm, squared2, var2_mm, ln2_done, rstd2_done, ymul_done, y_set = (
            sem("center2_mm"), sem("squared2"), sem("var2_mm"), sem("ln2_done"), sem("rstd2_done"),
            sem("ymul_done"), sem("y_set"))
        s_mm, s_biased, max_done, shifted, exp_done, t_mm, pt_set, pv_mm = (
            sem("s_mm"), sem("s_biased"), sem("max_done"), sem("shifted"), sem("exp_done"), sem("t_mm"), sem("pt_set"), sem("pv_mm"))

        def w(name):
            return PACK2.at(cw, name)

        pairs = B // 2

        def each_chunk(body):
            split = (RC - 1) * pairs // 2
            last = CHUNKS // 2 - 1
            body(0, 0, 0, 0)
            body(1, 0, 1, 0)
            for low, start, end in ((0, 1, split), (1, split, last)):
                with body.engine.Fori(start, end) as m:
                    body(m * 2, m, 0, low)
                    body(m * 2 + 1, m, 1, low)
            body(CHUNKS - 2, last, 0, 1)
            body(CHUNKS - 1, last, 1, 1)

        def at_edges(n):
            if isinstance(n, int):
                return n >= 2, n >= 1, n + 1 < CHUNKS, n + 2 < CHUNKS
            return True, True, True, True

        def windows(ap):
            return ap.rearrange("c (r w k) -> c w r k", r=WS, w=NWC)

        block = ctx.enter_context(nc.Block())

        @block.sync
        def _(sp):
            sp.dma_start(cw[:, :], pack).then_inc(weights_in, 16)

            def load(n, a):
                for i in range(2):
                    sp.dma_start(xin[a][BO * i:BO * i + C, :, 0:W],
                                 x1s[n, C * i:C * i + C, :].rearrange("c (r n) -> c r n", r=WS)).then_inc(x_in[a], 16)

            def store(n, a):
                sp.wait_ge(x2_set, n + 1)
                sp.wait_ge(y_set, n + 1)
                for i in range(2):
                    sp.dma_start(x2s[n, C * i:C * i + C, :].rearrange("c (r n) -> c r n", r=WS),
                                 xo[a][BO * i:BO * i + C, :, :]).then_inc(x2_out[a], 16)
                    sp.dma_start(ys[n, C * i:C * i + C, :].rearrange("c (r n) -> c r n", r=WS),
                                 y[a][BO * i:BO * i + C, :, :]).then_inc(y_out[a], 16)

            def load_ahead(n, a):
                sp.wait_ge(xres_set, n + 1)
                sp.wait_ge(center_mm, n + 1)
                load(n + 2, a)

            sp.wait_ge(xin_zeroed, 1)
            load(0, 0)
            load(1, 1)
            load_ahead(0, 0)
            load_ahead(1, 1)
            with sp.Fori(1, CHUNKS // 2 - 1) as m:
                for a in range(2):
                    load_ahead(m * 2 + a, a)
                    store(m * 2 + a - 2, a)
            for n in range(CHUNKS - 4, CHUNKS):
                store(n, n % 2)
            for a in range(2):
                sp.wait_ge(x2_out[a], CHUNKS // 2 * 32)
                sp.wait_ge(y_out[a], CHUNKS // 2 * 32)

        @block.gpsimd
        def _(pool):
            for a in range(2):
                ins = pool.memset(xin[a][:, :, :], 0.0)
            ins.then_inc(xin_zeroed, 1)
            for a in range(2):
                pool.memset(qbd[a][:, :, :], 0.0)
                pool.memset(y[a][:, :, :], 0.0)
                ins = pool.memset(pt[a][:, 2 * HN:], 0.0)
            ins.then_inc(zeroed, 1)
            pool.wait_ge(zeroed, 2)
            pool.wait_ge(weights_in, 16)
            ones = w("vones").rearrange("q (j h) -> q j h", j=HEADS // 2)
            for a in range(2):
                for win in range(NWC):
                    for o in (C, BO + C):
                        ins = pool.tensor_copy(vex[a][:, win, :, o:o + HEADS], ones)
            ins.then_inc(vones_set, 1)

            def split_squares(n):
                pool.wait_ge(squared, n + 1)
                pool.tensor_tensor(sq_lo[:, :], sq[:, :], sq_hi[:, :], ALU.subtract).then_inc(sq_split, 1)

            def split_squares2(n):
                pool.wait_ge(squared2, n + 1)
                pool.tensor_tensor(sq2_lo[:, :], sq2[:, :], sq2_hi[:, :], ALU.subtract).then_inc(sq2_split, 1)

            def twice(n):
                pool.wait_ge(rstd_done, n + 1)
                if at_edges(n)[1]:
                    pool.wait_ge(v_mm, n * 2)
                pool.tensor_tensor(h[:, :, 1, :].rearrange("c w (r k) -> c w r k", r=WS), windows(xc[:, :]), windows(rstd[:, :]),
                                   ALU.mult).then_inc(h_twice, 1)

            def keys(n, a):
                pool.wait_ge(k_set, n + 1)
                if at_edges(n)[0]:
                    pool.wait_ge(s_mm, n * NWC - NWC)
                for win in range(NWC):
                    pool.tensor_tensor(kex[a][:, win, :, :],
                                       ks[:, win, :].unsqueeze(1).to_broadcast([PP, HEADS, N]),
                                       w("head").unsqueeze(2).to_broadcast([PP, HEADS, N]), ALU.mult).then_inc(kex_set, 1)

            def divide(n, a):
                pool.wait_ge(rden_set, n + 1)
                if at_edges(n)[1]:
                    pool.wait_ge(proj_mm, n)
                pool.tensor_tensor(odiv[:, :], osb[a][0:PP, :, :].rearrange("c r n -> c (r n)"), rden[:, :],
                                   ALU.mult).then_inc(odiv_set, 1)

            def normalize2(n, m, a):
                pool.wait_ge(rstd2_done, n + 1)
                if at_edges(n)[0]:
                    pool.wait_ge(y_out[a], m * 32)
                pool.tensor_tensor(y[a][:, :, 1:1 + W], xc2[:, :].rearrange("c (r n) -> c r n", r=WS),
                                   rstd2[:, :].rearrange("c (r n) -> c r n", r=WS), ALU.mult).then_inc(ymul_done, 1)

            def body(n, m, a, low):
                before2, before, after, after2 = at_edges(n)
                if after:
                    split_squares(n + 1)
                if before2:
                    split_squares2(n - 2)
                    normalize2(n - 2, m - 1, a)
                if after:
                    twice(n + 1)
                if before:
                    divide(n - 1, 1 - a)
                if after:
                    keys(n + 1, 1 - a)

            split_squares(0)
            twice(0)
            keys(0, 0)
            body.engine = pool
            each_chunk(body)
            last = CHUNKS // 2 - 1
            split_squares2(CHUNKS - 2)
            normalize2(CHUNKS - 2, last, 0)
            divide(CHUNKS - 1, 1)
            split_squares2(CHUNKS - 1)
            normalize2(CHUNKS - 1, last, 1)

        @block.tensor
        def _(pe):
            pe.wait_ge(weights_in, 16)
            for i, name in enumerate(("wq", "wk", "wvd")):
                mm = pe.matmul(ps_m[0][0:PP, i:i + 1], w(name), w("be1"), start=True, stop=True)
            mm.then_inc(bias_mm, 1)
            pe.wait_ge(biases, 3)
            pe.matmul(ps_m[0][0:PP, 3:4], w("wp"), bvs[:, :], start=True, stop=True).then_inc(bp_mm, 1)
            pe.wait_ge(pad_set, 1)
            pe.wait_ge(folded, 3)

            def scores(n, d, a):
                if d == 0:
                    pe.wait_ge(q_set, n * 2 + 2)
                pe.wait_ge(kex_set, n * NWC + 2 * d + 2)
                for win in (2 * d, 2 * d + 1):
                    if win >= 3:
                        pe.wait_ge(s_biased, n * NWC + win - 2)
                    elif at_edges(n)[1]:
                        pe.wait_ge(s_biased, n * NWC + (-1, 0, -2)[win])
                    pe.matmul(ps_s[win % 3][0:2 * N, 0:HN], qbd[a][:, win, :],
                              kex[a][:, win, :, :].rearrange("c h k -> c (h k)"), start=True, stop=True).then_inc(s_mm, 1)

            def transposes(n, d):
                t = n * DUOS + d
                pe.wait_ge(exp_done, t + 1)
                if not isinstance(n, int) or t >= 1:
                    pe.wait_ge(pt_set, t)
                for i in range(2):
                    for j in range(HEADS // 2):
                        part = slice(j * 2 * N, (j + 1) * 2 * N)
                        mm = pe.transpose(ps_t[0:2 * N, i, part], s_sb[d % 2][:, i, part], w("ident"))
                mm.then_inc(t_mm, 1)

            def values(n, d, a):
                t = n * DUOS + d
                pe.wait_ge(pt_set, t + 1)
                if d == 0:
                    pe.wait_ge(v_set, n * 2 + 2)
                if d % 2 == 0 and (not isinstance(n, int) or t >= 2):
                    pe.wait_ge(o_set, n * 2 + d // 2)
                for i in range(2):
                    win = 2 * d + i
                    for j in range(HEADS // 2):
                        start = i * HN + j * 2 * N
                        mm = pe.matmul(ps_o[0:OP, (win % 4) * OP:(win % 4 + 1) * OP], vex[a][:, win, j, 0:OP],
                                       pt[d % 2][:, start:start + OP], start=j == 0, stop=j == HEADS // 2 - 1)
                mm.then_inc(pv_mm, 1)

            def misc(bank, lhs, rhs, signal):
                pe.matmul(ps_m[bank][0:PP, 0:T2], lhs, rhs, start=True, stop=True).then_inc(signal, 1)

            def sum_squares(bank, hi, lo, signal):
                pe.matmul(ps_m[bank][0:PP, 0:T2], sum_r[:, :], hi[:, :], start=True, stop=False)
                pe.matmul(ps_m[bank][0:PP, 0:T2], sum_r[:, :], lo[:, :], start=False, stop=True).then_inc(signal, 1)

            def center(n, a):
                pe.wait_ge(wrapped, n + 1)
                misc(0, w("center"), xin[a][:, :, SHIFT:XP], center_mm)

            def variance(n):
                pe.wait_ge(sq_split, n + 1)
                sum_squares(0, sq_hi, sq_lo, var_mm)

            def queries(n):
                pe.wait_ge(h_done, n + 1)
                misc(1, wqs[:, :], h[:, :, 0, :], q_mm)

            def keys(n):
                misc(0, wks[:, :], h[:, :, 0, :], k_mm)

            def value_rows(n, half):
                if half == 0:
                    pe.wait_ge(h_twice, n + 1)
                    pe.wait_ge(q_set, n * 2 + 2)
                else:
                    pe.wait_ge(k_set, n + 1)
                for i in range(4):
                    win = 4 * half + i
                    mm = pe.matmul(ps_m[1 - half][0:2 * N, i * 2 * C:(i + 1) * 2 * C],
                                   h[:, win, :, :].rearrange("c i k -> c (i k)"), wvs[:, :], start=True, stop=True)
                mm.then_inc(v_mm, 1)

            def denominators(n, a):
                pe.wait_ge(o_set, n * 2 + 2)
                misc(0, w("den"), osb[a][:, :, :].rearrange("c r n -> c (r n)"), den_mm)

            def project(n):
                pe.wait_ge(odiv_set, n + 1)
                misc(1, w("wp"), odiv[:, :], proj_mm)

            def center2(n, a):
                pe.wait_ge(x2_set, n + 1)
                misc(1, w("center"), xo[a][:, :, :], center2_mm)

            def variance2(n):
                pe.wait_ge(sq2_split, n + 1)
                sum_squares(1, sq2_hi, sq2_lo, var2_mm)

            def body(n, m, a, low):
                before2, before, after, _ = at_edges(n)
                scores(n, 0, a)
                if before:
                    values(n - 1, 2, 1 - a)
                pe.wait_ge(v_set, n * 2 + 2)
                if after:
                    center(n + 1, 1 - a)
                if before:
                    transposes(n - 1, 3)
                if before2:
                    center2(n - 2, a)

                scores(n, 1, a)
                if before:
                    values(n - 1, 3, 1 - a)
                if after:
                    variance(n + 1)
                transposes(n, 0)

                scores(n, 2, a)
                if before2:
                    variance2(n - 2)
                values(n, 0, a)
                if before2:
                    pe.wait_ge(ln2_done, n - 1)
                if after:
                    pe.wait_ge(ln_done, n + 2)
                    queries(n + 1)
                if before:
                    denominators(n - 1, 1 - a)
                transposes(n, 1)

                scores(n, 3, a)
                if after:
                    if before:
                        pe.wait_ge(lnd_done, n)
                    keys(n + 1)
                    value_rows(n + 1, 0)
                values(n, 1, a)
                if after:
                    value_rows(n + 1, 1)
                transposes(n, 2)
                if before:
                    if after:
                        pe.wait_ge(v_set, n * 2 + 3)
                    project(n - 1)

            pe.wait_ge(biases, 4)
            pe.wait_ge(sum_set, 1)
            center(0, 0)
            variance(0)
            queries(0)
            pe.wait_ge(ln_done, 1)
            keys(0)
            pe.wait_ge(vones_set, 1)
            value_rows(0, 0)
            value_rows(0, 1)
            body.engine = pe
            each_chunk(body)
            n = CHUNKS - 1
            values(n, 2, 1)
            center2(n - 1, 0)
            transposes(n, 3)
            variance2(n - 1)
            values(n, 3, 1)
            pe.wait_ge(lnd_done, n)
            denominators(n, 1)
            pe.wait_ge(ln2_done, n)
            project(n)
            center2(n, 1)
            variance2(n)

        @block.scalar
        def _(act):
            act.preload_act_table_set("natural_log_exp_and_others")

            def wrap(n, m, a):
                act.wait_ge(x_in[a], m * 32 + 32)
                act.activation(xin[a][:, :, W:XP], xin[a][:, :, 0:SHIFT], ACT.Copy).then_inc(wrapped, 1)

            def centered(n):
                act.wait_ge(center_mm, n + 1)
                if at_edges(n)[1]:
                    act.wait_ge(h_done, n)
                    act.wait_ge(h_twice, n)
                act.activation(xc[:, :], ps_m[0][0:PP, 0:T2], ACT.Copy)

            def squares():
                act.activation(sq[:, :], ps_m[0][0:PP, 0:T2], ACT.Square)
                act.activation(sq_hi[:, :], ps_m[0][0:PP, 0:T2], ACT.Square).then_inc(squared, 1)

            def ln(n):
                act.wait_ge(var_mm, n + 1)
                act.activation(lnv[:, :], ps_m[0][0:PP, 0:T2], ACT.Ln, bias=w("eps"), scale=1 / C).then_inc(ln_done, 1)

            def rsqrt(n):
                act.wait_ge(ln_done, n + 1)
                act.activation(rstd[:, :], lnv[:, :], ACT.Exp, scale=-0.5).then_inc(rstd_done, 1)

            def queries(n, a):
                act.wait_ge(q_mm, n + 1)
                if at_edges(n)[0]:
                    act.wait_ge(s_mm, n * NWC - NWC)
                for i in range(2):
                    rows = slice(BO * i, BO * i + C)
                    act.activation(qbd[a][rows, :, i * N:(i + 1) * N], ps_m[1][rows, 0:T2].rearrange("c (w k) -> c w k", w=NWC),
                                   ACT.Identity, bias=bqs[rows, :]).then_inc(q_set, 1)

            def keys(n):
                act.wait_ge(k_mm, n + 1)
                if at_edges(n)[1]:
                    act.wait_ge(kex_set, n * NWC)
                act.activation(ks[:, :, :], ps_m[0][0:PP, 0:T2].rearrange("c (w k) -> c w k", w=NWC),
                               ACT.Identity, bias=bks[:, :]).then_inc(k_set, 1)

            def outputs(n, half, a):
                act.wait_ge(pv_mm, n * DUOS + 2 * half + 2)
                for i, rows in enumerate((slice(0, BO), slice(BO, OP))):
                    ins = act.activation(
                        osb[a][rows, :, half * 4 * WS:(half + 1) * 4 * WS].rearrange("c r (w k) -> c w r k", w=4),
                        ps_o[rows, 0:4 * OP].rearrange("c (w n) -> c w n", w=4)[:, :, i * N:(i + 1) * N].rearrange(
                            "c w (r k) -> c w r k", r=WS), ACT.Copy)
                ins.then_inc(o_set, 1)

            def reciprocals(n):
                act.wait_ge(den_mm, n + 1)
                act.activation(lnd[:, :], ps_m[0][0:PP, 0:T2], ACT.Ln).then_inc(lnd_done, 1)
                act.wait_ge(lnd_done, n + 1)
                if at_edges(n)[1]:
                    act.wait_ge(odiv_set, n)
                act.activation(rden[:, :], lnd[:, :], ACT.Exp, scale=-1.0).then_inc(rden_set, 1)

            def exps(n, d):
                act.wait_ge(shifted, n * DUOS + d + 1)
                act.activation(s_sb[d % 2][:, :, :], s_sb[d % 2][:, :, :], ACT.Exp).then_inc(exp_done, 1)

            def transposed(n, d):
                t = n * DUOS + d
                act.wait_ge(t_mm, t + 1)
                if not isinstance(n, int) or t >= 2:
                    act.wait_ge(pv_mm, t - 1)
                act.activation(pt[d % 2][:, 0:2 * HN].rearrange("q (w n) -> q w n", w=2), ps_t[0:2 * N, :, 0:HN],
                               ACT.Copy).then_inc(pt_set, 1)

            def centered2(n):
                act.wait_ge(center2_mm, n + 1)
                if at_edges(n)[1]:
                    act.wait_ge(ymul_done, n)
                act.activation(xc2[:, :], ps_m[1][0:PP, 0:T2], ACT.Copy)
                act.activation(sq2[:, :], ps_m[1][0:PP, 0:T2], ACT.Square)
                act.activation(sq2_hi[:, :], ps_m[1][0:PP, 0:T2], ACT.Square).then_inc(squared2, 1)

            def ln2(n):
                act.wait_ge(var2_mm, n + 1)
                act.activation(lnv2[:, :], ps_m[1][0:PP, 0:T2], ACT.Ln, bias=w("eps"), scale=1 / C).then_inc(ln2_done, 1)

            def rsqrt2(n):
                act.wait_ge(ln2_done, n + 1)
                if at_edges(n)[1]:
                    act.wait_ge(ymul_done, n)
                act.activation(rstd2[:, :], lnv2[:, :], ACT.Exp, scale=-0.5).then_inc(rstd2_done, 1)

            def body(n, m, a, low):
                before2, before, after, after2 = at_edges(n)
                if before:
                    transposed(n - 1, 2)
                    exps(n - 1, 3)
                if after:
                    centered(n + 1)
                if before:
                    transposed(n - 1, 3)
                if after:
                    squares()
                exps(n, 0)
                if before2:
                    centered2(n - 2)
                if before:
                    outputs(n - 1, 1, 1 - a)
                if after:
                    ln(n + 1)
                transposed(n, 0)
                if after:
                    rsqrt(n + 1)
                if before2:
                    ln2(n - 2)
                exps(n, 1)
                if before2:
                    rsqrt2(n - 2)
                if after:
                    queries(n + 1, 1 - a)
                if before:
                    reciprocals(n - 1)
                transposed(n, 1)
                exps(n, 2)
                if after:
                    keys(n + 1)
                if after2:
                    wrap(n + 2, m + 1, a)
                outputs(n, 0, a)

            act.wait_ge(weights_in, 16)
            act.wait_ge(zeroed, 2)
            act.wait_ge(xin_zeroed, 1)
            wrap(0, 0, 0)
            wrap(1, 0, 1)
            centered(0)
            squares()
            ln(0)
            rsqrt(0)
            queries(0, 0)
            keys(0)
            body.engine = act
            each_chunk(body)
            n = CHUNKS - 1
            transposed(n, 2)
            exps(n, 3)
            centered2(n - 1)
            transposed(n, 3)
            ln2(n - 1)
            rsqrt2(n - 1)
            outputs(n, 1, 1)
            reciprocals(n)
            centered2(n)
            ln2(n)
            rsqrt2(n)

        @block.vector
        def _(dve):
            for a in range(2):
                ins = dve.memset(vex[a][:, :, :, :], 0.0)
            ins.then_inc(zeroed, 1)
            dve.wait_ge(weights_in, 16)
            dve.tensor_copy(sum_r[:, :], w("sum")).then_inc(sum_set, 1)
            dve.tensor_scalar(wqs[:, :], w("wq"), w("g1"), SCALE, op0=ALU.mult, op1=ALU.mult).then_inc(folded, 1)
            dve.tensor_scalar(wks[:, :], w("wk"), w("g1"), None, op0=ALU.mult).then_inc(folded, 1)
            dve.tensor_scalar(wvs[:, :], w("wv"), w("g1"), None, op0=ALU.mult).then_inc(folded, 1)
            masked = w("masked").rearrange("q (s k) -> q s k", s=4)
            for s in range(4):
                dve.tensor_tensor(bias[:, s // 2, s % 2, :].rearrange("q (h k) -> q h k", h=HEADS),
                                  w("rel").rearrange("q (h k) -> q h k", h=HEADS),
                                  masked[:, s, :].unsqueeze(1).to_broadcast([2 * N, HEADS, N]), ALU.add).then_inc(tables, 1)
            dve.wait_ge(bias_mm, 1)
            dve.tensor_scalar(bqs[:, :], ps_m[0][0:PP, 0:1], w("bq"), SCALE, op0=ALU.add, op1=ALU.mult).then_inc(biases, 1)
            dve.tensor_scalar(bks[:, :], ps_m[0][0:PP, 1:2], w("bk"), None, op0=ALU.add).then_inc(biases, 1)
            dve.tensor_scalar(bvs[:, :], ps_m[0][0:PP, 2:3], w("bv"), None, op0=ALU.add).then_inc(biases, 1)
            dve.wait_ge(bp_mm, 1)
            dve.tensor_scalar(bps[:, :], ps_m[0][0:PP, 3:4], w("bp"), None, op0=ALU.add).then_inc(biases, 1)
            dve.wait_ge(biases, 4)
            dve.wait_ge(tables, 4)
            dve.wait_ge(zeroed, 2)
            dve.engine_nop().then_inc(pad_set, 1)

            def add_tables(n, d, low):
                t = n * DUOS + d
                i = d % 2
                for k in range(2):
                    win = 2 * d + k
                    dve.wait_ge(s_mm, n * NWC + win + 1)
                    if k == 0 and (not isinstance(n, int) or t >= 2):
                        dve.wait_ge(t_mm, t - 1)
                    dve.tensor_tensor(s_sb[i][:, k, :], ps_s[win % 3][0:2 * N, 0:HN],
                                      bias[:, low, int(win == NWC - 1), :], ALU.add).then_inc(s_biased, 1)

            def shift(n, d):
                t = n * DUOS + d
                i = d % 2
                s4 = s_sb[i][:, :, :].rearrange("q w (h k) -> q (w h) k", h=HEADS)
                dve.wait_ge(s_biased, n * NWC + 2 * d + 2)
                mxi = mx[i][:, :, :].rearrange("q w h -> q (w h)")
                dve.tensor_reduce(mxi, s4, AX.X, ALU.max).then_inc(max_done, 1)
                dve.wait_ge(max_done, t + 1)
                dve.tensor_tensor(s4, s4, mxi.unsqueeze(2).to_broadcast([2 * N, 2 * HEADS, N]),
                                  ALU.subtract).then_inc(shifted, 1)

            def normalize(n):
                dve.wait_ge(rstd_done, n + 1)
                if at_edges(n)[1]:
                    dve.wait_ge(v_mm, n * 2)
                dve.tensor_tensor(h[:, :, 0, :].rearrange("c w (r k) -> c w r k", r=WS), windows(xc[:, :]), windows(rstd[:, :]),
                                  ALU.mult).then_inc(h_done, 1)

            def residual(n, m, a):
                dve.wait_ge(proj_mm, n + 1)
                dve.wait_ge(xres_set, n + 1)
                if at_edges(n)[0]:
                    dve.wait_ge(x2_out[a], m * 32)
                rolled = ps_m[1][0:PP, 0:T2].rearrange("c (r n) -> c r n", r=WS)
                cut = W - SHIFT
                dve.tensor_tensor(xo[a][:, :, SHIFT:W], rolled[:, :, 0:cut], xres[a][:, :, 0:cut], ALU.add)
                dve.tensor_tensor(xo[a][:, :, 0:SHIFT], rolled[:, :, cut:W], xres[a][:, :, cut:W], ALU.add).then_inc(x2_set, 1)

            def residual_in(n, a):
                dve.wait_ge(wrapped, n + 1)
                if at_edges(n)[0]:
                    dve.wait_ge(x2_set, n - 1)
                dve.tensor_scalar(xres[a][:, :, :], xin[a][:, :, SHIFT:XP], bps[:, 0:1], None, op0=ALU.add).then_inc(xres_set, 1)

            def value_rows(n, half, a):
                dve.wait_ge(v_mm, n * 2 + half + 1)
                if half == 0 and at_edges(n)[0]:
                    dve.wait_ge(pv_mm, n * DUOS - DUOS)
                rows = ps_m[1 - half][0:2 * N, 0:4 * 2 * C].rearrange("q (w i c) -> q w i c", w=4, i=2)
                to = vex[a][:, half * 4:half * 4 + 4, :, :]
                for head in range(HEADS):
                    own = slice(head * HD, (head + 1) * HD)
                    ins = dve.tensor_scalar(
                        to[:, :, head // 2, 0:2 * BO].rearrange("q w (i c) -> q w i c", i=2)[:, :, :, own],
                        rows[:, :, :, own], w("couple")[:, head % 2:head % 2 + 1], None, op0=ALU.mult)
                ins.then_inc(v_set, 1)

            def y_affine(n, a):
                dve.wait_ge(ymul_done, n + 1)
                dve.tensor_scalar(y[a][:, :, 1:1 + W], y[a][:, :, 1:1 + W], w("g2"), w("be2"),
                                  op0=ALU.mult, op1=ALU.add).then_inc(y_set, 1)

            def body(n, m, a, low):
                before2, before, after, _ = at_edges(n)
                for d in range(2):
                    add_tables(n, d, low)
                    shift(n, d)
                if after:
                    normalize(n + 1)
                add_tables(n, 2, low)
                shift(n, 2)
                if before2:
                    y_affine(n - 2, a)
                add_tables(n, 3, low)
                if after:
                    value_rows(n + 1, 0, 1 - a)
                shift(n, 3)
                if after:
                    value_rows(n + 1, 1, 1 - a)
                if before:
                    residual(n - 1, m - 1 + a, 1 - a)
                if after:
                    residual_in(n + 1, 1 - a)

            normalize(0)
            residual_in(0, 0)
            dve.wait_ge(vones_set, 1)
            value_rows(0, 0, 0)
            value_rows(0, 1, 0)
            body.engine = dve
            each_chunk(body)
            n = CHUNKS - 1
            y_affine(n - 1, 0)
            residual(n, CHUNKS // 2 - 1, 1)
            y_affine(n, 1)


def feed_forward(nc, x2s, ys, pack, out):
    ctx = ExitStack()
    with ctx:
        def sb(name, shape, dtype=F32):
            return ctx.enter_context(nc.sbuf_tensor(name, shape, dtype))

        def sem(name):
            return ctx.enter_context(nc.semaphore(name))

        half = HID // 2
        rest = 128 - 2 * C
        slots = 4
        first_rows = 2 * R1
        cw = sb("cw3", [128, PACK3.width])
        wa_hi, wa_lo = sb("wa_hi", [128, 3 * HID], F32R), sb("wa_lo", [128, 3 * HID], F32R)
        wb_hi, wb_lo = sb("wb_hi", [PP, HID], F32R), sb("wb_lo", [PP, HID], F32R)
        wf_hi, wf_lo = sb("wf_hi", [half, 2 * C], F32R), sb("wf_lo", [half, 2 * C], F32R)
        ya = sb("ya", [128, H * YW])
        yb = sb("yb", [BO, H * YW])
        ya_hi = [sb(f"ya_hi{a}", [128, H * YW], F32R) for a in range(2)]
        ya_lo = [sb(f"ya_lo{a}", [128, H * YW], F32R) for a in range(2)]
        yb_sp = [sb(f"yb_sp{a}", [PP, H * YW], F32R) for a in range(2)]
        xr = [sb(f"xr{a}", [C, HW]) for a in range(2)]
        hid = sb("hid", [half, slots, T1])
        hid_hi, hid_lo = sb("hid_hi", [half, slots, T1], F32R), sb("hid_lo", [half, slots, T1], F32R)
        ps_h = [ctx.enter_context(nc.psum_tensor(f"ps_h{i}", [128, 512], F32)) for i in range(slots)]
        ps_f = [ctx.enter_context(nc.psum_tensor(f"ps_f{i}", [128, 512], F32)) for i in range(2)]

        weights_in, ya_zeroed, yb_zeroed = sem("ff_weights_in"), sem("ya_zeroed"), sem("yb_zeroed")
        w_hi_set, w_lo_set = sem("w_hi_set"), sem("w_lo_set")
        ya_in, yb_in = sem("ya_in"), sem("yb_in")
        x2_in = [sem(f"x2_in{a}") for a in range(2)]
        out_done = [sem(f"out_done{a}") for a in range(2)]
        ya_hi_set, yb_hi_set, y_lo_set = sem("ya_hi_set"), sem("yb_hi_set"), sem("y_lo_set")
        first_hi_set, first_lo_set = sem("first_hi_set"), sem("first_lo_set")
        h_mm, gelu_done, f_mm, shift_added, result = sem("h_mm"), sem("ff_gelu_done"), sem("f_mm"), sem("shift_added"), sem("result")
        hid_hi_set, hid_lo_set = sem("hid_hi_set"), sem("hid_lo_set")
        Y_DMAS, X_DMAS = 9, 3

        def w(name):
            return PACK3.at(cw, name)

        def by_column(tile):
            return tile[:, :].rearrange("q (k m) -> q k m", k=3)

        block = ctx.enter_context(nc.Block())

        @block.sync
        def _(sp):
            sp.dma_start(cw[:, :], pack).then_inc(weights_in, 16)

            def load_rows(pair, a, tile, first, channels, shift, move, signal):
                count = channels.stop - channels.start
                src = ys[:, pair, a * C + channels.start:a * C + channels.stop, :]
                mid = (RC - 1) * WS
                to = (SHIFT + 1 - shift) * YW - move
                sp.dma_start(tile[first:first + count, to:to + mid * YW].rearrange("c (n t) -> c n t", n=RC - 1),
                             src[0:RC - 1, :, :].rearrange("n c t -> c n t")).then_inc(signal, 16)
                low = H - SHIFT - mid - (1 if shift == 0 else 0)
                to += mid * YW
                sp.dma_start(tile[first:first + count, to:to + low * YW], src[RC - 1, :, 0:low * YW]).then_inc(signal, 16)
                skip = 1 if shift == 2 else 0
                start = (H - SHIFT - mid + skip) * YW + move
                size = (SHIFT - skip) * YW - move
                to = (skip + 1 - shift) * YW
                sp.dma_start(tile[first:first + count, to:to + size], src[RC - 1, :, start:start + size]).then_inc(signal, 16)

            def load_ya(pair, a):
                load_rows(pair, a, ya, 0, slice(0, C), 0, 0, ya_in)
                load_rows(pair, a, ya, C, slice(0, C), 1, 0, ya_in)
                load_rows(pair, a, ya, 2 * C, slice(0, rest), 2, 0, ya_in)

            def load_yb(pair, a):
                for kw in range(3):
                    load_rows(pair, a, yb, kw * (C - rest), slice(rest, C), 2, kw, yb_in)

            def load_x(pair, a):
                src = x2s[:, pair, a * C:(a + 1) * C, :]
                mid, edge = (RC - 1) * T2, SHIFT * W
                sp.dma_start(xr[a][:, edge:edge + mid].rearrange("c (n t) -> c n t", n=RC - 1),
                             src[0:RC - 1, :, :].rearrange("n c t -> c n t")).then_inc(x2_in[a], 16)
                sp.dma_start(xr[a][:, edge + mid:HW], src[RC - 1, :, 0:T2 - edge]).then_inc(x2_in[a], 16)
                sp.dma_start(xr[a][:, 0:edge], src[RC - 1, :, T2 - edge:T2]).then_inc(x2_in[a], 16)

            sp.wait_ge(ya_zeroed, 1)
            load_ya(0, 0)
            sp.wait_ge(yb_zeroed, 1)
            load_yb(0, 0)
            load_x(0, 0)
            load_x(0, 1)
            sp.wait_ge(y_lo_set, 2)
            load_ya(0, 1)
            load_yb(0, 1)
            with sp.Fori(0, B // 2 - 1) as m:
                for a in range(2):
                    image = m * 2 + a
                    sp.wait_ge(y_lo_set, image * 2 + 4)
                    load_ya(m + 1, a)
                    load_yb(m + 1, a)
                    sp.wait_ge(result, image * C1 + C1)
                    sp.dma_start(out[image, :, :], xr[a][:, :]).then_inc(out_done[a], 16)
                    sp.wait_ge(out_done[a], m * 16 + 16)
                    load_x(m + 1, a)
            for a in range(2):
                sp.wait_ge(result, (B - 2 + a) * C1 + C1)
                sp.dma_start(out[B - 2 + a, :, :], xr[a][:, :]).then_inc(out_done[a], 16)
            for a in range(2):
                sp.wait_ge(out_done[a], B // 2 * 16)

        @block.gpsimd
        def _(pool):
            for row in (0, H - 1):
                ins = pool.memset(ya[:, row * YW:(row + 1) * YW], 0.0)
            ins.then_inc(ya_zeroed, 1)

            def images(m):
                for U in range(4 * C1):
                    pool.wait_ge(hid_hi_set, m * (4 * C1) + U + 1)
                    pool.tensor_tensor(hid_lo[:, U % slots, :], hid[:, U % slots, :], hid_hi[:, U % slots, :],
                                       ALU.subtract).then_inc(hid_lo_set, 1)

            with pool.Fori(0, B // 2) as m:
                images(m)

        @block.tensor
        def _(pe):
            def convolve(bank, a, c, k):
                rows = slice(c * R1, (c + 1) * R1)
                hidden = slice(k * half, (k + 1) * half)

                def pixels(tile, kw):
                    return tile.rearrange("q (r n) -> q r n", r=H)[:, rows, kw:kw + W]

                for kw in range(3):
                    for i, (weights, image) in enumerate(((wa_hi, ya_hi), (wa_hi, ya_lo), (wa_lo, ya_hi))):
                        pe.matmul(ps_h[bank][0:half, 0:T1], by_column(weights)[:, kw, hidden],
                                  pixels(image[a][:, :], kw), start=kw == 0 and i == 0, stop=False)
                pe.matmul(ps_h[bank][0:half, 0:T1], wb_hi[:, hidden], pixels(yb_sp[a][:, :], 0), start=False, stop=False)
                pe.matmul(ps_h[bank][0:half, 0:T1], wb_lo[:, hidden], pixels(yb_sp[a][:, :], 0),
                          start=False, stop=True).then_inc(h_mm, 1)

            def feed_back(t, T):
                pe.wait_ge(hid_lo_set, 2 * t + 2)
                if not isinstance(t, int) or t >= 2:
                    pe.wait_ge(result, t - 1)
                for k in range(2):
                    slot, m = (2 * T + k) % slots, slice(k * C, (k + 1) * C)
                    for i, (weights, hidden) in enumerate(((wf_hi, hid_hi), (wf_lo, hid_hi), (wf_hi, hid_lo))):
                        mm = pe.matmul(ps_f[T % 2][0:C, 0:T1], weights[:, m], hidden[:, slot, :],
                                       start=k == 0 and i == 0, stop=k == 1 and i == 2)
                mm.then_inc(f_mm, 1)

            def images(m):
                for a in range(2):
                    start = isinstance(m, int) and a == 0
                    if start:
                        pe.wait_ge(first_lo_set, 2)
                    else:
                        pe.wait_ge(y_lo_set, m * 4 + a * 2 + 2)
                    for c in range(C1):
                        if start and c == first_rows // R1:
                            pe.wait_ge(y_lo_set, 2)
                        T = a * C1 + c
                        t = m * (2 * C1) + T
                        for k in range(2):
                            if not isinstance(m, int) or t * 2 + k >= slots:
                                pe.wait_ge(gelu_done, t * 2 + k - slots + 1)
                            convolve((2 * T + k) % slots, a, c, k)
                        if not isinstance(m, int) or t >= 1:
                            feed_back(t - 1, (T - 1) % (2 * C1))

            pe.wait_ge(w_lo_set, 3)
            images(0)
            with pe.Fori(1, B // 2) as m:
                images(m)
            feed_back(B * C1 - 1, 2 * C1 - 1)

        @block.scalar
        def _(act):
            def images(m):
                for U in range(4 * C1):
                    u = m * (4 * C1) + U
                    act.wait_ge(h_mm, u + 1)
                    if not isinstance(m, int) or u >= slots:
                        act.wait_ge(f_mm, m * (2 * C1) + (U - slots) // 2 + 1)
                    act.activation(hid[:, U % slots, :], ps_h[U % slots][0:half, 0:T1], ACT.Gelu,
                                   bias=w("t1")[:, U % 2:U % 2 + 1], scale=w("s1")[:, U % 2:U % 2 + 1]).then_inc(gelu_done, 1)
                    act.wait_ge(gelu_done, u + 1)
                    act.activation(hid_hi[:, U % slots, :], hid[:, U % slots, :], ACT.Copy).then_inc(hid_hi_set, 1)

            act.wait_ge(weights_in, 16)
            images(0)
            with act.Fori(1, B // 2) as m:
                images(m)

        @block.vector
        def _(dve):
            dve.memset(yb[:, (H - 1) * YW - 2:], 0.0)
            dve.memset(yb[BO // 2:BO, 0:(H - 1) * YW - 2], 0.0).then_inc(yb_zeroed, 1)
            dve.wait_ge(weights_in, 16)
            dve.tensor_copy(wa_hi[:, :], w("wa")).then_inc(w_hi_set, 1)
            dve.tensor_copy(wb_hi[:, :], w("wb")).then_inc(w_hi_set, 1)
            dve.tensor_copy(wf_hi[:, :], w("wf2")).then_inc(w_hi_set, 1)
            dve.wait_ge(w_hi_set, 3)
            dve.tensor_tensor(wf_lo[:, :], w("wf2"), wf_hi[:, :], ALU.subtract).then_inc(w_lo_set, 1)
            dve.tensor_tensor(wa_lo[:, :], w("wa"), wa_hi[:, :], ALU.subtract).then_inc(w_lo_set, 1)
            dve.tensor_tensor(wb_lo[:, :], w("wb"), wb_hi[:, :], ALU.subtract).then_inc(w_lo_set, 1)

            def split_hi_a(a, px, signal):
                return dve.tensor_copy(ya_hi[a][:, px], ya[:, px]).then_inc(signal, 1)

            def split_hi_b(a, px, signal):
                return dve.tensor_copy(yb_sp[a][0:BO, px], yb[:, px]).then_inc(signal, 1)

            def split_lo_a(a, px, signal):
                return dve.tensor_tensor(ya_lo[a][:, px], ya[:, px], ya_hi[a][:, px], ALU.subtract).then_inc(signal, 1)

            def split_lo_b(a, px, signal):
                return dve.tensor_tensor(yb_sp[a][BO:PP, px], yb[0:C, px], yb_sp[a][0:C, px], ALU.subtract).then_inc(signal, 1)

            def split(image, a, step, px=slice(0, H * YW)):
                if step == 0:
                    dve.wait_ge(ya_in, image * (Y_DMAS * 16) + Y_DMAS * 16)
                    split_hi_a(a, px, ya_hi_set)
                elif step == 1:
                    dve.wait_ge(yb_in, image * (Y_DMAS * 16) + Y_DMAS * 16)
                    split_hi_b(a, px, yb_hi_set)
                elif step == 2:
                    dve.wait_ge(ya_hi_set, image + 1)
                    split_lo_a(a, px, y_lo_set)
                else:
                    dve.wait_ge(yb_hi_set, image + 1)
                    split_lo_b(a, px, y_lo_set)

            def add_shift(m, a):
                dve.wait_ge(x2_in[a], m * (X_DMAS * 16) + X_DMAS * 16)
                dve.tensor_scalar(xr[a][:, :], xr[a][:, :], w("t2"), None, op0=ALU.add).then_inc(shift_added, 1)

            def image_done(m, a, split_next):
                image = m * 2 + a
                dve.wait_ge(shift_added, image + 1)
                for c in range(C1):
                    dve.wait_ge(f_mm, image * C1 + c + 1)
                    cols = slice(c * T1, (c + 1) * T1)
                    dve.scalar_tensor_tensor(out=xr[a][:, cols], in0=ps_f[(a * C1 + c) % 2][0:C, 0:T1], scalar=w("s2"),
                                             in1=xr[a][:, cols], op0=ALU.mult, op1=ALU.add).then_inc(result, 1)
                    if split_next and 1 <= c <= 4:
                        split(image + 1, 1 - a, c - 1)

            first, others = slice(0, first_rows * YW), slice(first_rows * YW, H * YW)
            dve.wait_ge(ya_in, Y_DMAS * 16)
            split_hi_a(0, first, first_hi_set)
            dve.wait_ge(first_hi_set, 1)
            split_lo_a(0, first, first_lo_set)
            dve.wait_ge(yb_in, Y_DMAS * 16)
            split_hi_b(0, first, first_hi_set)
            dve.wait_ge(first_hi_set, 2)
            split_lo_b(0, first, first_lo_set)
            for step in range(4):
                split(0, 0, step, others)
            with dve.Fori(0, B // 2 - 1) as m:
                for a in range(2):
                    add_shift(m, a)
                    image_done(m, a, True)
            for a in range(2):
                add_shift(B // 2 - 1, a)
                image_done(B // 2 - 1, a, a == 0)


def program(nc, x, pack1, pack2, pack3, out):
    scratch = (RC, B // 2, 2 * C, T2)
    x1s = nc.dram_tensor("x1_chunks", scratch, F32, kind="Internal").ap()
    x2s = nc.dram_tensor("x2_chunks", scratch, F32, kind="Internal").ap()
    ys = nc.dram_tensor("y_chunks", (RC, B // 2, 2 * C, TY), F32, kind="Internal").ap()

    def chunks(s):
        return s.rearrange("n p c t -> (n p) c t")

    layer0(nc, x, pack1, x1s)
    attention(nc, chunks(x1s), pack2, chunks(x2s), chunks(ys))
    feed_forward(nc, x2s, ys, pack3, out)


def packed_layer0(W1, b1, W2, b2, mask_token, Wh, bh, Wd, bd, Wu, bu):
    w1d = np.zeros((2, C, 2, 2, D), np.float32)
    wu = np.zeros((GI, D, PAIRS, 2, C), np.float32)
    w2 = np.zeros((GI, D, GI, D), np.float32)
    mt = np.zeros((GI, D, GI, M), np.float32)
    for i in range(GI):
        p, a = divmod(i, 2)
        wu[i, :, p, a, :] = Wu.T
        w2[i, :, i, :] = W2.T
        mt[i, :, i, :] = mask_token.T
    for a in range(2):
        w1d[a, :, 0, a, :] = W1.T
        w1d[a, :, 1, a, :] = Wd.T
    wh = Wh.reshape(D, D, TAPS, D).transpose(1, 3, 2, 0).reshape(2, 128, TAPS * D).transpose(1, 0, 2)
    bht = bh.reshape(D, D, TAPS).transpose(1, 2, 0)
    ci = np.zeros((D // 2, D, 2, D), np.float32)
    for c in range(D):
        ci[c % (D // 2), :, c // (D // 2), c] = 1
    spread = np.tile(np.eye(D, dtype=np.float32), (1, GI))
    return PACK1.filled({
        "w1d": w1d, "w2": w2, "mt": mt, "wh": wh, "bh": bht, "wu": wu,
        "b1": np.tile(b1, GI), "b2": np.tile(b2, GI), "bd": np.tile(bd, GI), "bu": np.tile(bu, 2),
        "same_image": np.kron(np.eye(GI), np.ones((M, D))), "same_k": np.kron(np.ones((GI, D // 2)), np.eye(D)),
        "image": np.kron(np.eye(GI), np.ones((D, 1))), "ci": ci, "spread_ci": spread,
    })


def both(v):
    out = np.zeros((PP,) + v.shape[1:], np.float32)
    out[0:C] = v
    out[BO:PP] = v
    return out


def diagonal(v):
    out = np.zeros((PP, PP), np.float32)
    out[0:C, 0:C] = v
    out[BO:PP, BO:PP] = v
    return out


def packed_attention(ln1_g, ln1_b, w_qkv, b_qkv, bias_table, w_proj, b_proj, ln2_g, ln2_b):
    r, c = (v.reshape(-1) for v in np.meshgrid(np.arange(WS), np.arange(WS), indexing="ij"))
    place = (r[:, None] - r[None, :] + WS - 1) * (2 * WS - 1) + (c[:, None] - c[None, :] + WS - 1)
    rel = bias_table[place].transpose(0, 2, 1)
    cut = WS - SHIFT
    row_cut = (r[:, None] < cut) != (r[None, :] < cut)
    col_cut = (c[:, None] < cut) != (c[None, :] < cut)
    none = np.zeros((N, N), bool)
    masked = np.stack([none, col_cut, row_cut, row_cut | col_cut], 1) * np.float32(-100.0)
    wv = np.zeros((PP, 2 * C), np.float32)
    wv[0:C, 0:C] = w_qkv[:, 2 * C:]
    wv[BO:PP, C:] = w_qkv[:, 2 * C:]
    head = np.kron(np.eye(HEADS), np.ones((HD, 1)))
    vones = np.zeros((2, N, HEADS // 2, HEADS), np.float32)
    for j in range(HEADS // 2):
        for i in range(2):
            vones[i, :, j, 2 * j + i] = 1
    den = np.zeros((OP, PP), np.float32)
    for o in (0, BO):
        den[o + C:o + C + HEADS, o:o + C] = head.T
    den[C, C:BO] = 1
    third = [slice(i * C, (i + 1) * C) for i in range(3)]
    return PACK2.filled({
        "wq": diagonal(w_qkv[:, third[0]]), "wk": diagonal(w_qkv[:, third[1]]), "wv": wv,
        "wvd": diagonal(w_qkv[:, third[2]]), "wp": diagonal(w_proj),
        "g1": both(ln1_g), "be1": both(ln1_b), "bq": both(b_qkv[third[0]]), "bk": both(b_qkv[third[1]]),
        "bv": both(b_qkv[third[2]]), "bp": both(b_proj), "g2": both(ln2_g), "be2": both(ln2_b),
        "rel": np.concatenate([rel, rel]), "masked": np.concatenate([masked, masked]),
        "center": diagonal(np.eye(C) - 1 / C), "sum": diagonal(np.ones((C, C))),
        "head": both(head), "eps": np.full(PP, EPS, np.float32), "couple": np.kron(np.eye(2), np.ones((N, 1))), "vones": vones, "den": den,
        "ident": np.eye(2 * N),
    })


def packed_feed_forward(w_ffn1, bn1_scale, bn1_shift, w_ffn2, bn2_scale, bn2_shift):
    rest = 128 - 2 * C
    half = HID // 2
    taps = w_ffn1.transpose(1, 0, 2, 3)
    wa = taps.reshape(3, 3 * C, HID)[:, 0:128].transpose(1, 0, 2)
    wb = both(taps[:, 2, rest:].reshape(C, HID))
    wf2 = w_ffn2.reshape(2, half, C).transpose(1, 0, 2)
    return PACK3.filled({
        "wa": wa, "wb": wb, "wf2": wf2, "s1": bn1_scale.reshape(2, half).T, "t1": bn1_shift.reshape(2, half).T,
        "s2": bn2_scale, "t2": bn2_shift,
    })


def kernel(x, **weights):
    import concourse.bacc as bacc
    from concourse.bass_utils import run_bass_kernel_spmd

    a = {name: np.asarray(v) for name, v in weights.items()}

    def take(prefix, *names):
        return [a[prefix + name] for name in names]

    arrays = {
        "x": np.ascontiguousarray(np.asarray(x).reshape(B, HW, C).transpose(0, 2, 1)).reshape(B * C, HW),
        "pack1": packed_layer0(*take("L0_conv_", "W1", "b1", "W2", "b2", "mask_token", "Wh", "bh", "Wd", "bd", "Wu", "bu")),
        "pack2": packed_attention(*take("L1_conv_", "ln1_g", "ln1_b", "w_qkv", "b_qkv", "bias_table", "w_proj", "b_proj",
                                        "ln2_g", "ln2_b")),
        "pack3": packed_feed_forward(*take("L1_conv_", "w_ffn1", "bn1_scale", "bn1_shift", "w_ffn2", "bn2_scale",
                                           "bn2_shift")),
    }
    nc = bacc.Bacc("TRN2", target_bir_lowering=False, num_devices=1)
    aps = [nc.dram_tensor(name, v.shape, F32, kind="ExternalInput").ap() for name, v in arrays.items()]
    out = nc.dram_tensor("out", (B, C, HW), F32, kind="ExternalOutput").ap()
    program(nc, *aps, out)
    result = run_bass_kernel_spmd(nc, [arrays], core_ids=[0])
    return np.ascontiguousarray(result.results[0]["out"].transpose(0, 2, 1)).reshape(B, H, W, C)
```
